# Optimizing a Trainium2 kernel written in Bass

```python
import numpy as np
import jax
import jax.numpy as jnp

def _softmax(x, axis=-1):
    return jax.nn.softmax(x, axis=axis)

def _gelu(x):
    return jax.nn.gelu(x, approximate=True)

def _silu(x):
    return jax.nn.silu(x)

def _sigmoid(x):
    return jax.nn.sigmoid(x)

def _layernorm(x, axis=-1, eps=1e-05):
    m = jnp.mean(x, axis=axis, keepdims=True)
    v = jnp.var(x, axis=axis, keepdims=True)
    return (x - m) / jnp.sqrt(v + eps)

def _scatter_add(tgt, idx, src, axis=0):
    return tgt.at[idx].add(src)

def _segment_sum(src, seg, n):
    return jax.ops.segment_sum(src, seg, n)
kernel_name = 'mk_adj_seq_d4_adj_r2_bf3813'

def setup_inputs(seed: int=0):
    np.random.seed(seed)
    _w = jnp.asarray

    def _rec_inputs():
        import jax
        import jax.numpy as jnp
        _gk = jax.random.key(seed)
        x = -0.0005207 + 1.001 * jax.random.normal(jax.random.fold_in(_gk, 1), (16, 512, 256), jnp.float32)
        _a = jax.random.bernoulli(jax.random.fold_in(_gk, 2), 0.03125, (16, 512, 512))
        _a = jnp.logical_or(_a, jnp.swapaxes(_a, -1, -2))
        _a = jnp.logical_or(_a, jnp.eye(512, dtype=bool))
        adj = _a.astype(jnp.int32)
        return (x, adj)
    x, adj = _rec_inputs()

    def _L0_gnn_setup():
        import jax, jax.numpy as jnp
        import numpy as np
        B, S, D, H = (2, 1024, 256, 8)
        HD = D // H
        EPS = 1e-05

        def _ln(x, g, b):
            mu = jnp.mean(x, axis=-1, keepdims=True)
            var = jnp.mean((x - mu) ** 2, axis=-1, keepdims=True)
            return (x - mu) * jax.lax.rsqrt(var + EPS) * g + b
        key = jax.random.key(seed)
        ks = jax.random.split(key, 16)
        x = jax.random.normal(ks[0], (B, S, D), dtype=jnp.float32)
        adj = jax.random.randint(ks[1], (B, S, S), 0, 2, dtype=jnp.int32)
        adj = adj.at[:, jnp.arange(S), jnp.arange(S)].set(1)
        edge_attr = jax.random.normal(ks[2], (B, S, S), dtype=jnp.float32)
        sc = 1.0 / np.sqrt(D)
        p = lambda k, shp: jax.random.normal(k, shp, dtype=jnp.float32) * sc
        return {'x': x, 'adj_matrix': adj, 'edge_attr_matrix': edge_attr, 'ln1_g': jnp.ones((D,)), 'ln1_b': jnp.zeros((D,)), 'ln2_g': jnp.ones((D,)), 'ln2_b': jnp.zeros((D,)), 'wq': p(ks[3], (D, D)), 'bq': jnp.zeros((D,)), 'wk': p(ks[4], (D, D)), 'bk': jnp.zeros((D,)), 'wv': p(ks[5], (D, D)), 'bv': jnp.zeros((D,)), 'wo': p(ks[6], (D, D)), 'bo': jnp.zeros((D,)), 'w1': p(ks[7], (D, 4 * D)), 'b1': jnp.zeros((4 * D,)), 'w2': p(ks[8], (4 * D, D)), 'b2': jnp.zeros((D,))}
    _L0_gnn_all = _L0_gnn_setup()
    _L0_gnn_in = {k: v for k, v in _L0_gnn_all.items() if k in ('ln1_g', 'ln1_b', 'ln2_g', 'ln2_b', 'wq', 'bq', 'wk', 'bk', 'wv', 'bv', 'wo', 'bo', 'w1', 'b1', 'w2', 'b2')}
    del _L0_gnn_all

    def _L1_gnn_setup():
        import jax, jax.numpy as jnp
        import numpy as np
        B, N, D, H = (4, 1024, 256, 8)
        HD = D // H
        EPS = 1e-05
        key = jax.random.key(seed)
        ks = jax.random.split(key, 12)
        x = jax.random.normal(ks[0], (B, N, D), dtype=jnp.float32)
        adj = jax.random.randint(ks[1], (B, N, N), 0, 2, dtype=jnp.int32)
        adj = jnp.maximum(adj, jnp.eye(N, dtype=jnp.int32)[None, :, :])
        s = 1.0 / np.sqrt(D)
        Wq = jax.random.uniform(ks[2], (D, D), jnp.float32, -s, s)
        bq = jnp.zeros((D,), jnp.float32)
        Wk = jax.random.uniform(ks[3], (D, D), jnp.float32, -s, s)
        bk = jnp.zeros((D,), jnp.float32)
        Wv = jax.random.uniform(ks[4], (D, D), jnp.float32, -s, s)
        bv = jnp.zeros((D,), jnp.float32)
        Wo = jax.random.uniform(ks[5], (D, D), jnp.float32, -s, s)
        bo = jnp.zeros((D,), jnp.float32)
        gamma = jnp.ones((D,), jnp.float32)
        beta = jnp.zeros((D,), jnp.float32)
        return {'x': x, 'adj': adj, 'Wq': Wq, 'bq': bq, 'Wk': Wk, 'bk': bk, 'Wv': Wv, 'bv': bv, 'Wo': Wo, 'bo': bo, 'gamma': gamma, 'beta': beta}
    _L1_gnn_all = _L1_gnn_setup()
    _L1_gnn_in = {k: v for k, v in _L1_gnn_all.items() if k in ('Wq', 'bq', 'Wk', 'bk', 'Wv', 'bv', 'Wo', 'bo', 'gamma', 'beta')}
    del _L1_gnn_all

    def _L2_gnn_setup():
        import jax, jax.numpy as jnp
        import numpy as np
        import math
        D = 256
        B, L = (8, 1024)
        EPS = 1e-05

        def layer_norm(y, gamma, beta):
            mu = jnp.mean(y, axis=-1, keepdims=True)
            var = jnp.mean(jnp.square(y - mu), axis=-1, keepdims=True)
            return (y - mu) * jax.lax.rsqrt(var + EPS) * gamma + beta
        key = jax.random.key(seed)
        ks = jax.random.split(key, 8)
        s = 1.0 / math.sqrt(D)
        x = jax.random.normal(ks[0], (B, L, D), dtype=jnp.float32)
        adj = jax.random.randint(ks[1], (B, L, L), 0, 2, dtype=jnp.int32)
        Wq = jax.random.normal(ks[2], (D, D), dtype=jnp.float32) * s
        Wk = jax.random.normal(ks[3], (D, D), dtype=jnp.float32) * s
        Wv = jax.random.normal(ks[4], (D, D), dtype=jnp.float32) * s
        Wo = jax.random.normal(ks[5], (D, D), dtype=jnp.float32) * s
        bo = jnp.zeros((D,), dtype=jnp.float32)
        gamma = jnp.ones((D,), dtype=jnp.float32)
        beta = jnp.zeros((D,), dtype=jnp.float32)
        return {'x': x, 'adj': adj, 'Wq': Wq, 'Wk': Wk, 'Wv': Wv, 'Wo': Wo, 'bo': bo, 'gamma': gamma, 'beta': beta}
    _L2_gnn_all = _L2_gnn_setup()
    _L2_gnn_in = {k: v for k, v in _L2_gnn_all.items() if k in ('Wq', 'Wk', 'Wv', 'Wo', 'bo', 'gamma', 'beta')}
    del _L2_gnn_all

    def _L3_gnn_setup():
        import jax, jax.numpy as jnp
        import numpy as np
        B, N, H, D = (8, 512, 256, 4)
        EPS = 1e-08
        LN_EPS = 1e-05

        def _linear(x, W, b):
            return x @ W.T + b
        key = jax.random.key(seed)
        ks = jax.random.split(key, 20)
        inp = {'adj': jax.random.randint(ks[0], (B, N, N), 0, D + 1, dtype=jnp.int32), 'relative_pos': jax.random.randint(ks[1], (B, N, N), 0, 16, dtype=jnp.int32), 'hid': jax.random.normal(ks[2], (B, N, H), dtype=jnp.float32), 'Wd': jax.random.normal(ks[3], (H, D * H), dtype=jnp.float32) * (1.0 / np.sqrt(D * H)), 'bd': jnp.zeros((H,), jnp.float32)}
        s = 1.0 / np.sqrt(H)
        for i, nm in enumerate(['ri', 'rh', 'zi', 'zh', 'ni', 'nh']):
            inp['W' + nm] = jax.random.normal(ks[4 + i], (H, H), dtype=jnp.float32) * s
            inp['b' + nm] = jnp.zeros((H,), jnp.float32)
        inp['gamma'] = jnp.ones((H,), jnp.float32)
        inp['beta'] = jnp.zeros((H,), jnp.float32)
        return inp
    _L3_gnn_all = _L3_gnn_setup()
    _L3_gnn_in = {k: v for k, v in _L3_gnn_all.items() if k in ('Wd', 'bd', 'Wri', 'bri', 'Wrh', 'brh', 'Wzi', 'bzi', 'Wzh', 'bzh', 'Wni', 'bni', 'Wnh', 'bnh', 'gamma', 'beta')}
    del _L3_gnn_all
    return {'x': x, 'adj': adj, 'L0_gnn_ln1_g': _L0_gnn_in['ln1_g'], 'L0_gnn_ln1_b': _L0_gnn_in['ln1_b'], 'L0_gnn_ln2_g': _L0_gnn_in['ln2_g'], 'L0_gnn_ln2_b': _L0_gnn_in['ln2_b'], 'L0_gnn_wq': _L0_gnn_in['wq'], 'L0_gnn_bq': _L0_gnn_in['bq'], 'L0_gnn_wk': _L0_gnn_in['wk'], 'L0_gnn_bk': _L0_gnn_in['bk'], 'L0_gnn_wv': _L0_gnn_in['wv'], 'L0_gnn_bv': _L0_gnn_in['bv'], 'L0_gnn_wo': _L0_gnn_in['wo'], 'L0_gnn_bo': _L0_gnn_in['bo'], 'L0_gnn_w1': _L0_gnn_in['w1'], 'L0_gnn_b1': _L0_gnn_in['b1'], 'L0_gnn_w2': _L0_gnn_in['w2'], 'L0_gnn_b2': _L0_gnn_in['b2'], 'L1_gnn_Wq': _L1_gnn_in['Wq'], 'L1_gnn_bq': _L1_gnn_in['bq'], 'L1_gnn_Wk': _L1_gnn_in['Wk'], 'L1_gnn_bk': _L1_gnn_in['bk'], 'L1_gnn_Wv': _L1_gnn_in['Wv'], 'L1_gnn_bv': _L1_gnn_in['bv'], 'L1_gnn_Wo': _L1_gnn_in['Wo'], 'L1_gnn_bo': _L1_gnn_in['bo'], 'L1_gnn_gamma': _L1_gnn_in['gamma'], 'L1_gnn_beta': _L1_gnn_in['beta'], 'L2_gnn_Wq': _L2_gnn_in['Wq'], 'L2_gnn_Wk': _L2_gnn_in['Wk'], 'L2_gnn_Wv': _L2_gnn_in['Wv'], 'L2_gnn_Wo': _L2_gnn_in['Wo'], 'L2_gnn_bo': _L2_gnn_in['bo'], 'L2_gnn_gamma': _L2_gnn_in['gamma'], 'L2_gnn_beta': _L2_gnn_in['beta'], 'L3_gnn_Wd': _L3_gnn_in['Wd'], 'L3_gnn_bd': _L3_gnn_in['bd'], 'L3_gnn_Wri': _L3_gnn_in['Wri'], 'L3_gnn_bri': _L3_gnn_in['bri'], 'L3_gnn_Wrh': _L3_gnn_in['Wrh'], 'L3_gnn_brh': _L3_gnn_in['brh'], 'L3_gnn_Wzi': _L3_gnn_in['Wzi'], 'L3_gnn_bzi': _L3_gnn_in['bzi'], 'L3_gnn_Wzh': _L3_gnn_in['Wzh'], 'L3_gnn_bzh': _L3_gnn_in['bzh'], 'L3_gnn_Wni': _L3_gnn_in['Wni'], 'L3_gnn_bni': _L3_gnn_in['bni'], 'L3_gnn_Wnh': _L3_gnn_in['Wnh'], 'L3_gnn_bnh': _L3_gnn_in['bnh'], 'L3_gnn_gamma': _L3_gnn_in['gamma'], 'L3_gnn_beta': _L3_gnn_in['beta']}

def reference(x, adj, L0_gnn_ln1_g, L0_gnn_ln1_b, L0_gnn_ln2_g, L0_gnn_ln2_b, L0_gnn_wq, L0_gnn_bq, L0_gnn_wk, L0_gnn_bk, L0_gnn_wv, L0_gnn_bv, L0_gnn_wo, L0_gnn_bo, L0_gnn_w1, L0_gnn_b1, L0_gnn_w2, L0_gnn_b2, L1_gnn_Wq, L1_gnn_bq, L1_gnn_Wk, L1_gnn_bk, L1_gnn_Wv, L1_gnn_bv, L1_gnn_Wo, L1_gnn_bo, L1_gnn_gamma, L1_gnn_beta, L2_gnn_Wq, L2_gnn_Wk, L2_gnn_Wv, L2_gnn_Wo, L2_gnn_bo, L2_gnn_gamma, L2_gnn_beta, L3_gnn_Wd, L3_gnn_bd, L3_gnn_Wri, L3_gnn_bri, L3_gnn_Wrh, L3_gnn_brh, L3_gnn_Wzi, L3_gnn_bzi, L3_gnn_Wzh, L3_gnn_bzh, L3_gnn_Wni, L3_gnn_bni, L3_gnn_Wnh, L3_gnn_bnh, L3_gnn_gamma, L3_gnn_beta):
    import jax
    import jax.numpy as jnp

    def _L0_gnn_ref(x, adj_matrix, edge_attr_matrix, ln1_g, ln1_b, ln2_g, ln2_b, wq, bq, wk, bk, wv, bv, wo, bo, w1, b1, w2, b2):
        import jax, jax.numpy as jnp
        import numpy as np
        B, S, D, H = (2, 1024, 256, 8)
        HD = D // H
        EPS = 1e-05

        def _ln(x, g, b):
            mu = jnp.mean(x, axis=-1, keepdims=True)
            var = jnp.mean((x - mu) ** 2, axis=-1, keepdims=True)
            return (x - mu) * jax.lax.rsqrt(var + EPS) * g + b
        b, s, d = x.shape
        residual = x
        nx = _ln(x, ln1_g, ln1_b)
        q = (nx @ wq + bq).reshape(b, s, H, HD).transpose(0, 2, 1, 3)
        k = (nx @ wk + bk).reshape(b, s, H, HD).transpose(0, 2, 1, 3)
        v = (nx @ wv + bv).reshape(b, s, H, HD).transpose(0, 2, 1, 3)
        adjf = adj_matrix.astype(jnp.float32)
        bias = jnp.where(adj_matrix > 0, 0.1 * edge_attr_matrix * adjf, -jnp.inf)[:, None]
        scores = jnp.einsum('bhqd,bhkd->bhqk', q, k) / np.sqrt(HD) + bias
        attn = jax.nn.softmax(scores, axis=-1)
        out = jnp.einsum('bhqk,bhkd->bhqd', attn, v)
        out = out.transpose(0, 2, 1, 3).reshape(b, s, d)
        x1 = residual + (out @ wo + bo)
        n2 = _ln(x1, ln2_g, ln2_b)
        mlp = jax.nn.gelu(n2 @ w1 + b1, approximate=False) @ w2 + b2
        return x1 + mlp

    def _L1_gnn_ref(x, adj, Wq, bq, Wk, bk, Wv, bv, Wo, bo, gamma, beta):
        import jax, jax.numpy as jnp
        import numpy as np
        B, N, D, H = (4, 1024, 256, 8)
        HD = D // H
        EPS = 1e-05
        b, n, d = x.shape
        scale = 1.0 / np.sqrt(HD).astype(np.float32)
        q = (x @ Wq + bq).reshape(b, n, H, HD)
        k = (x @ Wk + bk).reshape(b, n, H, HD)
        v = (x @ Wv + bv).reshape(b, n, H, HD)
        scores = jnp.einsum('bnhd,bmhd->bhnm', q, k) * scale
        mask = (adj == 0)[:, None, :, :]
        scores = jnp.where(mask, jnp.float32(-jnp.inf), scores)
        attn = jax.nn.softmax(scores, axis=-1)
        h = jnp.einsum('bhnm,bmhd->bnhd', attn, v).reshape(b, n, d)
        h = h @ Wo + bo
        y = h + x
        mu = jnp.mean(y, axis=-1, keepdims=True)
        var = jnp.mean(jnp.square(y - mu), axis=-1, keepdims=True)
        return (y - mu) * jax.lax.rsqrt(var + EPS) * gamma + beta

    def _L2_gnn_ref(x, adj, Wq, Wk, Wv, Wo, bo, gamma, beta):
        import jax, jax.numpy as jnp
        import numpy as np
        import math
        D = 256
        B, L = (8, 1024)
        EPS = 1e-05

        def layer_norm(y, gamma, beta):
            mu = jnp.mean(y, axis=-1, keepdims=True)
            var = jnp.mean(jnp.square(y - mu), axis=-1, keepdims=True)
            return (y - mu) * jax.lax.rsqrt(var + EPS) * gamma + beta
        d_out = Wq.shape[1]
        scale = 1.0 / math.sqrt(d_out)
        Q = x @ Wq
        K = x @ Wk
        V = x @ Wv
        sc = jnp.einsum('bld,bmd->blm', Q, K) * scale
        mask = adj == 0
        sc = jnp.where(mask, -jnp.inf, sc)
        all_inf = jnp.all(mask, axis=-1, keepdims=True)
        sc = jnp.where(all_inf, 0.0, sc)
        w = jax.nn.softmax(sc, axis=-1)
        out = jnp.einsum('blm,bmd->bld', w, V)
        y = x + out @ Wo + bo
        return layer_norm(y, gamma, beta)

    def _L3_gnn_ref(adj, relative_pos, hid, Wd, bd, Wri, bri, Wrh, brh, Wzi, bzi, Wzh, bzh, Wni, bni, Wnh, bnh, gamma, beta):
        import jax, jax.numpy as jnp
        import numpy as np
        B, N, H, D = (8, 512, 256, 4)
        EPS = 1e-08
        LN_EPS = 1e-05

        def _linear(x, W, b):
            return x @ W.T + b
        dt = hid.dtype
        labels = jnp.arange(1, D + 1, dtype=adj.dtype)
        mask = (adj[None] == labels[:, None, None, None]).astype(dt)
        weight = mask / (jnp.sum(mask, axis=-1, keepdims=True) + EPS)
        agg = jnp.einsum('dbmn,bnh->bmdh', weight, hid).reshape(hid.shape[0], hid.shape[1], D * H)
        out = jax.nn.relu(_linear(agg, Wd, bd))
        r = jax.nn.sigmoid(_linear(out, Wri, bri) + _linear(hid, Wrh, brh))
        z = jax.nn.sigmoid(_linear(out, Wzi, bzi) + _linear(hid, Wzh, bzh))
        n = jnp.tanh(_linear(out, Wni, bni) + r * _linear(hid, Wnh, bnh))
        out = (1.0 - z) * n + z * hid
        mu = jnp.mean(out, axis=-1, keepdims=True)
        var = jnp.var(out, axis=-1, keepdims=True)
        return (out - mu) / jnp.sqrt(var + LN_EPS) * gamma + beta
    x = _L0_gnn_ref(x, adj, adj, L0_gnn_ln1_g, L0_gnn_ln1_b, L0_gnn_ln2_g, L0_gnn_ln2_b, L0_gnn_wq, L0_gnn_bq, L0_gnn_wk, L0_gnn_bk, L0_gnn_wv, L0_gnn_bv, L0_gnn_wo, L0_gnn_bo, L0_gnn_w1, L0_gnn_b1, L0_gnn_w2, L0_gnn_b2)
    x = _L1_gnn_ref(x, adj, L1_gnn_Wq, L1_gnn_bq, L1_gnn_Wk, L1_gnn_bk, L1_gnn_Wv, L1_gnn_bv, L1_gnn_Wo, L1_gnn_bo, L1_gnn_gamma, L1_gnn_beta)
    x = _L2_gnn_ref(x, adj, L2_gnn_Wq, L2_gnn_Wk, L2_gnn_Wv, L2_gnn_Wo, L2_gnn_bo, L2_gnn_gamma, L2_gnn_beta)
    x = _L3_gnn_ref(adj, adj, x, L3_gnn_Wd, L3_gnn_bd, L3_gnn_Wri, L3_gnn_bri, L3_gnn_Wrh, L3_gnn_brh, L3_gnn_Wzi, L3_gnn_bzi, L3_gnn_Wzh, L3_gnn_bzh, L3_gnn_Wni, L3_gnn_bni, L3_gnn_Wnh, L3_gnn_bnh, L3_gnn_gamma, L3_gnn_beta)
    return x

_drawn_inputs = setup_inputs


def setup_inputs(seed=0):
    import zlib

    import numpy as np

    out = dict(_drawn_inputs(seed))
    spreads = {'L0_gnn_ln1_g': (1.0, 0.2),
     'L0_gnn_ln1_b': (0.0, 0.1),
     'L0_gnn_ln2_g': (1.0, 0.2),
     'L0_gnn_ln2_b': (0.0, 0.1),
     'L0_gnn_bq': (0.0, 0.316),
     'L0_gnn_bk': (0.0, 0.8),
     'L0_gnn_bv': (0.0, 0.1),
     'L0_gnn_bo': (0.0, 0.1),
     'L0_gnn_b1': (0.0, 0.1),
     'L0_gnn_b2': (0.0, 0.1),
     'L1_gnn_bq': (0.0, 0.8),
     'L1_gnn_bk': (0.0, 0.8),
     'L1_gnn_bv': (0.0, 0.1),
     'L1_gnn_bo': (0.0, 0.1),
     'L1_gnn_gamma': (1.0, 0.2),
     'L1_gnn_beta': (0.0, 0.1),
     'L2_gnn_bo': (0.0, 0.1),
     'L2_gnn_gamma': (1.0, 0.2),
     'L2_gnn_beta': (0.0, 0.1),
     'L3_gnn_bd': (0.0, 0.1),
     'L3_gnn_bri': (0.0, 0.676),
     'L3_gnn_brh': (0.0, 0.672),
     'L3_gnn_bzi': (0.0, 0.1),
     'L3_gnn_bzh': (0.0, 0.1),
     'L3_gnn_bni': (0.0, 0.1),
     'L3_gnn_bnh': (0.0, 0.1),
     'L3_gnn_gamma': (1.0, 0.2),
     'L3_gnn_beta': (0.0, 0.1)}
    factors = {}
    for name, (base, spread) in spreads.items():
        noise = np.random.default_rng([zlib.crc32(name.encode()), seed]).standard_normal(out[name].shape)
        drawn = base * np.exp(spread * noise) if base else spread * noise
        out[name] = jnp.asarray(drawn.astype(out[name].dtype))
    for name, factor in factors.items():
        out[name] = (out[name] * factor).astype(out[name].dtype)
    return out
```

```python
from contextlib import ExitStack

import concourse.bass as bass
import numpy as np
from concourse import mybir

F32 = mybir.dt.float32
F32R = mybir.dt.float32r
BF16 = mybir.dt.bfloat16
I32 = mybir.dt.int32
ALU = mybir.AluOpType
ACT = mybir.ActivationFunctionType

P = 128
N = 512
D = 256
HEADS = 8
HD = D // HEADS
NT = N // P
CT = D // P
GROUPS = CT
GH = HEADS // GROUPS
FF = 4 * D
LABELS = 4
STREAMS = 2
EPS = 1e-5
MASKED = -(2.0 ** 100)
HEAD_SCALE = float(HD) ** -0.5
TILES = HEADS * NT

LAG_T = 3
LAG_V = LAG_T + 5
STEPS = TILES + LAG_V
LAG = 1
STACKED = 16 * 4


def merged(stages, lag):
    order = []
    for t in range(len(stages) + lag):
        if t < len(stages):
            order.append((stages[t], 0))
        if t >= lag:
            order.append((stages[t - lag], 1))
    return order


class Phase:

    def __init__(self, nc, ctx, name):
        self.nc, self.ctx, self.name = nc, ctx, name
        self.all = []

    def buf(self, name, shape, dt=F32):
        return self.ctx.enter_context(self.nc.sbuf_tensor(f"{self.name}_{name}", shape, dt))

    def bufs(self, name, shape, dt=F32):
        return [self.buf(f"{name}{s}", shape, dt) for s in range(STREAMS)]

    def sem(self, name):
        h = self.ctx.enter_context(self.nc.semaphore(f"{self.name}_{name}"))
        self.all.append(h)
        return h

    def sems(self, name):
        return [self.sem(f"{name}{s}") for s in range(STREAMS)]

    def clear(self):
        nums = [h.num for h in self.all]
        self.nc.all_engine_barrier(sems_to_clear=range(min(nums), max(nums) + 1))


def rows(ap):
    return ap.rearrange("(t p) n -> p t n", p=P)


def product(pe, out, left, right, first, last):
    (lh, ll), (rh, rl) = left, right
    pe.matmul(out, lh, rh, start=first, stop=False)
    pe.matmul(out, ll, rh, start=False, stop=False)
    return pe.matmul(out, lh, rl, start=False, stop=last)


def load_weights(nc, ph, weights, vectors, staging):
    loaded, parts = ph.sem("weights_loaded"), ph.sem("weights_split")
    places, used = [], [0] * len(staging)
    for src, hi, lo in weights:
        k, m = src.shape
        size = k // P * m
        n = next(i for i, b in enumerate(staging) if used[i] + size <= b.shape[1])
        places.append(staging[n][:, used[n]:used[n] + size].rearrange("p (t m) -> p t m", m=m))
        used[n] += size
    with nc.Block(no_gpsimd_drain=True) as block:
        @block.sync
        def _(sp):
            for (src, _, _), raw in zip(weights, places):
                sp.dma_start(raw, src.rearrange("(t p) m -> p t m", p=P)).then_inc(loaded, 16)
            for src, to in vectors:
                sp.dma_start(to, src).then_inc(loaded, 16)
            sp.wait_ge(loaded, 16 * (len(weights) + len(vectors)))

        @block.vector
        def _(dve):
            dve.wait_ge(loaded, 16 * (len(weights) + len(vectors)))
            for n, ((_, hi, lo), raw) in enumerate(zip(weights, places)):
                dve.tensor_copy(hi[:], raw).then_inc(parts, 1)
                dve.wait_ge(parts, 2 * n + 1)
                dve.tensor_tensor(lo[:], raw, hi[:].bitcast(F32), ALU.subtract).then_inc(parts, 1)
            dve.wait_ge(parts, 2 * len(weights))


def make_constants(nc, ph, power, ident, *others):
    made = ph.sem("identity_made")
    with nc.Block(no_gpsimd_drain=True) as block:
        @block.gpsimd
        def _(pool):
            pool.memset(power[:], -0.5)
            pool.memset(ident[:], 0.0).then_inc(made, 1)
            pool.wait_ge(made, 1)
            pool.affine_select(out=ident[:], in_=ident[:], compare_op=ALU.not_equal, fill=1.0, base=0,
                               pattern=[[-1, P]], channel_multiplier=1).then_inc(made, 1)
            pool.wait_ge(made, 2)
            for n, other in enumerate(others):
                pool.tensor_copy(other[:], ident[:]).then_inc(made, 1)
            pool.wait_ge(made, 2 + len(others))


def encoder_phase(nc, name, x_in, adj, out, w, graphs, ffn):
    with ExitStack() as ctx:
        ph = Phase(nc, ctx, name)
        split = {}
        for k, m in (("wq", D), ("wk", D), ("wv", D), ("wo", D)) + ((("w1", FF),) if ffn else ()):
            split[k] = (ph.buf(k + "h", [P, CT, m], F32R), ph.buf(k + "l", [P, CT, m], F32R))
        if ffn:
            split["w2"] = (ph.buf("w2h", [P, FF // P, D], F32R), ph.buf("w2l", [P, FF // P, D], F32R))
        ident = ph.buf("ident", [P, P])
        power = ph.buf("power", [P, NT])
        bq, bk, bv = ph.buf("bq", [P, CT]), ph.buf("bk", [P, CT]), ph.buf("bv", [P, CT])
        bo = ph.buf("bo", [P, D])
        if ffn:
            ln1_g, ln1_b = ph.buf("ln1_g", [P, CT]), ph.buf("ln1_b", [P, CT])
            ln2_g, ln2_b = ph.buf("ln2_g", [P, CT]), ph.buf("ln2_b", [P, CT])
            b1, b2 = ph.buf("b1", [P, FF // P]), ph.buf("b2", [P, D])
        else:
            ln_g, ln_b = ph.buf("ln_g", [P, D]), ph.buf("ln_b", [P, D])
        xres = ph.bufs("xres", [P, NT, D])
        bias = ph.bufs("bias", [P, NT, N], F32 if ffn else BF16)
        norm = ph.bufs("norm", [P, NT, D])
        feats = ph.bufs("feats", [P, 2, CT, N], F32R)
        parts = ph.bufs("parts", [P, 4, N], F32R)
        stack = ph.bufs("stack", [P, 2, GH, N], F32R)
        value = ph.bufs("value", [P, NT, D])
        prob = ph.bufs("prob", [P, 4, N])
        probT = ph.bufs("probT", [P, 2, NT, N])
        low = ph.bufs("low", [P, TILES])
        total = ph.bufs("total", [P, TILES])
        stat, mean_var = ph.bufs("stat", [P, NT, 6]), ph.bufs("mean_var", [P, NT, 2])
        veps, rstd = ph.bufs("veps", [P, NT]), ph.bufs("rstd", [P, NT])
        bank = [ctx.enter_context(nc.psum_tensor(f"{name}_bank{s}", [P, 4, N], F32)) for s in range(STREAMS)]
        adj_sb = [probT[s][:, 0].bitcast(I32) for s in range(STREAMS)]
        sq = [probT[s][:, 1] for s in range(STREAMS)]
        normT = [norm[s][:].rearrange("p t d -> p (t d)").rearrange("p (c n) -> p c n", c=CT) for s in range(STREAMS)]
        mixT = [parts[s][:].rearrange("p (a c) n -> p a c n", a=2) for s in range(STREAMS)]
        wide = [prob[s][:, 0:2].rearrange("p a n -> p (a n)").rearrange("p (q d) -> p q d", d=D)
                for s in range(STREAMS)]
        hidden = stack

        load_weights(
            nc, ph, [(w[k], *split[k]) for k in split],
            [(w["bq"], bq[:]), (w["bk"], bk[:]), (w["bv"], bv[:]),
             (w["bo"].partition_broadcast(P), bo[:])]
            + ([(w["ln1_g"], ln1_g[:]), (w["ln1_b"], ln1_b[:]), (w["ln2_g"], ln2_g[:]),
                (w["ln2_b"], ln2_b[:]), (w["b1"], b1[:]), (w["b2"].partition_broadcast(P), b2[:])]
               if ffn else [(w["ln_g"].partition_broadcast(P), ln_g[:]), (w["ln_b"].partition_broadcast(P), ln_b[:])]),
            [probT[s][:].rearrange("p a t n -> p (a t n)") for s in range(STREAMS)])
        make_constants(nc, ph, power, ident)
        x_loaded, adj_loaded = ph.sems("x_loaded"), ph.sems("adj_loaded")
        bias_made = ph.sems("bias_made")
        res_made = ph.sems("res_made")
        stats_done, rstd_done, normed = ph.sems("stats_done"), ph.sems("rstd_done"), ph.sems("normed")
        turned_x, feats_hi, feats_lo = ph.sems("turned_x"), ph.sems("feats_hi"), ph.sems("feats_lo")
        qk_done, qk_hi, qk_lo = ph.sems("qk_done"), ph.sems("qk_hi"), ph.sems("qk_lo")
        stacked = [ph.sems(f"stacked{h}_") for h in range(GH)]
        v_done, v_ready = ph.sems("v_done"), ph.sems("v_ready")
        scores, biased, probs, turned = ph.sems("scores"), ph.sems("biased"), ph.sems("probs"), ph.sems("turned")
        copied_dve, copied_act = ph.sems("copied_dve"), ph.sems("copied_act")
        mixed, mix_raw, inverse, spread = ph.sems("mixed"), ph.sems("mix_raw"), ph.sems("inverse"), ph.sems("spread")
        mix_scaled, mix_hi, mix_lo = ph.sems("mix_scaled"), ph.sems("mix_hi"), ph.sems("mix_lo")
        projected, x1_made = ph.sems("projected"), ph.sems("x1_made")
        hid_done, hid_gelu, hid_hi, hid_lo = ph.sems("hid_done"), ph.sems("hid_gelu"), ph.sems("hid_hi"), ph.sems("hid_lo")
        down_done, summed, stored = ph.sems("down_done"), ph.sems("summed"), ph.sems("stored")
        feats_full, gained = ph.sems("feats_full"), ph.sems("gained")

        stages = ["load", "norm1", "turn1", "qk0", "v", "qk1"] + [f"heads{j}" for j in range(STEPS)]
        stages += ["mix", "project", "norm2"]
        stages += ["turn2", "ffn0", "ffn1", "store"] if ffn else ["store"]
        order = merged(stages, LAG)
        second_group = [f"heads{(h + 1) * NT - 1}" for h in range(GH)]

        def wait_copied(eng, s, i):
            eng.wait_ge(copied_dve[s], i // 2 + 1)
            if i >= 1:
                eng.wait_ge(copied_act[s], (i + 1) // 2)

        def out_tile(ap, i):
            h, q = divmod(i, NT)
            return ap[:, h % 2, :, q * P:(q + 1) * P]

        with nc.Fori(0, graphs // STREAMS) as pair:
            with nc.Block(no_gpsimd_drain=True) as block:
                @block.sync
                def _(sp):
                    def stack_head(s, h):
                        src = parts[s][HD * h:HD * (h + 1)].bitcast(F32)
                        for n, part in enumerate((src[:, 0::2], src[:, 0::3], src[:, 1:3], src[:, 1::2])):
                            sp.dma_start(stack[s][HD * n:HD * (n + 1), :, h].bitcast(F32), part)\
                                .then_inc(stacked[h][s], 16)

                    for s in range(STREAMS):
                        sp.dma_start(xres[s][:], rows(x_in[pair * STREAMS + s])).then_inc(x_loaded[s], 16)
                        sp.dma_start(adj_sb[s], rows(adj[pair * STREAMS + s])).then_inc(adj_loaded[s], 16)
                    for stage, s in order:
                        if stage == "qk0":
                            sp.wait_ge(qk_hi[s], 2)
                            sp.wait_ge(qk_lo[s], 2)
                            for h in range(GH):
                                stack_head(s, h)
                        elif stage in second_group:
                            h = second_group.index(stage)
                            sp.wait_ge(qk_hi[s], 4)
                            sp.wait_ge(qk_lo[s], 4)
                            sp.wait_ge(scores[s], NT * (h + 1))
                            stack_head(s, h)
                        elif stage == "store":
                            sp.wait_ge(summed[s], 4 if ffn else NT)
                            sp.dma_start(rows(out[pair * STREAMS + s]), xres[s][:]).then_inc(stored[s], 16)
                    for s in range(STREAMS):
                        sp.wait_ge(stored[s], 16)

                @block.gpsimd
                def _(pool):
                    def reciprocal_root(s, n):
                        pool.wait_ge(stats_done[s], 2 * NT * (n + 1))
                        pool.tensor_scalar(veps[s][:], mean_var[s][:, :, 1], EPS, 1.0, ALU.add, ALU.mult)\
                            .then_inc(rstd_done[s], 1)
                        pool.wait_ge(rstd_done[s], 2 * n + 1)
                        pool.tensor_tensor(rstd[s][:], veps[s][:], power[:], ALU.pow).then_inc(rstd_done[s], 1)

                    for stage, s in order:
                        if stage == "norm1" and ffn:
                            reciprocal_root(s, 0)
                            pool.wait_ge(normed[s], NT)
                            pool.tensor_tensor(xres[s][:], xres[s][:],
                                               bo[:].unsqueeze(1).to_broadcast([P, NT, D]), ALU.add)\
                                .then_inc(res_made[s], 1)
                        elif stage == "turn1" and not ffn:
                            pool.wait_ge(turned_x[s], CT)
                            pool.tensor_tensor(xres[s][:], xres[s][:],
                                               bo[:].unsqueeze(1).to_broadcast([P, NT, D]), ALU.add)\
                                .then_inc(res_made[s], 1)
                        elif stage == "norm2":
                            reciprocal_root(s, 1 if ffn else 0)
                            if ffn:
                                pool.wait_ge(normed[s], 2 * NT)
                                pool.tensor_tensor(xres[s][:], xres[s][:],
                                                   b2[:].unsqueeze(1).to_broadcast([P, NT, D]), ALU.add)\
                                    .then_inc(res_made[s], 1)
                        elif stage in ("ffn0", "ffn1"):
                            half = int(stage[3])
                            for k in range(4):
                                i = 4 * half + k
                                pool.wait_ge(hid_hi[s], i + 1)
                                if half and k == 0:
                                    pool.wait_ge(down_done[s], 2)
                                pool.tensor_tensor(hidden[s][:, 1, k], prob[s][:, i % 4],
                                                   hidden[s][:, 0, k].bitcast(F32), ALU.subtract)\
                                    .then_inc(hid_lo[s], 1)

                @block.tensor
                def _(pe):
                    def turn(s, src, n, ready):
                        for wait in ready:
                            pe.wait_ge(*wait)
                        for c in range(CT):
                            for t in range(NT):
                                mm = pe.transpose(bank[s][:, c, t * P:(t + 1) * P],
                                                  src[:, t, c * P:(c + 1) * P], ident[:])
                            mm.then_inc(turned_x[s], 1)

                    def feature(s, c, lo, hi):
                        return feats[s][:, 0, c, lo:hi], feats[s][:, 1, c, lo:hi]

                    def weight(k, c, lo, hi):
                        return split[k][0][:, c, lo:hi], split[k][1][:, c, lo:hi]

                    def step(s, j):
                        if j < TILES:
                            h, q = divmod(j, NT)
                            if q == 0:
                                pe.wait_ge(stacked[h % GH][s], STACKED * (h // GH + 1))
                            if j == 0:
                                pe.wait_ge(v_ready[s], 2)
                                pe.wait_ge(qk_hi[s], 2 * GROUPS)
                                pe.wait_ge(qk_lo[s], 2 * GROUPS)
                            if j - 2 - LAG_T >= 0:
                                wait_copied(pe, s, j - 2 - LAG_T)
                            elif j >= 3:
                                pe.wait_ge(biased[s], j - 2)
                            pe.matmul(bank[s][:, 2 * j % 3], stack[s][:, 0, h % GH, q * P:(q + 1) * P],
                                      stack[s][:, 1, h % GH], start=True, stop=True).then_inc(scores[s], 1)
                        i = j - LAG_T
                        if 0 <= i < TILES:
                            pe.wait_ge(probs[s], i + 1)
                            if j - 1 < TILES:
                                pe.wait_ge(biased[s], j)
                            else:
                                wait_copied(pe, s, i - 3)
                            for k in range(NT):
                                mm = pe.transpose(bank[s][:, (2 * j + 1) % 3, k * P:(k + 1) * P],
                                                  prob[s][:, i % 4, k * P:(k + 1) * P], ident[:])
                            mm.then_inc(turned[s], 1)
                        i = j - LAG_V
                        if 0 <= i < TILES:
                            h, k = divmod(i, NT)
                            if k == 0:
                                wait_copied(pe, s, NT * h + NT - 1)
                                if h == GH:
                                    pe.wait_ge(mix_raw[s], 1)
                            mm = pe.matmul(bank[s][HD * (h % GH):HD * (h % GH + 1), 3],
                                           value[s][:, k, HD * h:HD * (h + 1)], probT[s][:, h % 2, k],
                                           start=k == 0, stop=k == NT - 1)
                            if k == NT - 1:
                                mm.then_inc(mixed[s], 1)

                    for stage, s in order:
                        if stage == "turn1":
                            turn(s, norm[s] if ffn else xres[s], 0,
                                 [(normed[s], NT)] if ffn else [(x_loaded[s], 16)])
                        elif stage in ("qk0", "qk1"):
                            g = int(stage[2])
                            pe.wait_ge(feats_hi[s], CT)
                            pe.wait_ge(feats_lo[s], CT)
                            if g:
                                pe.wait_ge(qk_hi[s], 2 * g)
                                pe.wait_ge(qk_lo[s], 2 * g)
                            for b, k in enumerate(("wq", "wk")):
                                for c in range(CT):
                                    mm = product(pe, bank[s][:, b], weight(k, c, g * P, (g + 1) * P),
                                                 feature(s, c, 0, N), c == 0, c == CT - 1)
                                mm.then_inc(qk_done[s], 1)
                        elif stage == "v":
                            for t in range(NT):
                                for c in range(CT):
                                    mm = product(pe, bank[s][:, 2 + t // 2, t % 2 * D:(t % 2 + 1) * D],
                                                 feature(s, c, t * P, (t + 1) * P), weight("wv", c, 0, D),
                                                 c == 0, c == CT - 1)
                                if t % 2:
                                    mm.then_inc(v_done[s], 1)
                        elif stage.startswith("heads"):
                            step(s, int(stage[5:]))
                        elif stage == "mix":
                            pe.wait_ge(inverse[s], 2)
                            wait_copied(pe, s, TILES - 1)
                            for g in range(GROUPS):
                                for q in range(NT):
                                    mm = pe.transpose(bank[s][:, g, q * P:(q + 1) * P],
                                                      wide[s][:, q, g * P:(g + 1) * P], ident[:])
                                mm.then_inc(spread[s], 1)
                        elif stage == "project":
                            pe.wait_ge(mix_raw[s], GROUPS)
                            pe.wait_ge(mix_hi[s], GROUPS)
                            pe.wait_ge(mix_lo[s], GROUPS)
                            for t in range(NT):
                                for c in range(CT):
                                    mm = product(pe, bank[s][:, 2 + t // 2, t % 2 * D:(t % 2 + 1) * D],
                                                 (mixT[s][:, 0, c, t * P:(t + 1) * P],
                                                  mixT[s][:, 1, c, t * P:(t + 1) * P]),
                                                 weight("wo", c, 0, D), c == 0, c == CT - 1)
                                if t % 2:
                                    mm.then_inc(projected[s], 1)
                        elif stage == "turn2":
                            turn(s, norm[s], 1, [(normed[s], 2 * NT)])
                        elif stage in ("ffn0", "ffn1"):
                            half = int(stage[3])
                            if not half:
                                pe.wait_ge(feats_hi[s], 2 * CT)
                                pe.wait_ge(feats_lo[s], 2 * CT)
                            for k in range(4):
                                i = 4 * half + k
                                if i >= 2:
                                    pe.wait_ge(hid_gelu[s], i - 1)
                                for c in range(CT):
                                    mm = product(pe, bank[s][:, i % 2], weight("w1", c, i * P, (i + 1) * P),
                                                 feature(s, c, 0, N), c == 0, c == CT - 1)
                                mm.then_inc(hid_done[s], 1)
                            pe.wait_ge(hid_lo[s], 4 * half + 4)
                            if half:
                                pe.wait_ge(summed[s], 2)
                            for t in range(NT):
                                for k in range(4):
                                    mm = product(pe, bank[s][:, 2 + t // 2, t % 2 * D:(t % 2 + 1) * D],
                                                 (hidden[s][:, 0, k, t * P:(t + 1) * P],
                                                  hidden[s][:, 1, k, t * P:(t + 1) * P]),
                                                 weight("w2", 4 * half + k, 0, D), k == 0, k == 3)
                                if t % 2:
                                    mm.then_inc(down_done[s], 1)

                @block.scalar
                def _(act):
                    for stage, s in order:
                        if stage in ("turn1", "turn2"):
                            n = int(stage[4]) - 1
                            for c in range(CT):
                                act.wait_ge(turned_x[s], CT * n + (CT if ffn else c + 1))
                                if ffn:
                                    gain, off = ((ln1_g, ln1_b), (ln2_g, ln2_b))[n]
                                    act.activation(normT[s][:, c], bank[s][:, c], ACT.Identity,
                                                   scale=gain[:, c:c + 1], bias=off[:, c:c + 1])\
                                        .then_inc(feats_full[s], 1)
                                    act.wait_ge(feats_full[s], CT * n + c + 1)
                                    act.activation(feats[s][:, 0, c], normT[s][:, c], ACT.Copy)\
                                        .then_inc(feats_hi[s], 1)
                                else:
                                    act.activation(feats[s][:, 0, c], bank[s][:, c], ACT.Copy)\
                                        .then_inc(feats_hi[s], 1)
                        elif stage in ("qk0", "qk1"):
                            g = int(stage[2])
                            for b, vec in enumerate((bq, bk)):
                                act.wait_ge(qk_done[s], 2 * g + b + 1)
                                if g and b == 0:
                                    for copied_head in stacked:
                                        act.wait_ge(copied_head[s], STACKED)
                                act.activation(parts[s][:, 2 * b], bank[s][:, b], ACT.Identity,
                                               bias=vec[:, g:g + 1]).then_inc(qk_hi[s], 1)
                        elif stage.startswith("heads"):
                            j = int(stage[5:])
                            if j < TILES:
                                act.wait_ge(biased[s], j + 1)
                                act.activation(prob[s][:, j % 4], prob[s][:, j % 4], ACT.Exp,
                                               bias=low[s][:, j:j + 1], scale=-1.0,
                                               accum_out=total[s][:, j:j + 1]).then_inc(probs[s], 1)
                            i = j - LAG_T
                            if 0 <= i < TILES and i % 2:
                                act.wait_ge(turned[s], i + 1)
                                if i >= 2 * NT:
                                    act.wait_ge(mixed[s], i // NT - 1)
                                act.activation(
                                    out_tile(probT[s], i),
                                    bank[s][:, (2 * j + 1) % 3].rearrange("p (k q) -> p k q", q=P),
                                    ACT.Copy).then_inc(copied_act[s], 1)
                            i = j - LAG_V
                            if 0 <= i < TILES and i % (GH * NT) == GH * NT - 1:
                                g = i // (GH * NT)
                                act.wait_ge(mixed[s], GH * (g + 1))
                                act.activation(normT[s][:, g], bank[s][:, 3], ACT.Copy)\
                                    .then_inc(mix_raw[s], 1)
                        elif stage == "mix":
                            for copied_head in stacked:
                                act.wait_ge(copied_head[s], GROUPS * STACKED)
                            for g in range(GROUPS):
                                act.wait_ge(mix_scaled[s], 2 * g + 2)
                                act.activation(mixT[s][:, 0, g], normT[s][:, g], ACT.Copy).then_inc(mix_hi[s], 1)
                        elif stage in ("ffn0", "ffn1"):
                            half = int(stage[3])
                            for k in range(4):
                                i = 4 * half + k
                                act.wait_ge(hid_done[s], i + 1)
                                if half:
                                    act.wait_ge(hid_lo[s], i - 3)
                                act.activation(prob[s][:, i % 4], bank[s][:, i % 2], ACT.Gelu,
                                               bias=b1[:, i:i + 1]).then_inc(hid_gelu[s], 1)

                @block.vector
                def _(dve):
                    def norm_rows(s, src, to, n):
                        for t in range(NT):
                            dve.bn_stats(stat[s][:, t], src[:, t]).then_inc(stats_done[s], 1)
                        for t in range(NT):
                            dve.wait_ge(stats_done[s], 2 * NT * n + t + 1)
                            dve.bn_aggr(mean_var[s][:, t], stat[s][:, t]).then_inc(stats_done[s], 1)
                        dve.wait_ge(rstd_done[s], 2 * n + 2)
                        for t in range(NT):
                            dve.tensor_scalar(to[:, t], src[:, t], mean_var[s][:, t, 0:1], rstd[s][:, t:t + 1],
                                              ALU.subtract, ALU.mult).then_inc(normed[s], 1)

                    for stage, s in order:
                        if stage == "load":
                            dve.wait_ge(adj_loaded[s], 16)
                            if ffn:
                                dve.tensor_scalar(bias[s][:], adj_sb[s], 0.0, MASKED, ALU.is_le, ALU.mult)\
                                    .then_inc(bias_made[s], 1)
                                dve.scalar_tensor_tensor(
                                    out=sq[s].rearrange("p t n -> p (t n)"),
                                    in0=adj_sb[s].rearrange("p t n -> p (t n)"), scalar=0.1 / HEAD_SCALE,
                                    in1=adj_sb[s].rearrange("p t n -> p (t n)"), op0=ALU.mult, op1=ALU.mult)\
                                    .then_inc(bias_made[s], 1)
                                dve.wait_ge(bias_made[s], 2)
                                dve.tensor_tensor(bias[s][:], bias[s][:], sq[s], ALU.add).then_inc(bias_made[s], 1)
                            else:
                                dve.tensor_scalar(bias[s][:], adj_sb[s], 0.0, MASKED, ALU.is_equal, ALU.mult)\
                                    .then_inc(bias_made[s], 1)
                        elif stage == "norm1" and ffn:
                            dve.wait_ge(x_loaded[s], 16)
                            norm_rows(s, xres[s], norm[s], 0)
                        elif stage in ("turn1", "turn2"):
                            n = int(stage[4]) - 1
                            for c in range(CT):
                                dve.wait_ge(feats_hi[s], CT * n + c + 1)
                                dve.tensor_tensor(feats[s][:, 1, c], normT[s][:, c] if ffn else bank[s][:, c],
                                                  feats[s][:, 0, c].bitcast(F32), ALU.subtract)\
                                    .then_inc(feats_lo[s], 1)
                        elif stage in ("qk0", "qk1"):
                            g = int(stage[2])
                            for b, vec in enumerate((bq, bk)):
                                dve.wait_ge(qk_hi[s], 2 * g + b + 1)
                                dve.scalar_tensor_tensor(
                                    out=parts[s][:, 2 * b + 1], in0=bank[s][:, b], scalar=vec[:, g:g + 1],
                                    in1=parts[s][:, 2 * b].bitcast(F32), op0=ALU.add, op1=ALU.subtract)\
                                    .then_inc(qk_lo[s], 1)
                        elif stage == "v":
                            for b in range(2):
                                dve.wait_ge(v_done[s], b + 1)
                                dve.tensor_copy(value[s][:, 2 * b:2 * b + 2],
                                                bank[s][:, 2 + b].rearrange("p (t d) -> p t d", d=D))\
                                    .then_inc(v_ready[s], 1)
                        elif stage.startswith("heads"):
                            j = int(stage[5:])
                            if j < TILES:
                                dve.wait_ge(scores[s], j + 1)
                                if j == 0:
                                    dve.wait_ge(bias_made[s], 3 if ffn else 1)
                                if j >= 4:
                                    dve.wait_ge(turned[s], j - 3)
                                dve.tensor_tensor_reduce(
                                    prob[s][:, j % 4], bank[s][:, 2 * j % 3], bias[s][:, j % NT],
                                    -HEAD_SCALE, 3e38, ALU.add, ALU.min, low[s][:, j:j + 1])\
                                    .then_inc(biased[s], 1)
                            i = j - LAG_T
                            if 0 <= i < TILES and i % 2 == 0:
                                dve.wait_ge(turned[s], i + 1)
                                if i >= 2 * NT:
                                    dve.wait_ge(mixed[s], i // NT - 1)
                                dve.tensor_copy(
                                    out_tile(probT[s], i),
                                    bank[s][:, (2 * j + 1) % 3].rearrange("p (k q) -> p k q", q=P))\
                                    .then_inc(copied_dve[s], 1)
                        elif stage == "mix":
                            dve.wait_ge(probs[s], TILES)
                            dve.reciprocal(total[s][:], total[s][:]).then_inc(inverse[s], 1)
                            dve.wait_ge(inverse[s], 1)
                            dve.wait_ge(turned[s], TILES)
                            dve.tensor_copy(
                                wide[s].rearrange("p q (h d) -> p q h d", d=HD),
                                total[s][:].rearrange("p (h q) -> p q h", q=NT).unsqueeze(3)
                                .to_broadcast([P, NT, HEADS, HD])).then_inc(inverse[s], 1)
                            for g in range(GROUPS):
                                dve.wait_ge(spread[s], g + 1)
                                dve.wait_ge(mix_raw[s], g + 1)
                                dve.tensor_tensor(normT[s][:, g], normT[s][:, g], bank[s][:, g], ALU.mult)\
                                    .then_inc(mix_scaled[s], 1)
                                dve.wait_ge(mix_scaled[s], 2 * g + 1)
                                dve.tensor_scalar(normT[s][:, g], normT[s][:, g], bv[:, g:g + 1], None, ALU.add)\
                                    .then_inc(mix_scaled[s], 1)
                            for g in range(GROUPS):
                                dve.wait_ge(mix_hi[s], g + 1)
                                dve.tensor_tensor(mixT[s][:, 1, g], normT[s][:, g],
                                                  mixT[s][:, 0, g].bitcast(F32), ALU.subtract)\
                                    .then_inc(mix_lo[s], 1)
                        elif stage == "project":
                            dve.wait_ge(res_made[s], 1)
                            for b in range(2):
                                dve.wait_ge(projected[s], b + 1)
                                dve.tensor_tensor(xres[s][:, 2 * b:2 * b + 2],
                                                  bank[s][:, 2 + b].rearrange("p (t d) -> p t d", d=D),
                                                  xres[s][:, 2 * b:2 * b + 2], ALU.add).then_inc(x1_made[s], 1)
                        elif stage == "norm2":
                            dve.wait_ge(x1_made[s], 2)
                            if ffn:
                                dve.wait_ge(mix_lo[s], GROUPS)
                                norm_rows(s, xres[s], norm[s], 1)
                            else:
                                norm_rows(s, xres[s], xres[s], 0)
                                for t in range(NT):
                                    dve.wait_ge(normed[s], t + 1)
                                    dve.tensor_tensor(xres[s][:, t], xres[s][:, t], ln_g[:], ALU.mult)\
                                        .then_inc(gained[s], 1)
                                for t in range(NT):
                                    dve.wait_ge(gained[s], t + 1)
                                    dve.tensor_tensor(xres[s][:, t], xres[s][:, t], ln_b[:], ALU.add)\
                                        .then_inc(summed[s], 1)
                        elif stage in ("ffn0", "ffn1"):
                            half = int(stage[3])
                            for k in range(4):
                                i = 4 * half + k
                                dve.wait_ge(hid_gelu[s], i + 1)
                                if half and k == 0:
                                    dve.wait_ge(down_done[s], 2)
                                dve.tensor_copy(hidden[s][:, 0, k], prob[s][:, i % 4]).then_inc(hid_hi[s], 1)
                            dve.wait_ge(res_made[s], 2)
                            for b in range(2):
                                dve.wait_ge(down_done[s], 2 * half + b + 1)
                                if half:
                                    dve.wait_ge(summed[s], b + 1)
                                dve.tensor_tensor(xres[s][:, 2 * b:2 * b + 2],
                                                  bank[s][:, 2 + b].rearrange("p (t d) -> p t d", d=D),
                                                  xres[s][:, 2 * b:2 * b + 2], ALU.add).then_inc(summed[s], 1)
            ph.clear()


def graph_attention_phase(nc, name, x_in, adj, out_t, w, graphs):
    scale = float(D) ** -0.5
    with ExitStack() as ctx:
        ph = Phase(nc, ctx, name)
        raw_names = ("wq_t", "wk_t", "wv_t", "wo")
        split = {k: (ph.buf(k + "h", [P, CT, D], F32R), ph.buf(k + "l", [P, CT, D], F32R)) for k in raw_names}
        folded = {k: (ph.buf(k + "h", [P, CT, D], F32R), ph.buf(k + "l", [P, CT, D], F32R)) for k in ("qk", "vo")}
        ident, power = ph.buf("ident", [P, P]), ph.buf("power", [P, NT])
        bo, ln_g, ln_b = ph.buf("bo", [P, D]), ph.buf("ln_g", [P, CT]), ph.buf("ln_b", [P, CT])
        xres = ph.bufs("xres", [P, NT, D])
        adj_sb = ph.bufs("adj", [P, NT, N], I32)
        bias = ph.bufs("bias", [P, NT, N], BF16)
        norm = ph.bufs("norm", [P, NT, D])
        feats = ph.bufs("feats", [P, 2, CT, N], F32R)
        query = ph.bufs("query", [P, 2, CT, N], F32R)
        value = ph.bufs("value", [P, NT, D])
        prob = ph.bufs("prob", [P, NT, N])
        probT = ph.bufs("probT", [P, NT, N])
        hid_t = ph.bufs("hid_t", [P, CT, N])
        low, total = ph.bufs("low", [P, NT]), ph.bufs("total", [P, NT])
        stat, mean_var = ph.bufs("stat", [P, NT, 6]), ph.bufs("mean_var", [P, NT, 2])
        veps, rstd = ph.bufs("veps", [P, NT]), ph.bufs("rstd", [P, NT])
        bank = [ctx.enter_context(nc.psum_tensor(f"{name}_bank{s}", [P, 4, N], F32)) for s in range(STREAMS)]
        load_weights(nc, ph, [(w[k], *split[k]) for k in raw_names],
                     [(w["bo"].partition_broadcast(P), bo[:]), (w["ln_g"], ln_g[:]), (w["ln_b"], ln_b[:])],
                     [prob[s][:].rearrange("p t n -> p (t n)") for s in range(STREAMS)])
        make_constants(nc, ph, power, ident)
        multiplied, folded_hi, folded_lo = ph.sem("multiplied"), ph.sem("folded_hi"), ph.sem("folded_lo")
        with nc.Block(no_gpsimd_drain=True) as block:
            pairs = (("qk", "wq_t", "wk_t"), ("vo", "wv_t", "wo"))

            @block.tensor
            def _(pe):
                for s, (_, left, right) in enumerate(pairs):
                    for i in range(CT):
                        for c in range(CT):
                            mm = product(pe, bank[s][:, i, 0:D],
                                         (split[left][0][:, c, i * P:(i + 1) * P], split[left][1][:, c, i * P:(i + 1) * P]),
                                         (split[right][0][:, c], split[right][1][:, c]), c == 0, c == CT - 1)
                        mm.then_inc(multiplied, 1)

            @block.vector
            def _(dve):
                for s, (k, _, _) in enumerate(pairs):
                    for i in range(CT):
                        dve.wait_ge(multiplied, CT * s + i + 1)
                        dve.tensor_copy(folded[k][0][:, i], bank[s][:, i, 0:D]).then_inc(folded_hi, 1)
                        dve.wait_ge(folded_hi, CT * s + i + 1)
                        dve.tensor_tensor(folded[k][1][:, i], bank[s][:, i, 0:D],
                                          folded[k][0][:, i].bitcast(F32), ALU.subtract).then_inc(folded_lo, 1)
        x_loaded, adj_loaded, bias_made, res_made = (ph.sems(k) for k in ("x_loaded", "adj_loaded", "bias_made", "res_made"))
        turned_x, feats_hi, feats_lo = (ph.sems(k) for k in ("turned_x", "feats_hi", "feats_lo"))
        q_done, q_hi, q_lo, v_done, v_ready = (ph.sems(k) for k in ("q_done", "q_hi", "q_lo", "v_done", "v_ready"))
        scores, biased, probs, turned, copied = (ph.sems(k) for k in ("scores", "biased", "probs", "turned", "copied"))
        inverse, mixed, x1_made = (ph.sems(k) for k in ("inverse", "mixed", "x1_made"))
        stats_done, rstd_done, normed = (ph.sems(k) for k in ("stats_done", "rstd_done", "normed"))
        turned_out, out_made, stored = (ph.sems(k) for k in ("turned_out", "out_made", "stored"))

        lag_t, lag_v = 2, 3
        steps = [f"step{j}" for j in range(NT + lag_v)]
        stages = ["load", "turn", "query", "value"] + steps + ["norm", "turn_out", "store"]
        order = merged(stages, LAG)

        with nc.Fori(0, graphs // STREAMS) as pair:
            with nc.Block(no_gpsimd_drain=True) as block:
                @block.sync
                def _(sp):
                    for stage, s in order:
                        if stage == "load":
                            sp.dma_start(xres[s][:], rows(x_in[pair * STREAMS + s])).then_inc(x_loaded[s], 16)
                            sp.dma_start(adj_sb[s][:], rows(adj[pair * STREAMS + s])).then_inc(adj_loaded[s], 16)
                        elif stage == "store":
                            sp.wait_ge(out_made[s], CT)
                            sp.dma_start(out_t[pair * STREAMS + s].rearrange("(c p) n -> p c n", p=P), hid_t[s][:])\
                                .then_inc(stored[s], 16)
                    for s in range(STREAMS):
                        sp.wait_ge(stored[s], 16)

                @block.gpsimd
                def _(pool):
                    for stage, s in order:
                        if stage == "query":
                            pool.wait_ge(turned_x[s], CT)
                            pool.tensor_tensor(xres[s][:], xres[s][:],
                                               bo[:].unsqueeze(1).to_broadcast([P, NT, D]), ALU.add)\
                                .then_inc(res_made[s], 1)
                        elif stage == "norm":
                            pool.wait_ge(stats_done[s], 2 * NT)
                            pool.tensor_scalar(veps[s][:], mean_var[s][:, :, 1], EPS, 1.0, ALU.add, ALU.mult)\
                                .then_inc(rstd_done[s], 1)
                            pool.wait_ge(rstd_done[s], 1)
                            pool.tensor_tensor(rstd[s][:], veps[s][:], power[:], ALU.pow).then_inc(rstd_done[s], 1)

                @block.tensor
                def _(pe):
                    def turn(s, src, done):
                        for c in range(CT):
                            for t in range(NT):
                                mm = pe.transpose(bank[s][:, c, t * P:(t + 1) * P],
                                                  src[:, t, c * P:(c + 1) * P], ident[:])
                            mm.then_inc(done, 1)

                    for stage, s in order:
                        if stage == "turn":
                            pe.wait_ge(x_loaded[s], 16)
                            turn(s, xres[s], turned_x[s])
                        elif stage == "query":
                            pe.wait_ge(feats_hi[s], CT)
                            pe.wait_ge(feats_lo[s], CT)
                            for b in range(CT):
                                for c in range(CT):
                                    mm = product(pe, bank[s][:, b],
                                                 (folded["qk"][0][:, c, b * P:(b + 1) * P],
                                                  folded["qk"][1][:, c, b * P:(b + 1) * P]),
                                                 (feats[s][:, 0, c], feats[s][:, 1, c]), c == 0, c == CT - 1)
                                mm.then_inc(q_done[s], 1)
                        elif stage == "value":
                            for t in range(NT):
                                for c in range(CT):
                                    mm = product(pe, bank[s][:, 2 + t // 2, t % 2 * D:(t % 2 + 1) * D],
                                                 (feats[s][:, 0, c, t * P:(t + 1) * P],
                                                  feats[s][:, 1, c, t * P:(t + 1) * P]),
                                                 (folded["vo"][0][:, c], folded["vo"][1][:, c]), c == 0, c == CT - 1)
                                if t % 2:
                                    mm.then_inc(v_done[s], 1)
                        elif stage in steps:
                            j = int(stage[4:])
                            if j < NT:
                                pe.wait_ge(q_hi[s], CT)
                                pe.wait_ge(q_lo[s], CT)
                                if j >= 2:
                                    pe.wait_ge(biased[s], j - 1)
                                for c in range(CT):
                                    mm = product(pe, bank[s][:, j % 2],
                                                 (query[s][:, 0, c, j * P:(j + 1) * P],
                                                  query[s][:, 1, c, j * P:(j + 1) * P]),
                                                 (feats[s][:, 0, c], feats[s][:, 1, c]), c == 0, c == CT - 1)
                                mm.then_inc(scores[s], 1)
                            i = j - lag_t
                            if 0 <= i < NT:
                                pe.wait_ge(probs[s], i + 1)
                                if i == 0:
                                    pe.wait_ge(v_ready[s], 2)
                                else:
                                    pe.wait_ge(copied[s], i)
                                for k in range(NT):
                                    mm = pe.transpose(bank[s][:, 2, k * P:(k + 1) * P],
                                                      prob[s][:, i, k * P:(k + 1) * P], ident[:])
                                mm.then_inc(turned[s], 1)
                            i = j - lag_v
                            if 0 <= i < NT:
                                pe.wait_ge(copied[s], i + 1)
                                if i >= 1:
                                    pe.wait_ge(x1_made[s], i)
                                for k in range(NT):
                                    mm = pe.matmul(bank[s][:, 3, 0:D],
                                                   probT[s][:, k, i * P:(i + 1) * P], value[s][:, k],
                                                   start=k == 0, stop=k == NT - 1)
                                mm.then_inc(mixed[s], 1)
                        elif stage == "turn_out":
                            pe.wait_ge(normed[s], NT)
                            turn(s, norm[s], turned_out[s])

                @block.scalar
                def _(act):
                    for stage, s in order:
                        if stage == "turn":
                            for c in range(CT):
                                act.wait_ge(turned_x[s], c + 1)
                                act.activation(feats[s][:, 0, c], bank[s][:, c], ACT.Copy).then_inc(feats_hi[s], 1)
                        elif stage == "query":
                            for b in range(CT):
                                act.wait_ge(q_done[s], b + 1)
                                act.activation(query[s][:, 0, b], bank[s][:, b], ACT.Copy).then_inc(q_hi[s], 1)
                        elif stage in steps:
                            j = int(stage[4:])
                            if j < NT:
                                act.wait_ge(biased[s], j + 1)
                                act.activation(prob[s][:, j], prob[s][:, j], ACT.Exp, bias=low[s][:, j:j + 1],
                                               scale=-1.0, accum_out=total[s][:, j:j + 1]).then_inc(probs[s], 1)
                            i = j - lag_t
                            if 0 <= i < NT:
                                act.wait_ge(turned[s], i + 1)
                                act.activation(probT[s][:, :, i * P:(i + 1) * P],
                                               bank[s][:, 2].rearrange("p (k q) -> p k q", q=P), ACT.Copy)\
                                    .then_inc(copied[s], 1)
                        elif stage == "turn_out":
                            for c in range(CT):
                                act.wait_ge(turned_out[s], c + 1)
                                act.activation(hid_t[s][:, c], bank[s][:, c], ACT.Identity,
                                               scale=ln_g[:, c:c + 1], bias=ln_b[:, c:c + 1]).then_inc(out_made[s], 1)

                @block.vector
                def _(dve):
                    for stage, s in order:
                        if stage == "load":
                            dve.wait_ge(adj_loaded[s], 16)
                            dve.tensor_scalar(bias[s][:], adj_sb[s][:], 0.0, MASKED, ALU.is_equal, ALU.mult)\
                                .then_inc(bias_made[s], 1)
                        elif stage == "turn":
                            for c in range(CT):
                                dve.wait_ge(feats_hi[s], c + 1)
                                dve.tensor_tensor(feats[s][:, 1, c], bank[s][:, c], feats[s][:, 0, c].bitcast(F32),
                                                  ALU.subtract).then_inc(feats_lo[s], 1)
                        elif stage == "query":
                            for b in range(CT):
                                dve.wait_ge(q_hi[s], b + 1)
                                dve.tensor_tensor(query[s][:, 1, b], bank[s][:, b], query[s][:, 0, b].bitcast(F32),
                                                  ALU.subtract).then_inc(q_lo[s], 1)
                        elif stage == "value":
                            for b in range(2):
                                dve.wait_ge(v_done[s], b + 1)
                                dve.tensor_copy(value[s][:, 2 * b:2 * b + 2],
                                                bank[s][:, 2 + b].rearrange("p (t d) -> p t d", d=D))\
                                    .then_inc(v_ready[s], 1)
                        elif stage in steps:
                            j = int(stage[4:])
                            if j < NT:
                                dve.wait_ge(scores[s], j + 1)
                                if j == 0:
                                    dve.wait_ge(bias_made[s], 1)
                                dve.tensor_tensor_reduce(prob[s][:, j], bank[s][:, j % 2], bias[s][:, j],
                                                         -scale, 3e38, ALU.add, ALU.min, low[s][:, j:j + 1])\
                                    .then_inc(biased[s], 1)
                            i = j - lag_v
                            if 0 <= i < NT:
                                if i == 0:
                                    dve.wait_ge(probs[s], NT)
                                    dve.reciprocal(total[s][:], total[s][:]).then_inc(inverse[s], 1)
                                    dve.wait_ge(inverse[s], 1)
                                    dve.wait_ge(res_made[s], 1)
                                dve.wait_ge(mixed[s], i + 1)
                                dve.scalar_tensor_tensor(
                                    out=xres[s][:, i], in0=bank[s][:, 3, 0:D],
                                    scalar=total[s][:, i:i + 1], in1=xres[s][:, i], op0=ALU.mult, op1=ALU.add)\
                                    .then_inc(x1_made[s], 1)
                        elif stage == "norm":
                            for t in range(NT):
                                dve.wait_ge(x1_made[s], t + 1)
                                dve.bn_stats(stat[s][:, t], xres[s][:, t]).then_inc(stats_done[s], 1)
                            for t in range(NT):
                                dve.wait_ge(stats_done[s], t + 1)
                                dve.bn_aggr(mean_var[s][:, t], stat[s][:, t]).then_inc(stats_done[s], 1)
                            dve.wait_ge(rstd_done[s], 2)
                            for t in range(NT):
                                dve.tensor_scalar(norm[s][:, t], xres[s][:, t], mean_var[s][:, t, 0:1],
                                                  rstd[s][:, t:t + 1], ALU.subtract, ALU.mult)\
                                    .then_inc(normed[s], 1)
            ph.clear()


def gated_phase(nc, name, hid_t, adj, out, w, graphs):
    with ExitStack() as ctx:
        ph = Phase(nc, ctx, name)
        gates = ("ri", "zi", "ni", "rh", "zh", "nh")
        split = {"wd": (ph.buf("wdh", [P, CT, LABELS * D], F32R), ph.buf("wdl", [P, CT, LABELS * D], F32R))}
        for k in gates:
            split["w" + k] = (ph.buf(f"w{k}h", [P, CT, D], F32R), ph.buf(f"w{k}l", [P, CT, D], F32R))
        ident, ident_b, power = ph.buf("ident", [P, P]), ph.buf("ident_b", [P, P], BF16), ph.buf("power", [P, NT])
        ones = ph.buf("ones", [P, 2], F32R)
        bd, ln_g, ln_b = ph.buf("bd", [P, D]), ph.buf("ln_g", [P, D]), ph.buf("ln_b", [P, D])
        gate_bias = {k: ph.buf("b" + k, [P, CT]) for k in gates}
        adj_sb = ph.bufs("adj", [P, NT, N], I32)
        adj_b, adj_t = ph.bufs("adj_b", [P, NT, N], BF16), ph.bufs("adj_t", [P, NT, N], BF16)
        hid = ph.bufs("hid", [P, CT, N])
        feats = ph.bufs("feats", [P, 2, CT, N], F32R)
        mask = ph.bufs("mask", [P, 2, NT, N], F32R)
        mapped = ph.bufs("mapped", [P, 2, NT, 2 * D], F32R)
        acc = ph.bufs("acc", [P, NT, D])
        gate_r, gate_z = ph.bufs("gate_r", [P, CT, N]), ph.bufs("gate_z", [P, CT, N])
        count = ph.bufs("count", [P, LABELS, NT])
        stat, mean_var = ph.bufs("stat", [P, NT, 6]), ph.bufs("mean_var", [P, NT, 2])
        veps, rstd = ph.bufs("veps", [P, NT]), ph.bufs("rstd", [P, NT])
        bank = [ctx.enter_context(nc.psum_tensor(f"{name}_bank{s}", [P, 4, N], F32)) for s in range(STREAMS)]
        agg = [mask[s][:, 0].rearrange("p (a c) n -> p a c n", a=2) for s in range(STREAMS)]
        cand = [adj_b[s][:].bitcast(F32).rearrange("p (c a) n -> p c (a n)", c=CT) for s in range(STREAMS)]
        new_t = [adj_t[s][:].bitcast(F32).rearrange("p (c a) n -> p c (a n)", c=CT) for s in range(STREAMS)]
        load_weights(
            nc, ph, [(w[k], *split[k]) for k in split],
            [(w["bd"].partition_broadcast(P), bd[:]), (w["ln_g"].partition_broadcast(P), ln_g[:]),
             (w["ln_b"].partition_broadcast(P), ln_b[:])] + [(w["b" + k], gate_bias[k][:]) for k in gates],
            [adj_sb[s][:].bitcast(F32).rearrange("p t n -> p (t n)") for s in range(STREAMS)]
            + [hid[s][:].rearrange("p t n -> p (t n)") for s in range(STREAMS)])
        make_constants(nc, ph, power, ident, ident_b)
        summed_bias = ph.sem("summed_bias")
        with nc.Block(no_gpsimd_drain=True) as block:
            @block.vector
            def _(dve):
                for k in ("r", "z"):
                    dve.tensor_tensor(gate_bias[k + "i"][:], gate_bias[k + "i"][:], gate_bias[k + "h"][:], ALU.add)\
                        .then_inc(summed_bias, 1)
                dve.tensor_scalar(ones[:], ident[:, 0:2], 0.0, 1.0, ALU.mult, ALU.add).then_inc(summed_bias, 1)
        adj_loaded, hid_loaded, adj_cast, adj_turned, adj_ready = (
            ph.sems(k) for k in ("adj_loaded", "hid_loaded", "adj_cast", "adj_turned", "adj_ready"))
        feats_hi, feats_lo, map_done, map_hi, map_lo = (
            ph.sems(k) for k in ("feats_hi", "feats_lo", "map_done", "map_hi", "map_lo"))
        masked, averaged, counted, added = (ph.sems(k) for k in ("masked", "averaged", "counted", "added"))
        agg_turned, agg_hi, agg_lo = (ph.sems(k) for k in ("agg_turned", "agg_hi", "agg_lo"))
        gate_done, gate_ready, reset_done, cand_in, cand_ready, mix_steps = (
            ph.sems(k) for k in ("gate_done", "gate_ready", "reset_done", "cand_in", "cand_ready", "mix_steps"))
        new_turned, stats_done, rstd_done, normed, gained, finished, stored = (
            ph.sems(k) for k in ("new_turned", "stats_done", "rstd_done", "normed", "gained", "finished", "stored"))

        stages = ["load", "adj", "split", "map0", "label0", "label1", "map1", "label2", "label3", "turn",
                  "gates0", "gates1", "turn_new", "norm", "store"]
        order = merged(stages, LAG)

        with nc.Fori(0, graphs // STREAMS) as pair:
            with nc.Block(no_gpsimd_drain=True) as block:
                @block.sync
                def _(sp):
                    for stage, s in order:
                        if stage == "load":
                            sp.dma_start(adj_sb[s][:], rows(adj[pair * STREAMS + s])).then_inc(adj_loaded[s], 16)
                            sp.dma_start(hid[s][:], hid_t[pair * STREAMS + s].rearrange("(c p) n -> p c n", p=P))\
                                .then_inc(hid_loaded[s], 16)
                        elif stage == "store":
                            sp.wait_ge(finished[s], 1)
                            sp.dma_start(rows(out[pair * STREAMS + s]), acc[s][:]).then_inc(stored[s], 16)
                    for s in range(STREAMS):
                        sp.wait_ge(stored[s], 16)

                @block.gpsimd
                def _(pool):
                    for stage, s in order:
                        if stage in ("gates0", "gates1"):
                            b = int(stage[5])
                            pool.wait_ge(cand_ready[s], b + 1)
                            if b == 0:
                                pool.wait_ge(masked[s], LABELS)
                            pool.tensor_tensor(new_t[s][:, b], hid[s][:, b], cand[s][:, b], ALU.subtract)\
                                .then_inc(mix_steps[s], 1)
                            pool.wait_ge(mix_steps[s], 3 * b + 1)
                            pool.wait_ge(gate_ready[s], 2 * b + 2)
                            pool.tensor_tensor(new_t[s][:, b], new_t[s][:, b], gate_z[s][:, b], ALU.mult)\
                                .then_inc(mix_steps[s], 1)
                            pool.wait_ge(mix_steps[s], 3 * b + 2)
                            pool.tensor_tensor(new_t[s][:, b], new_t[s][:, b], cand[s][:, b], ALU.add)\
                                .then_inc(mix_steps[s], 1)
                        elif stage == "norm":
                            pool.wait_ge(stats_done[s], 2 * NT)
                            pool.tensor_scalar(veps[s][:], mean_var[s][:, :, 1], EPS, 1.0, ALU.add, ALU.mult)\
                                .then_inc(rstd_done[s], 1)
                            pool.wait_ge(rstd_done[s], 1)
                            pool.tensor_tensor(rstd[s][:], veps[s][:], power[:], ALU.pow).then_inc(rstd_done[s], 1)

                @block.tensor
                def _(pe):
                    for stage, s in order:
                        if stage == "adj":
                            pe.wait_ge(adj_cast[s], 1)
                            for t in range(NT):
                                for q in range(NT):
                                    mm = pe.transpose(bank[s][:, t].bitcast(BF16)[:, q * P:(q + 1) * P],
                                                      adj_b[s][:, q, t * P:(t + 1) * P], ident_b[:])
                                mm.then_inc(adj_turned[s], 1)
                        elif stage in ("map0", "map1"):
                            half = int(stage[3])
                            if half:
                                pe.wait_ge(added[s], 2 * NT)
                            else:
                                pe.wait_ge(feats_hi[s], CT)
                                pe.wait_ge(feats_lo[s], CT)
                                pe.wait_ge(adj_ready[s], NT)
                            for t in range(NT):
                                for c in range(CT):
                                    mm = product(pe, bank[s][:, t],
                                                 (feats[s][:, 0, c, t * P:(t + 1) * P],
                                                  feats[s][:, 1, c, t * P:(t + 1) * P]),
                                                 (split["wd"][0][:, c, half * N:(half + 1) * N],
                                                  split["wd"][1][:, c, half * N:(half + 1) * N]), c == 0, c == CT - 1)
                                mm.then_inc(map_done[s], 1)
                        elif stage.startswith("label"):
                            d = int(stage[5])
                            pe.wait_ge(masked[s], d + 1)
                            pe.wait_ge(map_hi[s], NT * (d // 2 + 1))
                            pe.wait_ge(map_lo[s], NT * (d // 2 + 1))
                            for m in range(NT):
                                if d % 2:
                                    pe.wait_ge(added[s], NT * d)
                                for k in range(NT):
                                    near = mask[s][:, d % 2, k, m * P:(m + 1) * P]
                                    for a in range(2):
                                        pe.matmul(bank[s][:, m, 0:D], near,
                                                  mapped[s][:, a, k, d % 2 * D:(d % 2 + 1) * D],
                                                  start=k == 0 and a == 0, stop=k == NT - 1 and a == 1)
                                for k in range(NT):
                                    mm = pe.matmul(bank[s][:, m, D:D + 2], mask[s][:, d % 2, k, m * P:(m + 1) * P],
                                                   ones[:], start=k == 0, stop=k == NT - 1)
                                mm.then_inc(averaged[s], 1)
                        elif stage == "turn":
                            pe.wait_ge(added[s], LABELS * NT)
                            for c in range(CT):
                                for t in range(NT):
                                    mm = pe.transpose(bank[s][:, c, t * P:(t + 1) * P],
                                                      acc[s][:, t, c * P:(c + 1) * P], ident[:])
                                mm.then_inc(agg_turned[s], 1)
                        elif stage in ("gates0", "gates1"):
                            b = int(stage[5])
                            pe.wait_ge(agg_hi[s], CT)
                            pe.wait_ge(agg_lo[s], CT)
                            if b:
                                pe.wait_ge(gate_ready[s], 2)
                                pe.wait_ge(cand_in[s], 1)
                            for n, terms in enumerate((("ri", "rh"), ("zi", "zh"), ("nh",), ("ni",))):
                                for a, k in enumerate(terms):
                                    x = agg[s] if k[1] == "i" else feats[s]
                                    for c in range(CT):
                                        wh, wl = split["w" + k]
                                        mm = product(pe, bank[s][:, n],
                                                     (wh[:, c, b * P:(b + 1) * P], wl[:, c, b * P:(b + 1) * P]),
                                                     (x[:, 0, c], x[:, 1, c]), a == 0 and c == 0,
                                                     a == len(terms) - 1 and c == CT - 1)
                                mm.then_inc(gate_done[s], 1)
                        elif stage == "turn_new":
                            pe.wait_ge(mix_steps[s], 3 * CT)
                            pe.wait_ge(gate_ready[s], 2 * CT)
                            for t in range(NT):
                                for c in range(CT):
                                    mm = pe.transpose(bank[s][:, t // 2, (t % 2 * CT + c) * P:(t % 2 * CT + c + 1) * P],
                                                      new_t[s][:, c, t * P:(t + 1) * P], ident[:])
                                mm.then_inc(new_turned[s], 1)

                @block.scalar
                def _(act):
                    for stage, s in order:
                        if stage == "adj":
                            for t in range(NT):
                                act.wait_ge(adj_turned[s], t + 1)
                                act.activation(adj_t[s][:, t], bank[s][:, t].bitcast(BF16)[:, 0:N], ACT.Copy)\
                                    .then_inc(adj_ready[s], 1)
                        elif stage == "split":
                            act.wait_ge(hid_loaded[s], 16)
                            for c in range(CT):
                                act.activation(feats[s][:, 0, c], hid[s][:, c], ACT.Copy).then_inc(feats_hi[s], 1)
                        elif stage in ("map0", "map1"):
                            half = int(stage[3])
                            for t in range(NT):
                                act.wait_ge(map_done[s], NT * half + t + 1)
                                act.activation(mapped[s][:, 0, t], bank[s][:, t], ACT.Copy).then_inc(map_hi[s], 1)
                        elif stage == "turn":
                            for c in range(CT):
                                act.wait_ge(agg_turned[s], c + 1)
                                act.activation(agg[s][:, 0, c], bank[s][:, c], ACT.Relu).then_inc(agg_hi[s], 1)
                        elif stage in ("gates0", "gates1"):
                            b = int(stage[5])
                            for n, (to, k) in enumerate(((gate_r, "ri"), (gate_z, "zi"))):
                                act.wait_ge(gate_done[s], 4 * b + n + 1)
                                act.activation(to[s][:, b], bank[s][:, n], ACT.Sigmoid,
                                               bias=gate_bias[k][:, b:b + 1]).then_inc(gate_ready[s], 1)
                            act.wait_ge(cand_in[s], b + 1)
                            act.activation(cand[s][:, b], cand[s][:, b], ACT.Tanh).then_inc(cand_ready[s], 1)

                @block.vector
                def _(dve):
                    for stage, s in order:
                        if stage == "load":
                            dve.wait_ge(adj_loaded[s], 16)
                            dve.tensor_copy(adj_b[s][:], adj_sb[s][:]).then_inc(adj_cast[s], 1)
                        elif stage == "split":
                            for c in range(CT):
                                dve.wait_ge(feats_hi[s], c + 1)
                                dve.tensor_tensor(feats[s][:, 1, c], hid[s][:, c], feats[s][:, 0, c].bitcast(F32),
                                                  ALU.subtract).then_inc(feats_lo[s], 1)
                        elif stage in ("map0", "map1"):
                            half = int(stage[3])
                            for d in (2 * half, 2 * half + 1):
                                dve.wait_ge(adj_ready[s], NT)
                                if half:
                                    dve.wait_ge(averaged[s], NT * (d - 1))
                                dve.tensor_scalar(mask[s][:, d % 2], adj_t[s][:], float(d + 1), None, ALU.is_equal)\
                                    .then_inc(masked[s], 1)
                            for t in range(NT):
                                dve.wait_ge(map_hi[s], NT * half + t + 1)
                                dve.tensor_tensor(mapped[s][:, 1, t], bank[s][:, t], mapped[s][:, 0, t].bitcast(F32),
                                                  ALU.subtract).then_inc(map_lo[s], 1)
                        elif stage.startswith("label"):
                            d = int(stage[5])
                            dve.wait_ge(averaged[s], NT * (d + 1))
                            dve.tensor_scalar(count[s][:, d], bank[s][:, :, D], 1e-8, None, ALU.add)\
                                .then_inc(counted[s], 1)
                            dve.wait_ge(counted[s], 2 * d + 1)
                            dve.reciprocal(count[s][:, d], count[s][:, d]).then_inc(counted[s], 1)
                            dve.wait_ge(counted[s], 2 * d + 2)
                            for m in range(NT):
                                if d:
                                    dve.wait_ge(added[s], NT * (d - 1) + m + 1)
                                dve.scalar_tensor_tensor(
                                    out=acc[s][:, m], in0=bank[s][:, m, 0:D], scalar=count[s][:, d, m:m + 1],
                                    in1=acc[s][:, m] if d else bd[:], op0=ALU.mult, op1=ALU.add)\
                                    .then_inc(added[s], 1)
                        elif stage == "turn":
                            for c in range(CT):
                                dve.wait_ge(agg_hi[s], c + 1)
                                dve.scalar_tensor_tensor(
                                    out=agg[s][:, 1, c], in0=bank[s][:, c], scalar=0.0,
                                    in1=agg[s][:, 0, c].bitcast(F32), op0=ALU.max, op1=ALU.subtract)\
                                    .then_inc(agg_lo[s], 1)
                        elif stage in ("gates0", "gates1"):
                            b = int(stage[5])
                            dve.wait_ge(gate_ready[s], 2 * b + 1)
                            dve.wait_ge(gate_done[s], 4 * b + 3)
                            dve.scalar_tensor_tensor(out=gate_r[s][:, b], in0=bank[s][:, 2],
                                                     scalar=gate_bias["nh"][:, b:b + 1], in1=gate_r[s][:, b],
                                                     op0=ALU.add, op1=ALU.mult).then_inc(reset_done[s], 1)
                            dve.wait_ge(reset_done[s], b + 1)
                            dve.wait_ge(gate_done[s], 4 * b + 4)
                            dve.scalar_tensor_tensor(out=cand[s][:, b], in0=bank[s][:, 3],
                                                     scalar=gate_bias["ni"][:, b:b + 1], in1=gate_r[s][:, b],
                                                     op0=ALU.add, op1=ALU.add).then_inc(cand_in[s], 1)
                        elif stage == "norm":
                            rows_of = [bank[s][:, t // 2, t % 2 * D:(t % 2 + 1) * D] for t in range(NT)]
                            for t in range(NT):
                                dve.wait_ge(new_turned[s], t // 2 * 2 + 2)
                                dve.bn_stats(stat[s][:, t], rows_of[t]).then_inc(stats_done[s], 1)
                            for t in range(NT):
                                dve.wait_ge(stats_done[s], t + 1)
                                dve.bn_aggr(mean_var[s][:, t], stat[s][:, t]).then_inc(stats_done[s], 1)
                            dve.wait_ge(rstd_done[s], 2)
                            for t in range(NT):
                                dve.tensor_scalar(acc[s][:, t], rows_of[t], mean_var[s][:, t, 0:1],
                                                  rstd[s][:, t:t + 1], ALU.subtract, ALU.mult).then_inc(normed[s], 1)
                            dve.wait_ge(normed[s], NT)
                            dve.tensor_tensor(acc[s][:], acc[s][:], ln_g[:].unsqueeze(1).to_broadcast([P, NT, D]),
                                              ALU.mult).then_inc(gained[s], 1)
                            dve.wait_ge(gained[s], 1)
                            dve.tensor_tensor(acc[s][:], acc[s][:], ln_b[:].unsqueeze(1).to_broadcast([P, NT, D]),
                                              ALU.add).then_inc(finished[s], 1)
            ph.clear()


def build(nc, a, out, graphs, only=None, x_in=None):
    x1 = nc.dram_tensor("x1", [graphs, N, D], F32, kind="Internal").ap()
    x2 = nc.dram_tensor("x2", [graphs, N, D], F32, kind="Internal").ap()
    x3_t = nc.dram_tensor("x3_t", [graphs, D, N], F32, kind="Internal").ap()
    adj = a["adj"]
    l0 = {k: a["L0_gnn_" + k] for k in ("wq", "wk", "wv", "wo", "w1", "w2", "bq", "bk", "bv", "bo", "b1", "b2",
                                        "ln1_g", "ln1_b", "ln2_g", "ln2_b")}
    encoder_phase(nc, "l0", a["x"], adj, x1, l0, graphs, True)
    l1 = {k: a["L1_gnn_W" + k[1]] for k in ("wq", "wk", "wv", "wo")} | {k: a["L1_gnn_" + k] for k in ("bq", "bk", "bv", "bo")}
    encoder_phase(nc, "l1", x1, adj, x2, l1 | {"ln_g": a["L1_gnn_gamma"], "ln_b": a["L1_gnn_beta"]}, graphs, False)
    l2 = {"wq_t": a["L2_gnn_Wq"], "wk_t": a["L2_gnn_Wk"], "wv_t": a["L2_gnn_Wv"], "wo": a["L2_gnn_Wo"],
          "bo": a["L2_gnn_bo"], "ln_g": a["L2_gnn_gamma"], "ln_b": a["L2_gnn_beta"]}
    graph_attention_phase(nc, "l2", x2, adj, x3_t, l2, graphs)
    gates = ("ri", "zi", "ni", "rh", "zh", "nh")
    l3 = {"wd": a["L3_gnn_Wd"], "bd": a["L3_gnn_bd"], "ln_g": a["L3_gnn_gamma"], "ln_b": a["L3_gnn_beta"]}
    l3 |= {"w" + k: a["L3_gnn_W" + k] for k in gates} | {"b" + k: a["L3_gnn_b" + k] for k in gates}
    gated_phase(nc, "l3", x3_t, adj, out, l3, graphs)


TRANSPOSED = ("L2_gnn_Wq", "L2_gnn_Wk", "L2_gnn_Wv") + tuple("L3_gnn_W" + k for k in ("ri", "zi", "ni", "rh", "zh", "nh"))

COLUMNS = tuple("L0_gnn_" + k for k in ("bq", "bk", "bv", "b1", "ln1_g", "ln1_b", "ln2_g", "ln2_b")) + (
    "L1_gnn_bq", "L1_gnn_bk", "L1_gnn_bv", "L2_gnn_gamma", "L2_gnn_beta") + tuple(
    "L3_gnn_b" + k for k in ("ri", "zi", "ni", "rh", "zh", "nh"))


def laid_out(name, a):
    if name in COLUMNS:
        return np.ascontiguousarray(a.reshape(-1, P).T)
    if name in TRANSPOSED:
        return np.ascontiguousarray(a.T)
    if name == "L3_gnn_Wd":
        return np.ascontiguousarray(a.reshape(D, LABELS, D).transpose(2, 1, 0).reshape(D, LABELS * D))
    return np.ascontiguousarray(a)


def kernel(**inputs):
    import concourse.bacc as bacc
    from concourse.bass_utils import run_bass_kernel_spmd

    nc = bacc.Bacc("TRN2", target_bir_lowering=False, num_devices=1)
    arrays = {name: laid_out(name, np.asarray(a)) for name, a in inputs.items()}
    args = {name: nc.dram_tensor(name, a.shape, mybir.dt.from_np(a.dtype), kind="ExternalInput").ap()
            for name, a in arrays.items()}
    graphs = arrays["x"].shape[0]
    out = nc.dram_tensor("out", (graphs, N, D), F32, kind="ExternalOutput").ap()
    build(nc, args, out, graphs)
    result = run_bass_kernel_spmd(nc, [arrays], core_ids=[0])
    return result.results[0]["out"]
```

```python
from contextlib import ExitStack

import concourse.bass as bass
import numpy as np
from concourse import mybir

F32 = mybir.dt.float32
F32R = mybir.dt.float32r
BF16 = mybir.dt.bfloat16
I32 = mybir.dt.int32
ALU = mybir.AluOpType
ACT = mybir.ActivationFunctionType

P = 128
N = 512
D = 256
HEADS = 8
HD = D // HEADS
NT = N // P
CT = D // P
GROUPS = CT
GH = HEADS // GROUPS
FF = 4 * D
LABELS = 4
STREAMS = 2
EPS = 1e-5
MASKED = -(2.0 ** 100)
HEAD_SCALE = float(HD) ** -0.5
TILES = HEADS * NT

LAG_T = 3
LAG_V = LAG_T + 5
STEPS = TILES + LAG_V
STACKED = 16 * 4


def merged(stages, lag):
    order = []
    for t in range(len(stages) + lag):
        if t < len(stages):
            order.append((stages[t], 0))
        if t >= lag:
            order.append((stages[t - lag], 1))
    return order


class Phase:

    def __init__(self, nc, ctx, name):
        self.nc, self.ctx, self.name = nc, ctx, name
        self.all = []

    def buf(self, name, shape, dt=F32):
        return self.ctx.enter_context(self.nc.sbuf_tensor(f"{self.name}_{name}", shape, dt))

    def bufs(self, name, shape, dt=F32):
        return [self.buf(f"{name}{s}", shape, dt) for s in range(STREAMS)]

    def sem(self, name):
        h = self.ctx.enter_context(self.nc.semaphore(f"{self.name}_{name}"))
        self.all.append(h)
        return h

    def sems(self, name):
        return [self.sem(f"{name}{s}") for s in range(STREAMS)]

    def clear(self):
        nums = [h.num for h in self.all]
        self.nc.all_engine_barrier(sems_to_clear=range(min(nums), max(nums) + 1))


def rows(ap):
    return ap.rearrange("(t p) n -> p t n", p=P)


def product(pe, out, left, right, first, last):
    (lh, ll), (rh, rl) = left, right
    pe.matmul(out, lh, rh, start=first, stop=False)
    pe.matmul(out, ll, rh, start=False, stop=False)
    return pe.matmul(out, lh, rl, start=False, stop=last)


def load_weights(nc, ph, weights, vectors, staging):
    loaded, parts = ph.sem("weights_loaded"), ph.sem("weights_split")
    places, used = [], [0] * len(staging)
    for src, hi, lo in weights:
        k, m = src.shape
        size = k // P * m
        n = next(i for i, b in enumerate(staging) if used[i] + size <= b.shape[1])
        places.append(staging[n][:, used[n]:used[n] + size].rearrange("p (t m) -> p t m", m=m))
        used[n] += size
    with nc.Block(no_gpsimd_drain=True) as block:
        @block.sync
        def _(sp):
            for (src, _, _), raw in zip(weights, places):
                sp.dma_start(raw, src.rearrange("(t p) m -> p t m", p=P)).then_inc(loaded, 16)
            for src, to in vectors:
                sp.dma_start(to, src).then_inc(loaded, 16)
            sp.wait_ge(loaded, 16 * (len(weights) + len(vectors)))

        @block.vector
        def _(dve):
            dve.wait_ge(loaded, 16 * (len(weights) + len(vectors)))
            for n, ((_, hi, lo), raw) in enumerate(zip(weights, places)):
                dve.tensor_copy(hi[:], raw).then_inc(parts, 1)
                dve.wait_ge(parts, 2 * n + 1)
                dve.tensor_tensor(lo[:], raw, hi[:].bitcast(F32), ALU.subtract).then_inc(parts, 1)
            dve.wait_ge(parts, 2 * len(weights))


def make_constants(nc, ph, power, ident, *others):
    made = ph.sem("identity_made")
    with nc.Block(no_gpsimd_drain=True) as block:
        @block.gpsimd
        def _(pool):
            pool.memset(power[:], -0.5)
            pool.memset(ident[:], 0.0).then_inc(made, 1)
            pool.wait_ge(made, 1)
            pool.affine_select(out=ident[:], in_=ident[:], compare_op=ALU.not_equal, fill=1.0, base=0,
                               pattern=[[-1, P]], channel_multiplier=1).then_inc(made, 1)
            pool.wait_ge(made, 2)
            for n, other in enumerate(others):
                pool.tensor_copy(other[:], ident[:]).then_inc(made, 1)
            pool.wait_ge(made, 2 + len(others))


def encoder_phase(nc, name, x_in, adj, out, w, graphs, ffn):
    with ExitStack() as ctx:
        ph = Phase(nc, ctx, name)
        split = {}
        for k, m in (("wq", D), ("wk", D), ("wv", D), ("wo", D)) + ((("w1", FF),) if ffn else ()):
            split[k] = (ph.buf(k + "h", [P, CT, m], F32R), ph.buf(k + "l", [P, CT, m], F32R))
        if ffn:
            split["w2"] = (ph.buf("w2h", [P, FF // P, D], F32R), ph.buf("w2l", [P, FF // P, D], F32R))
        ident = ph.buf("ident", [P, P])
        power = ph.buf("power", [P, NT])
        bq, bk, bv = ph.buf("bq", [P, CT]), ph.buf("bk", [P, CT]), ph.buf("bv", [P, CT])
        bo = ph.buf("bo", [P, D])
        if ffn:
            ln1_g, ln1_b = ph.buf("ln1_g", [P, CT]), ph.buf("ln1_b", [P, CT])
            ln2_g, ln2_b = ph.buf("ln2_g", [P, CT]), ph.buf("ln2_b", [P, CT])
            b1, b2 = ph.buf("b1", [P, FF // P]), ph.buf("b2", [P, D])
        else:
            ln_g, ln_b = ph.buf("ln_g", [P, D]), ph.buf("ln_b", [P, D])
        xres = ph.bufs("xres", [P, NT, D])
        bias = ph.bufs("bias", [P, NT, N], F32 if ffn else BF16)
        norm = ph.bufs("norm", [P, NT, D])
        feats = ph.bufs("feats", [P, 2, CT, N], F32R)
        parts = ph.bufs("parts", [P, 4, N], F32R)
        stack = ph.bufs("stack", [P, 2, GH, N], F32R)
        value = ph.bufs("value", [P, NT, D])
        prob = ph.bufs("prob", [P, 4, N])
        probT = ph.bufs("probT", [P, 2, NT, N])
        low = ph.bufs("low", [P, TILES])
        total = ph.bufs("total", [P, TILES])
        stat, mean_var = ph.bufs("stat", [P, NT, 6]), ph.bufs("mean_var", [P, NT, 2])
        veps, rstd = ph.bufs("veps", [P, NT]), ph.bufs("rstd", [P, NT])
        bank = [ctx.enter_context(nc.psum_tensor(f"{name}_bank{s}", [P, 4, N], F32)) for s in range(STREAMS)]
        adj_sb = [probT[s][:, 0].bitcast(I32) for s in range(STREAMS)]
        sq = [probT[s][:, 1] for s in range(STREAMS)]
        normT = [norm[s][:].rearrange("p t d -> p (t d)").rearrange("p (c n) -> p c n", c=CT) for s in range(STREAMS)]
        mixT = [parts[s][:].rearrange("p (a c) n -> p a c n", a=2) for s in range(STREAMS)]
        wide = [prob[s][:, 0:2].rearrange("p a n -> p (a n)").rearrange("p (q d) -> p q d", d=D)
                for s in range(STREAMS)]
        hidden = stack

        load_weights(
            nc, ph, [(w[k], *split[k]) for k in split],
            [(w["bq"], bq[:]), (w["bk"], bk[:]), (w["bv"], bv[:]),
             (w["bo"].partition_broadcast(P), bo[:])]
            + ([(w["ln1_g"], ln1_g[:]), (w["ln1_b"], ln1_b[:]), (w["ln2_g"], ln2_g[:]),
                (w["ln2_b"], ln2_b[:]), (w["b1"], b1[:]), (w["b2"].partition_broadcast(P), b2[:])]
               if ffn else [(w["ln_g"].partition_broadcast(P), ln_g[:]), (w["ln_b"].partition_broadcast(P), ln_b[:])]),
            [probT[s][:].rearrange("p a t n -> p (a t n)") for s in range(STREAMS)])
        make_constants(nc, ph, power, ident)
        x_loaded, adj_loaded = ph.sems("x_loaded"), ph.sems("adj_loaded")
        bias_made = ph.sems("bias_made")
        res_made = ph.sems("res_made")
        stats_done, rstd_done, normed = ph.sems("stats_done"), ph.sems("rstd_done"), ph.sems("normed")
        turned_x, feats_hi, feats_lo = ph.sems("turned_x"), ph.sems("feats_hi"), ph.sems("feats_lo")
        qk_done, qk_hi, qk_lo = ph.sems("qk_done"), ph.sems("qk_hi"), ph.sems("qk_lo")
        stacked = [ph.sems(f"stacked{h}_") for h in range(GH)]
        v_done, v_ready = ph.sems("v_done"), ph.sems("v_ready")
        scores, biased, probs, turned = ph.sems("scores"), ph.sems("biased"), ph.sems("probs"), ph.sems("turned")
        copied_dve, copied_act = ph.sems("copied_dve"), ph.sems("copied_act")
        mixed, mix_raw, inverse, spread = ph.sems("mixed"), ph.sems("mix_raw"), ph.sems("inverse"), ph.sems("spread")
        mix_scaled, mix_hi, mix_lo = ph.sems("mix_scaled"), ph.sems("mix_hi"), ph.sems("mix_lo")
        projected, x1_made = ph.sems("projected"), ph.sems("x1_made")
        hid_done, hid_gelu, hid_hi, hid_lo = ph.sems("hid_done"), ph.sems("hid_gelu"), ph.sems("hid_hi"), ph.sems("hid_lo")
        down_done, summed, stored = ph.sems("down_done"), ph.sems("summed"), ph.sems("stored")
        feats_full = ph.sems("feats_full")

        stages = ["qk0", "v"] + [f"heads{j}" for j in range(STEPS)]
        for place, stage in ((3, "q1"), (4, "k1")):
            stages.insert(stages.index(f"heads{place}") + 1, stage)
        if ffn:
            stages += ["mix", "scale", "load", "split_mix", "project", "x1", "stats2", "norm2", "turn2",
                       "feats2", "bias", "up0", "split0", "up1", "split1", "up2", "split2", "up3", "split3",
                       "stats1", "up4", "up5", "norm1", "down0", "split4", "split5", "sum0", "up6", "split6",
                       "up7", "split7", "sum1", "down1", "turn1", "feats1", "store"]
            prepare = ["load", "bias", "stats1", "norm1", "turn1", "feats1"]
        else:
            stages += ["mix", "load", "scale", "split_mix", "turn1", "project", "x1", "stats2", "norm2", "bias",
                       "feats1", "store"]
            prepare = ["load", "turn1", "feats1", "bias"]
        split_stages = [f"split{i}" for i in range(FF // P)]
        stage_parts = {"qk0": (0, 1), "q1": (2,), "k1": (3,)}
        first_group = ["qk0", "v", "heads0", "heads1"]
        second_group = [f"heads{max((h + 1) * NT - 1, 5)}" for h in range(GH)]

        def wait_copied(eng, s, i):
            eng.wait_ge(copied_dve[s], i // 2 + 1)
            if i >= 1:
                eng.wait_ge(copied_act[s], (i + 1) // 2)

        def out_tile(ap, i):
            h, q = divmod(i, NT)
            return ap[:, h % 2, :, q * P:(q + 1) * P]

        def emit(order, graph, following):
            early = 0 if graph is None or not ffn else 1

            with nc.Block(no_gpsimd_drain=True) as block:
                @block.sync
                def _(sp):
                    def stack_head(s, h):
                        src = parts[s][HD * h:HD * (h + 1)].bitcast(F32)
                        for n, part in enumerate((src[:, 0::2], src[:, 0::3], src[:, 1:3], src[:, 1::2])):
                            sp.dma_start(stack[s][HD * n:HD * (n + 1), :, h].bitcast(F32), part)\
                                .then_inc(stacked[h][s], 16)

                    for stage, s in order:
                        if stage == "load":
                            if graph is not None:
                                sp.wait_ge(mixed[s], HEADS)
                            sp.dma_start(value[s][:], rows(x_in[following + s])).then_inc(x_loaded[s], 16)
                            sp.dma_start(adj_sb[s], rows(adj[following + s])).then_inc(adj_loaded[s], 16)
                        elif stage in first_group:
                            if stage == "qk0":
                                sp.wait_ge(qk_hi[s], 2)
                                sp.wait_ge(qk_lo[s], 2)
                            stack_head(s, first_group.index(stage))
                        elif stage in second_group:
                            h = second_group.index(stage)
                            sp.wait_ge(qk_hi[s], 4)
                            sp.wait_ge(qk_lo[s], 4)
                            sp.wait_ge(scores[s], NT * (h + 1))
                            stack_head(s, h)
                        elif stage == "store":
                            sp.wait_ge(summed[s], 4 if ffn else NT)
                            sp.dma_start(rows(out[graph + s]), xres[s][:]).then_inc(stored[s], 16)
                    if graph is not None:
                        for s in range(STREAMS):
                            sp.wait_ge(stored[s], 16)

                @block.gpsimd
                def _(pool):
                    def reciprocal_root(s, n):
                        pool.wait_ge(stats_done[s], 2 * NT * (n + 1))
                        pool.tensor_scalar(veps[s][:], mean_var[s][:, :, 1], EPS, 1.0, ALU.add, ALU.mult)\
                            .then_inc(rstd_done[s], 1)
                        pool.wait_ge(rstd_done[s], 2 * n + 1)
                        pool.tensor_tensor(rstd[s][:], veps[s][:], power[:], ALU.pow).then_inc(rstd_done[s], 1)

                    for stage, s in order:
                        if stage == "stats1":
                            reciprocal_root(s, early)
                        elif stage == "stats2":
                            reciprocal_root(s, 0)
                        elif stage == "qk0":
                            pool.tensor_tensor(xres[s][:], value[s][:],
                                               bo[:].unsqueeze(1).to_broadcast([P, NT, D]), ALU.add)\
                                .then_inc(res_made[s], 1)
                        elif stage == "norm2" and ffn:
                            pool.wait_ge(normed[s], NT)
                            pool.tensor_tensor(xres[s][:], xres[s][:],
                                               b2[:].unsqueeze(1).to_broadcast([P, NT, D]), ALU.add)\
                                .then_inc(res_made[s], 1)

                @block.tensor
                def _(pe):
                    def turn(s, src, ready):
                        for sem, count in ready:
                            pe.wait_ge(sem, count)
                        for c in range(CT):
                            for t in range(NT):
                                mm = pe.transpose(bank[s][:, c, t * P:(t + 1) * P],
                                                  src[:, t, c * P:(c + 1) * P], ident[:])
                            mm.then_inc(turned_x[s], 1)

                    def feature(s, c, lo, hi):
                        return feats[s][:, 0, c, lo:hi], feats[s][:, 1, c, lo:hi]

                    def weight(k, c, lo, hi):
                        return split[k][0][:, c, lo:hi], split[k][1][:, c, lo:hi]

                    def step(s, j):
                        if j < TILES:
                            h, q = divmod(j, NT)
                            if q == 0:
                                pe.wait_ge(stacked[h % GH][s], STACKED * (h // GH + 1))
                            if j == 0:
                                pe.wait_ge(v_ready[s], 2)
                                pe.wait_ge(qk_hi[s], 2)
                                pe.wait_ge(qk_lo[s], 2)
                            if j - 2 - LAG_T >= 0:
                                wait_copied(pe, s, j - 2 - LAG_T)
                            elif j >= 3:
                                pe.wait_ge(biased[s], j - 2)
                            pe.matmul(bank[s][:, 2 * j % 3], stack[s][:, 0, h % GH, q * P:(q + 1) * P],
                                      stack[s][:, 1, h % GH], start=True, stop=True).then_inc(scores[s], 1)
                        i = j - LAG_T
                        if 0 <= i < TILES:
                            pe.wait_ge(probs[s], i + 1)
                            if j - 1 < TILES:
                                pe.wait_ge(biased[s], j)
                            else:
                                wait_copied(pe, s, i - 3)
                            for k in range(NT):
                                mm = pe.transpose(bank[s][:, (2 * j + 1) % 3, k * P:(k + 1) * P],
                                                  prob[s][:, i % 4, k * P:(k + 1) * P], ident[:])
                            mm.then_inc(turned[s], 1)
                        i = j - LAG_V
                        if 0 <= i < TILES:
                            h, k = divmod(i, NT)
                            if k == 0:
                                wait_copied(pe, s, NT * h + NT - 1)
                                if h == 0:
                                    pe.wait_ge(qk_hi[s], 4)
                                    pe.wait_ge(qk_lo[s], 4)
                                if h == GH:
                                    pe.wait_ge(mix_raw[s], 1)
                            mm = pe.matmul(bank[s][HD * (h % GH):HD * (h % GH + 1), 3],
                                           value[s][:, k, HD * h:HD * (h + 1)], probT[s][:, h % 2, k],
                                           start=k == 0, stop=k == NT - 1)
                            if k == NT - 1:
                                mm.then_inc(mixed[s], 1)

                    for stage, s in order:
                        if stage == "turn1":
                            ready = [(normed[s], NT * (early + 1))] if ffn else [(x_loaded[s], 16)]
                            if graph is not None:
                                ready += [(hid_gelu[s], FF // P)] if ffn else [(mix_scaled[s], 2 * GROUPS)]
                            turn(s, norm[s] if ffn else value[s], ready)
                        elif stage in stage_parts:
                            for n in stage_parts[stage]:
                                if n == 2:
                                    pe.wait_ge(v_ready[s], 2)
                                if n == 3:
                                    pe.wait_ge(qk_hi[s], 3)
                                    pe.wait_ge(qk_lo[s], 3)
                                for c in range(CT):
                                    mm = product(pe, bank[s][:, n if n < 2 else 3],
                                                 weight(("wq", "wk")[n % 2], c, n // 2 * P, (n // 2 + 1) * P),
                                                 feature(s, c, 0, N), c == 0, c == CT - 1)
                                mm.then_inc(qk_done[s], 1)
                        elif stage == "v":
                            for t in range(NT):
                                for c in range(CT):
                                    mm = product(pe, bank[s][:, 2 + t // 2, t % 2 * D:(t % 2 + 1) * D],
                                                 feature(s, c, t * P, (t + 1) * P), weight("wv", c, 0, D),
                                                 c == 0, c == CT - 1)
                                if t % 2:
                                    mm.then_inc(v_done[s], 1)
                        elif stage.startswith("heads"):
                            step(s, int(stage[5:]))
                        elif stage == "mix":
                            pe.wait_ge(inverse[s], 2)
                            wait_copied(pe, s, TILES - 1)
                            for g in range(GROUPS):
                                for q in range(NT):
                                    mm = pe.transpose(bank[s][:, g, q * P:(q + 1) * P],
                                                      wide[s][:, q, g * P:(g + 1) * P], ident[:])
                                mm.then_inc(spread[s], 1)
                        elif stage == "project":
                            pe.wait_ge(mix_raw[s], GROUPS)
                            pe.wait_ge(mix_hi[s], GROUPS)
                            pe.wait_ge(mix_lo[s], GROUPS)
                            for t in range(NT):
                                for c in range(CT):
                                    mm = product(pe, bank[s][:, 2 + t // 2, t % 2 * D:(t % 2 + 1) * D],
                                                 (mixT[s][:, 0, c, t * P:(t + 1) * P],
                                                  mixT[s][:, 1, c, t * P:(t + 1) * P]),
                                                 weight("wo", c, 0, D), c == 0, c == CT - 1)
                                if t % 2:
                                    mm.then_inc(projected[s], 1)
                        elif stage == "turn2":
                            turn(s, norm[s], [(normed[s], NT)])
                        elif stage.startswith("up"):
                            i = int(stage[2])
                            if i == 0:
                                pe.wait_ge(feats_hi[s], CT)
                                pe.wait_ge(feats_lo[s], CT)
                            if i >= 2:
                                pe.wait_ge(hid_gelu[s], i - 1)
                            for c in range(CT):
                                mm = product(pe, bank[s][:, i % 2], weight("w1", c, i * P, (i + 1) * P),
                                             feature(s, c, 0, N), c == 0, c == CT - 1)
                            mm.then_inc(hid_done[s], 1)
                        elif stage in ("down0", "down1"):
                            half = int(stage[4])
                            pe.wait_ge(hid_lo[s], 4 * half + 4)
                            if half:
                                pe.wait_ge(summed[s], 2)
                            for t in range(NT):
                                for k in range(4):
                                    mm = product(pe, bank[s][:, 2 + t // 2, t % 2 * D:(t % 2 + 1) * D],
                                                 (hidden[s][:, 0, k, t * P:(t + 1) * P],
                                                  hidden[s][:, 1, k, t * P:(t + 1) * P]),
                                                 weight("w2", 4 * half + k, 0, D), k == 0, k == 3)
                                if t % 2:
                                    mm.then_inc(down_done[s], 1)

                @block.scalar
                def _(act):
                    for stage, s in order:
                        if stage in ("feats1", "feats2"):
                            n = early if stage == "feats1" else 0
                            for c in range(CT):
                                act.wait_ge(turned_x[s], CT * n + (CT if ffn else c + 1))
                                if ffn:
                                    gain, off = (ln1_g, ln1_b) if stage == "feats1" else (ln2_g, ln2_b)
                                    act.activation(normT[s][:, c], bank[s][:, c], ACT.Identity,
                                                   scale=gain[:, c:c + 1], bias=off[:, c:c + 1])\
                                        .then_inc(feats_full[s], 1)
                                    act.wait_ge(feats_full[s], CT * n + c + 1)
                                    act.activation(feats[s][:, 0, c], normT[s][:, c], ACT.Copy)\
                                        .then_inc(feats_hi[s], 1)
                                else:
                                    act.activation(feats[s][:, 0, c], bank[s][:, c], ACT.Copy)\
                                        .then_inc(feats_hi[s], 1)
                        elif stage in stage_parts:
                            for n in stage_parts[stage]:
                                act.wait_ge(qk_done[s], n + 1)
                                if n == 2:
                                    for copied_head in stacked:
                                        act.wait_ge(copied_head[s], STACKED)
                                act.activation(parts[s][:, 2 * (n % 2)], bank[s][:, n if n < 2 else 3], ACT.Identity,
                                               bias=(bq, bk)[n % 2][:, n // 2:n // 2 + 1]).then_inc(qk_hi[s], 1)
                        elif stage.startswith("heads"):
                            j = int(stage[5:])
                            if j < TILES:
                                act.wait_ge(biased[s], j + 1)
                                act.activation(prob[s][:, j % 4], prob[s][:, j % 4], ACT.Exp,
                                               bias=low[s][:, j:j + 1], scale=-1.0,
                                               accum_out=total[s][:, j:j + 1]).then_inc(probs[s], 1)
                            i = j - LAG_T
                            if 0 <= i < TILES and i % 2:
                                act.wait_ge(turned[s], i + 1)
                                if i >= 2 * NT:
                                    act.wait_ge(mixed[s], i // NT - 1)
                                act.activation(
                                    out_tile(probT[s], i),
                                    bank[s][:, (2 * j + 1) % 3].rearrange("p (k q) -> p k q", q=P),
                                    ACT.Copy).then_inc(copied_act[s], 1)
                            i = j - LAG_V
                            if 0 <= i < TILES and i % (GH * NT) == GH * NT - 1:
                                g = i // (GH * NT)
                                act.wait_ge(mixed[s], GH * (g + 1))
                                act.activation(normT[s][:, g], bank[s][:, 3], ACT.Copy)\
                                    .then_inc(mix_raw[s], 1)
                        elif stage == "scale":
                            for copied_head in stacked:
                                act.wait_ge(copied_head[s], GROUPS * STACKED)
                            for g in range(GROUPS):
                                act.wait_ge(mix_scaled[s], 2 * g + 2)
                                act.activation(mixT[s][:, 0, g], normT[s][:, g], ACT.Copy).then_inc(mix_hi[s], 1)
                        elif stage.startswith("up"):
                            i = int(stage[2])
                            act.wait_ge(hid_done[s], i + 1)
                            if i >= 4:
                                act.wait_ge(hid_lo[s], i - 3)
                            act.activation(prob[s][:, i % 4], bank[s][:, i % 2], ACT.Gelu,
                                           bias=b1[:, i:i + 1]).then_inc(hid_gelu[s], 1)

                @block.vector
                def _(dve):
                    def row_stats(s, src, n):
                        for t in range(NT):
                            dve.bn_stats(stat[s][:, t], src[:, t]).then_inc(stats_done[s], 1)
                        for t in range(NT):
                            dve.wait_ge(stats_done[s], 2 * NT * n + t + 1)
                            dve.bn_aggr(mean_var[s][:, t], stat[s][:, t]).then_inc(stats_done[s], 1)

                    def norm_rows(s, src, to, n):
                        dve.wait_ge(rstd_done[s], 2 * n + 2)
                        for t in range(NT):
                            dve.tensor_scalar(to[:, t], src[:, t], mean_var[s][:, t, 0:1], rstd[s][:, t:t + 1],
                                              ALU.subtract, ALU.mult).then_inc(normed[s], 1)

                    for stage, s in order:
                        if stage == "bias":
                            dve.wait_ge(adj_loaded[s], 16)
                            if ffn:
                                dve.tensor_scalar(bias[s][:], adj_sb[s], 0.0, MASKED, ALU.is_le, ALU.mult)\
                                    .then_inc(bias_made[s], 1)
                                dve.scalar_tensor_tensor(
                                    out=sq[s].rearrange("p t n -> p (t n)"),
                                    in0=adj_sb[s].rearrange("p t n -> p (t n)"), scalar=0.1 / HEAD_SCALE,
                                    in1=adj_sb[s].rearrange("p t n -> p (t n)"), op0=ALU.mult, op1=ALU.mult)\
                                    .then_inc(bias_made[s], 1)
                                dve.wait_ge(bias_made[s], 2)
                                dve.tensor_tensor(bias[s][:], bias[s][:], sq[s], ALU.add).then_inc(bias_made[s], 1)
                            else:
                                dve.tensor_scalar(bias[s][:], adj_sb[s], 0.0, MASKED, ALU.is_equal, ALU.mult)\
                                    .then_inc(bias_made[s], 1)
                        elif stage == "stats1":
                            dve.wait_ge(x_loaded[s], 16)
                            row_stats(s, value[s], early)
                        elif stage == "norm1":
                            norm_rows(s, value[s], norm[s], early)
                        elif stage in ("feats1", "feats2"):
                            n = early if stage == "feats1" else 0
                            for c in range(CT):
                                dve.wait_ge(feats_hi[s], CT * n + c + 1)
                                dve.tensor_tensor(feats[s][:, 1, c], normT[s][:, c] if ffn else bank[s][:, c],
                                                  feats[s][:, 0, c].bitcast(F32), ALU.subtract)\
                                    .then_inc(feats_lo[s], 1)
                        elif stage in stage_parts:
                            for n in stage_parts[stage]:
                                dve.wait_ge(qk_hi[s], n + 1)
                                dve.scalar_tensor_tensor(
                                    out=parts[s][:, 2 * (n % 2) + 1], in0=bank[s][:, n if n < 2 else 3],
                                    scalar=(bq, bk)[n % 2][:, n // 2:n // 2 + 1],
                                    in1=parts[s][:, 2 * (n % 2)].bitcast(F32), op0=ALU.add, op1=ALU.subtract)\
                                    .then_inc(qk_lo[s], 1)
                        elif stage == "v":
                            dve.wait_ge(res_made[s], 1)
                            for b in range(2):
                                dve.wait_ge(v_done[s], b + 1)
                                dve.tensor_copy(value[s][:, 2 * b:2 * b + 2],
                                                bank[s][:, 2 + b].rearrange("p (t d) -> p t d", d=D))\
                                    .then_inc(v_ready[s], 1)
                        elif stage.startswith("heads"):
                            j = int(stage[5:])
                            if j < TILES:
                                dve.wait_ge(scores[s], j + 1)
                                if j >= 4:
                                    dve.wait_ge(turned[s], j - 3)
                                dve.tensor_tensor_reduce(
                                    prob[s][:, j % 4], bank[s][:, 2 * j % 3], bias[s][:, j % NT],
                                    -HEAD_SCALE, 3e38, ALU.add, ALU.min, low[s][:, j:j + 1])\
                                    .then_inc(biased[s], 1)
                            i = j - LAG_T
                            if 0 <= i < TILES and i % 2 == 0:
                                dve.wait_ge(turned[s], i + 1)
                                if i >= 2 * NT:
                                    dve.wait_ge(mixed[s], i // NT - 1)
                                dve.tensor_copy(
                                    out_tile(probT[s], i),
                                    bank[s][:, (2 * j + 1) % 3].rearrange("p (k q) -> p k q", q=P))\
                                    .then_inc(copied_dve[s], 1)
                        elif stage == "mix":
                            dve.wait_ge(probs[s], TILES)
                            dve.reciprocal(total[s][:], total[s][:]).then_inc(inverse[s], 1)
                            dve.wait_ge(inverse[s], 1)
                            dve.wait_ge(turned[s], TILES)
                            dve.tensor_copy(
                                wide[s].rearrange("p q (h d) -> p q h d", d=HD),
                                total[s][:].rearrange("p (h q) -> p q h", q=NT).unsqueeze(3)
                                .to_broadcast([P, NT, HEADS, HD])).then_inc(inverse[s], 1)
                        elif stage == "scale":
                            for g in range(GROUPS):
                                dve.wait_ge(spread[s], g + 1)
                                dve.wait_ge(mix_raw[s], g + 1)
                                dve.tensor_tensor(normT[s][:, g], normT[s][:, g], bank[s][:, g], ALU.mult)\
                                    .then_inc(mix_scaled[s], 1)
                                dve.wait_ge(mix_scaled[s], 2 * g + 1)
                                dve.tensor_scalar(normT[s][:, g], normT[s][:, g], bv[:, g:g + 1], None, ALU.add)\
                                    .then_inc(mix_scaled[s], 1)
                        elif stage == "split_mix":
                            for g in range(GROUPS):
                                dve.wait_ge(mix_hi[s], g + 1)
                                dve.tensor_tensor(mixT[s][:, 1, g], normT[s][:, g],
                                                  mixT[s][:, 0, g].bitcast(F32), ALU.subtract)\
                                    .then_inc(mix_lo[s], 1)
                        elif stage == "x1":
                            dve.wait_ge(res_made[s], 1)
                            for b in range(2):
                                dve.wait_ge(projected[s], b + 1)
                                dve.tensor_tensor(xres[s][:, 2 * b:2 * b + 2],
                                                  bank[s][:, 2 + b].rearrange("p (t d) -> p t d", d=D),
                                                  xres[s][:, 2 * b:2 * b + 2], ALU.add).then_inc(x1_made[s], 1)
                        elif stage == "stats2":
                            dve.wait_ge(x1_made[s], 2)
                            row_stats(s, xres[s], 0)
                        elif stage == "norm2":
                            if ffn:
                                norm_rows(s, xres[s], norm[s], 0)
                            else:
                                dve.wait_ge(stats_done[s], 2 * NT)
                                for t in range(NT):
                                    dve.scalar_tensor_tensor(out=xres[s][:, t], in0=xres[s][:, t],
                                                             scalar=mean_var[s][:, t, 0:1], in1=ln_g[:],
                                                             op0=ALU.subtract, op1=ALU.mult).then_inc(normed[s], 1)
                                dve.wait_ge(rstd_done[s], 2)
                                for t in range(NT):
                                    dve.wait_ge(normed[s], t + 1)
                                    dve.scalar_tensor_tensor(out=xres[s][:, t], in0=xres[s][:, t],
                                                             scalar=rstd[s][:, t:t + 1], in1=ln_b[:],
                                                             op0=ALU.mult, op1=ALU.add).then_inc(summed[s], 1)
                        elif stage in split_stages:
                            i = int(stage[5])
                            dve.wait_ge(hid_gelu[s], i + 1)
                            if i == 4:
                                dve.wait_ge(down_done[s], 2)
                            dve.tensor_copy(hidden[s][:, 0, i % 4], prob[s][:, i % 4]).then_inc(hid_hi[s], 1)
                            dve.wait_ge(hid_hi[s], i + 1)
                            dve.tensor_tensor(hidden[s][:, 1, i % 4], prob[s][:, i % 4],
                                              hidden[s][:, 0, i % 4].bitcast(F32), ALU.subtract)\
                                .then_inc(hid_lo[s], 1)
                        elif stage in ("sum0", "sum1"):
                            half = int(stage[3])
                            dve.wait_ge(res_made[s], 2)
                            for b in range(2):
                                dve.wait_ge(down_done[s], 2 * half + b + 1)
                                if half:
                                    dve.wait_ge(summed[s], b + 1)
                                dve.tensor_tensor(xres[s][:, 2 * b:2 * b + 2],
                                                  bank[s][:, 2 + b].rearrange("p (t d) -> p t d", d=D),
                                                  xres[s][:, 2 * b:2 * b + 2], ALU.add).then_inc(summed[s], 1)

        emit(merged(prepare, 1), None, 0)
        ph.clear()
        with nc.Fori(0, graphs // STREAMS) as pair:
            emit(merged(stages, 2 if ffn else 1), pair * STREAMS, (pair * STREAMS + STREAMS) % graphs)
            ph.clear()


def graph_attention_phase(nc, name, x_in, adj, out_t, w, graphs):
    scale = float(D) ** -0.5
    with ExitStack() as ctx:
        ph = Phase(nc, ctx, name)
        raw_names = ("wq_t", "wk_t", "wv_t", "wo")
        split = {k: (ph.buf(k + "h", [P, CT, D], F32R), ph.buf(k + "l", [P, CT, D], F32R)) for k in raw_names}
        folded = {k: (ph.buf(k + "h", [P, CT, D], F32R), ph.buf(k + "l", [P, CT, D], F32R)) for k in ("qk", "vo")}
        ident, power = ph.buf("ident", [P, P]), ph.buf("power", [P, NT])
        bo, ln_g, ln_b = ph.buf("bo", [P, D]), ph.buf("ln_g", [P, CT]), ph.buf("ln_b", [P, CT])
        x_sb, xres = ph.bufs("x_sb", [P, NT, D]), ph.bufs("xres", [P, NT, D])
        adj_sb = ph.bufs("adj", [P, NT, N], I32)
        bias = ph.bufs("bias", [P, NT, N], BF16)
        norm = ph.bufs("norm", [P, NT, D])
        feats = ph.bufs("feats", [P, 2, CT, N], F32R)
        query = ph.bufs("query", [P, 2, CT, N], F32R)
        value = ph.bufs("value", [P, NT, D])
        prob = ph.bufs("prob", [P, NT, N])
        probT = ph.bufs("probT", [P, NT, N])
        hid_t = ph.bufs("hid_t", [P, CT, N])
        low, total = ph.bufs("low", [P, NT]), ph.bufs("total", [P, NT])
        stat, mean_var = ph.bufs("stat", [P, NT, 6]), ph.bufs("mean_var", [P, NT, 2])
        veps, rstd = ph.bufs("veps", [P, NT]), ph.bufs("rstd", [P, NT])
        bank = [ctx.enter_context(nc.psum_tensor(f"{name}_bank{s}", [P, 4, N], F32)) for s in range(STREAMS)]
        load_weights(nc, ph, [(w[k], *split[k]) for k in raw_names],
                     [(w["bo"].partition_broadcast(P), bo[:]), (w["ln_g"], ln_g[:]), (w["ln_b"], ln_b[:])],
                     [prob[s][:].rearrange("p t n -> p (t n)") for s in range(STREAMS)])
        make_constants(nc, ph, power, ident)
        multiplied, folded_hi, folded_lo = ph.sem("multiplied"), ph.sem("folded_hi"), ph.sem("folded_lo")
        with nc.Block(no_gpsimd_drain=True) as block:
            pairs = (("qk", "wq_t", "wk_t"), ("vo", "wv_t", "wo"))

            @block.tensor
            def _(pe):
                for s, (_, left, right) in enumerate(pairs):
                    for i in range(CT):
                        for c in range(CT):
                            mm = product(pe, bank[s][:, i, 0:D],
                                         (split[left][0][:, c, i * P:(i + 1) * P], split[left][1][:, c, i * P:(i + 1) * P]),
                                         (split[right][0][:, c], split[right][1][:, c]), c == 0, c == CT - 1)
                        mm.then_inc(multiplied, 1)

            @block.vector
            def _(dve):
                for s, (k, _, _) in enumerate(pairs):
                    for i in range(CT):
                        dve.wait_ge(multiplied, CT * s + i + 1)
                        dve.tensor_copy(folded[k][0][:, i], bank[s][:, i, 0:D]).then_inc(folded_hi, 1)
                        dve.wait_ge(folded_hi, CT * s + i + 1)
                        dve.tensor_tensor(folded[k][1][:, i], bank[s][:, i, 0:D],
                                          folded[k][0][:, i].bitcast(F32), ALU.subtract).then_inc(folded_lo, 1)
        x_loaded, adj_loaded, bias_made, res_made = (ph.sems(k) for k in ("x_loaded", "adj_loaded", "bias_made", "res_made"))
        turned_x, feats_hi, feats_lo = (ph.sems(k) for k in ("turned_x", "feats_hi", "feats_lo"))
        q_done, q_hi, q_lo, v_done, v_ready = (ph.sems(k) for k in ("q_done", "q_hi", "q_lo", "v_done", "v_ready"))
        scores, biased, probs, turned, copied = (ph.sems(k) for k in ("scores", "biased", "probs", "turned", "copied"))
        inverse, mixed, x1_made = (ph.sems(k) for k in ("inverse", "mixed", "x1_made"))
        stats_done, rstd_done, normed = (ph.sems(k) for k in ("stats_done", "rstd_done", "normed"))
        turned_out, out_made, stored = (ph.sems(k) for k in ("turned_out", "out_made", "stored"))

        lag_t, lag_v = 2, 3
        steps = [f"step{j}" for j in range(NT + lag_v)]
        stages = ["residual", "load", "step0", "step1", "step2", "step3", "step4", "step5", "step6", "stats",
                  "turn", "feats", "norm", "query", "turn_out", "value", "bias", "store"]
        prepare = ["load", "turn", "feats", "query", "value", "bias"]

        def emit(order, graph, following):
            with nc.Block(no_gpsimd_drain=True) as block:
                @block.sync
                def _(sp):
                    for stage, s in order:
                        if stage == "load":
                            sp.dma_start(adj_sb[s][:], rows(adj[following + s])).then_inc(adj_loaded[s], 16)
                            if graph is not None:
                                sp.wait_ge(res_made[s], 1)
                            sp.dma_start(x_sb[s][:], rows(x_in[following + s])).then_inc(x_loaded[s], 16)
                        elif stage == "store":
                            sp.wait_ge(out_made[s], CT)
                            sp.dma_start(out_t[graph + s].rearrange("(c p) n -> p c n", p=P), hid_t[s][:])\
                                .then_inc(stored[s], 16)
                    if graph is not None:
                        for s in range(STREAMS):
                            sp.wait_ge(stored[s], 16)

                @block.gpsimd
                def _(pool):
                    for stage, s in order:
                        if stage == "residual":
                            pool.tensor_tensor(xres[s][:], x_sb[s][:],
                                               bo[:].unsqueeze(1).to_broadcast([P, NT, D]), ALU.add)\
                                .then_inc(res_made[s], 1)
                        elif stage == "stats":
                            pool.wait_ge(stats_done[s], 2 * NT)
                            pool.tensor_scalar(veps[s][:], mean_var[s][:, :, 1], EPS, 1.0, ALU.add, ALU.mult)\
                                .then_inc(rstd_done[s], 1)
                            pool.wait_ge(rstd_done[s], 1)
                            pool.tensor_tensor(rstd[s][:], veps[s][:], power[:], ALU.pow).then_inc(rstd_done[s], 1)

                @block.tensor
                def _(pe):
                    def turn(s, src, first, done):
                        for c in range(CT):
                            for t in range(NT):
                                mm = pe.transpose(bank[s][:, first + c, t * P:(t + 1) * P],
                                                  src[:, t, c * P:(c + 1) * P], ident[:])
                            mm.then_inc(done, 1)

                    for stage, s in order:
                        if stage == "turn":
                            pe.wait_ge(x_loaded[s], 16)
                            if graph is not None:
                                pe.wait_ge(biased[s], NT)
                            turn(s, x_sb[s], 0, turned_x[s])
                        elif stage == "query":
                            pe.wait_ge(feats_hi[s], CT)
                            pe.wait_ge(feats_lo[s], CT)
                            for b in range(CT):
                                for c in range(CT):
                                    mm = product(pe, bank[s][:, b],
                                                 (folded["qk"][0][:, c, b * P:(b + 1) * P],
                                                  folded["qk"][1][:, c, b * P:(b + 1) * P]),
                                                 (feats[s][:, 0, c], feats[s][:, 1, c]), c == 0, c == CT - 1)
                                mm.then_inc(q_done[s], 1)
                        elif stage == "value":
                            pe.wait_ge(q_hi[s], CT)
                            pe.wait_ge(q_lo[s], CT)
                            for t in range(NT):
                                for c in range(CT):
                                    mm = product(pe, bank[s][:, t // 2, t % 2 * D:(t % 2 + 1) * D],
                                                 (feats[s][:, 0, c, t * P:(t + 1) * P],
                                                  feats[s][:, 1, c, t * P:(t + 1) * P]),
                                                 (folded["vo"][0][:, c], folded["vo"][1][:, c]), c == 0, c == CT - 1)
                                if t % 2:
                                    mm.then_inc(v_done[s], 1)
                        elif stage in steps:
                            j = int(stage[4:])
                            if j < NT:
                                if j >= 2:
                                    pe.wait_ge(biased[s], j - 1)
                                for c in range(CT):
                                    mm = product(pe, bank[s][:, j % 2],
                                                 (query[s][:, 0, c, j * P:(j + 1) * P],
                                                  query[s][:, 1, c, j * P:(j + 1) * P]),
                                                 (feats[s][:, 0, c], feats[s][:, 1, c]), c == 0, c == CT - 1)
                                mm.then_inc(scores[s], 1)
                            i = j - lag_t
                            if 0 <= i < NT:
                                pe.wait_ge(probs[s], i + 1)
                                if i:
                                    pe.wait_ge(copied[s], i)
                                for k in range(NT):
                                    mm = pe.transpose(bank[s][:, 2, k * P:(k + 1) * P],
                                                      prob[s][:, i, k * P:(k + 1) * P], ident[:])
                                mm.then_inc(turned[s], 1)
                            i = j - lag_v
                            if 0 <= i < NT:
                                pe.wait_ge(copied[s], i + 1)
                                if i >= 1:
                                    pe.wait_ge(x1_made[s], i)
                                for k in range(NT):
                                    mm = pe.matmul(bank[s][:, 3, 0:D],
                                                   probT[s][:, k, i * P:(i + 1) * P], value[s][:, k],
                                                   start=k == 0, stop=k == NT - 1)
                                mm.then_inc(mixed[s], 1)
                        elif stage == "turn_out":
                            pe.wait_ge(normed[s], NT)
                            pe.wait_ge(copied[s], NT)
                            turn(s, norm[s], 2, turned_out[s])

                @block.scalar
                def _(act):
                    for stage, s in order:
                        if stage == "feats":
                            for c in range(CT):
                                act.wait_ge(turned_x[s], c + 1)
                                act.activation(feats[s][:, 0, c], bank[s][:, c], ACT.Copy).then_inc(feats_hi[s], 1)
                        elif stage == "query":
                            for b in range(CT):
                                act.wait_ge(q_done[s], b + 1)
                                act.activation(query[s][:, 0, b], bank[s][:, b], ACT.Copy).then_inc(q_hi[s], 1)
                        elif stage in steps:
                            j = int(stage[4:])
                            if j < NT:
                                act.wait_ge(biased[s], j + 1)
                                act.activation(prob[s][:, j], prob[s][:, j], ACT.Exp, bias=low[s][:, j:j + 1],
                                               scale=-1.0, accum_out=total[s][:, j:j + 1]).then_inc(probs[s], 1)
                            i = j - lag_t
                            if 0 <= i < NT:
                                act.wait_ge(turned[s], i + 1)
                                act.activation(probT[s][:, :, i * P:(i + 1) * P],
                                               bank[s][:, 2].rearrange("p (k q) -> p k q", q=P), ACT.Copy)\
                                    .then_inc(copied[s], 1)
                        elif stage == "turn_out":
                            for c in range(CT):
                                act.wait_ge(turned_out[s], c + 1)
                                act.activation(hid_t[s][:, c], bank[s][:, 2 + c], ACT.Identity,
                                               scale=ln_g[:, c:c + 1], bias=ln_b[:, c:c + 1]).then_inc(out_made[s], 1)

                @block.vector
                def _(dve):
                    for stage, s in order:
                        if stage == "bias":
                            dve.wait_ge(adj_loaded[s], 16)
                            dve.tensor_scalar(bias[s][:], adj_sb[s][:], 0.0, MASKED, ALU.is_equal, ALU.mult)\
                                .then_inc(bias_made[s], 1)
                        elif stage == "feats":
                            for c in range(CT):
                                dve.wait_ge(feats_hi[s], c + 1)
                                dve.tensor_tensor(feats[s][:, 1, c], bank[s][:, c], feats[s][:, 0, c].bitcast(F32),
                                                  ALU.subtract).then_inc(feats_lo[s], 1)
                        elif stage == "query":
                            for b in range(CT):
                                dve.wait_ge(q_hi[s], b + 1)
                                dve.tensor_tensor(query[s][:, 1, b], bank[s][:, b], query[s][:, 0, b].bitcast(F32),
                                                  ALU.subtract).then_inc(q_lo[s], 1)
                        elif stage == "value":
                            for b in range(2):
                                dve.wait_ge(v_done[s], b + 1)
                                if graph is not None:
                                    dve.wait_ge(mixed[s], NT)
                                dve.tensor_copy(value[s][:, 2 * b:2 * b + 2],
                                                bank[s][:, b].rearrange("p (t d) -> p t d", d=D))\
                                    .then_inc(v_ready[s], 1)
                        elif stage in steps:
                            j = int(stage[4:])
                            if j < NT:
                                dve.wait_ge(scores[s], j + 1)
                                dve.tensor_tensor_reduce(prob[s][:, j], bank[s][:, j % 2], bias[s][:, j],
                                                         -scale, 3e38, ALU.add, ALU.min, low[s][:, j:j + 1])\
                                    .then_inc(biased[s], 1)
                            i = j - lag_v
                            if 0 <= i < NT:
                                if i == 0:
                                    dve.wait_ge(probs[s], NT)
                                    dve.reciprocal(total[s][:], total[s][:]).then_inc(inverse[s], 1)
                                    dve.wait_ge(inverse[s], 1)
                                    dve.wait_ge(res_made[s], 1)
                                dve.wait_ge(mixed[s], i + 1)
                                dve.scalar_tensor_tensor(
                                    out=xres[s][:, i], in0=bank[s][:, 3, 0:D],
                                    scalar=total[s][:, i:i + 1], in1=xres[s][:, i], op0=ALU.mult, op1=ALU.add)\
                                    .then_inc(x1_made[s], 1)
                                dve.wait_ge(x1_made[s], i + 1)
                                dve.bn_stats(stat[s][:, i], xres[s][:, i]).then_inc(stats_done[s], 1)
                        elif stage == "stats":
                            for t in range(NT):
                                dve.wait_ge(stats_done[s], t + 1)
                                dve.bn_aggr(mean_var[s][:, t], stat[s][:, t]).then_inc(stats_done[s], 1)
                        elif stage == "norm":
                            dve.wait_ge(rstd_done[s], 2)
                            for t in range(NT):
                                dve.tensor_scalar(norm[s][:, t], xres[s][:, t], mean_var[s][:, t, 0:1],
                                                  rstd[s][:, t:t + 1], ALU.subtract, ALU.mult)\
                                    .then_inc(normed[s], 1)

        emit(merged(prepare, 1), None, 0)
        ph.clear()
        with nc.Fori(0, graphs // STREAMS) as pair:
            emit(merged(stages, 1), pair * STREAMS, (pair * STREAMS + STREAMS) % graphs)
            ph.clear()


def gated_phase(nc, name, hid_t, adj, out, w, graphs):
    with ExitStack() as ctx:
        ph = Phase(nc, ctx, name)
        gates = ("ri", "zi", "ni", "rh", "zh", "nh")
        split = {"wd": (ph.buf("wdh", [P, CT, LABELS * D], F32R), ph.buf("wdl", [P, CT, LABELS * D], F32R))}
        for k in gates:
            split["w" + k] = (ph.buf(f"w{k}h", [P, CT, D], F32R), ph.buf(f"w{k}l", [P, CT, D], F32R))
        ident, ident_b, power = ph.buf("ident", [P, P]), ph.buf("ident_b", [P, P], BF16), ph.buf("power", [P, NT])
        bd, ln_g, ln_b = ph.buf("bd", [P, D]), ph.buf("ln_g", [P, D]), ph.buf("ln_b", [P, D])
        gate_bias = {k: ph.buf("b" + k, [P, CT]) for k in gates}
        adj_sb = ph.bufs("adj", [P, NT, N], I32)
        adj_b, adj_t = ph.bufs("adj_b", [P, NT, N], BF16), ph.bufs("adj_t", [P, NT, N], BF16)
        hid_in, hid = ph.bufs("hid_in", [P, CT, N]), ph.bufs("hid", [P, CT, N])
        feats = ph.bufs("feats", [P, 2, CT, N], F32R)
        mask = ph.bufs("mask", [P, 2, NT, N], F32R)
        mapped_hi, mapped_lo = ph.bufs("mapped_hi", [P, NT, 2, D + 2], F32R), ph.bufs("mapped_lo", [P, NT, 2, D], F32R)
        acc = ph.bufs("acc", [P, NT, D])
        gate_r, gate_z = ph.bufs("gate_r", [P, CT, N]), ph.bufs("gate_z", [P, CT, N])
        count = ph.bufs("count", [P, LABELS, NT])
        stat, mean_var = ph.bufs("stat", [P, NT, 6]), ph.bufs("mean_var", [P, NT, 2])
        veps, rstd = ph.bufs("veps", [P, NT]), ph.bufs("rstd", [P, NT])
        bank = [ctx.enter_context(nc.psum_tensor(f"{name}_bank{s}", [P, 4, N], F32)) for s in range(STREAMS)]
        agg = [mapped_lo[s][:].rearrange("p (a c) l d -> p a c (l d)", a=2) for s in range(STREAMS)]
        cand = [acc[s][:].rearrange("p t d -> p (t d)").rearrange("p (c n) -> p c n", c=CT) for s in range(STREAMS)]
        new_t = gate_r
        load_weights(
            nc, ph, [(w[k], *split[k]) for k in split],
            [(w["bd"].partition_broadcast(P), bd[:]), (w["ln_g"].partition_broadcast(P), ln_g[:]),
             (w["ln_b"].partition_broadcast(P), ln_b[:])] + [(w["b" + k], gate_bias[k][:]) for k in gates],
            [adj_sb[s][:].bitcast(F32).rearrange("p t n -> p (t n)") for s in range(STREAMS)]
            + [hid[s][:].rearrange("p t n -> p (t n)") for s in range(STREAMS)])
        make_constants(nc, ph, power, ident, ident_b)
        summed_bias = ph.sem("summed_bias")
        with nc.Block(no_gpsimd_drain=True) as block:
            @block.vector
            def _(dve):
                for k in ("r", "z"):
                    dve.tensor_tensor(gate_bias[k + "i"][:], gate_bias[k + "i"][:], gate_bias[k + "h"][:], ALU.add)\
                        .then_inc(summed_bias, 1)
                for s in range(STREAMS):
                    for t in range(NT):
                        for d in range(2):
                            dve.tensor_scalar(mapped_hi[s][:, t, d, D:D + 2], ident[:, 0:2], 0.0, 1.0,
                                              ALU.mult, ALU.add).then_inc(summed_bias, 1)
        adj_loaded, hid_loaded, adj_cast, adj_turned, adj_ready = (
            ph.sems(k) for k in ("adj_loaded", "hid_loaded", "adj_cast", "adj_turned", "adj_ready"))
        feats_hi, feats_lo, map_done, map_hi, map_lo = (
            ph.sems(k) for k in ("feats_hi", "feats_lo", "map_done", "map_hi", "map_lo"))
        masked, averaged, counted, added = (ph.sems(k) for k in ("masked", "averaged", "counted", "added"))
        agg_turned, agg_hi, agg_lo = (ph.sems(k) for k in ("agg_turned", "agg_hi", "agg_lo"))
        gate_done, gate_ready, reset_done, cand_in, cand_ready, kept, blended, held = (
            ph.sems(k) for k in ("gate_done", "gate_ready", "reset_done", "cand_in", "cand_ready", "kept", "blended", "held"))
        new_turned, stats_done, rstd_done, normed, finished, stored = (
            ph.sems(k) for k in ("new_turned", "stats_done", "rstd_done", "normed", "finished", "stored"))

        stages = ["load", "hold", "map0", "label0", "mean0", "label1", "mean1", "mask1", "map1", "label2",
                  "mean2", "cast", "label3", "mean3", "turn", "gates0", "gates1", "blend0", "adj", "blend1",
                  "turn_new", "split", "stats", "norm", "store", "mask0"]
        prepare = ["load", "cast", "adj", "split", "mask0"]

        def emit(order, graph, following):
            with nc.Block(no_gpsimd_drain=True) as block:
                @block.sync
                def _(sp):
                    for stage, s in order:
                        if stage == "load":
                            sp.dma_start(adj_sb[s][:], rows(adj[following + s])).then_inc(adj_loaded[s], 16)
                            if graph is not None:
                                sp.wait_ge(held[s], 1)
                            sp.dma_start(hid_in[s][:], hid_t[following + s].rearrange("(c p) n -> p c n", p=P))\
                                .then_inc(hid_loaded[s], 16)
                        elif stage == "store":
                            sp.wait_ge(finished[s], NT)
                            sp.dma_start(rows(out[graph + s]), acc[s][:]).then_inc(stored[s], 16)
                    if graph is not None:
                        for s in range(STREAMS):
                            sp.wait_ge(stored[s], 16)

                @block.gpsimd
                def _(pool):
                    for stage, s in order:
                        if stage == "hold":
                            pool.tensor_copy(hid[s][:], hid_in[s][:]).then_inc(held[s], 1)
                        elif stage in ("blend0", "blend1"):
                            b = int(stage[5])
                            pool.wait_ge(held[s], 1)
                            pool.wait_ge(cand_in[s], b + 1)
                            pool.wait_ge(gate_ready[s], 2 * b + 2)
                            pool.tensor_tensor(new_t[s][:, b], hid[s][:, b], gate_z[s][:, b], ALU.mult)\
                                .then_inc(kept[s], 1)
                        elif stage == "stats":
                            pool.wait_ge(stats_done[s], 2 * NT)
                            pool.tensor_scalar(veps[s][:], mean_var[s][:, :, 1], EPS, 1.0, ALU.add, ALU.mult)\
                                .then_inc(rstd_done[s], 1)
                            pool.wait_ge(rstd_done[s], 1)
                            pool.tensor_tensor(rstd[s][:], veps[s][:], power[:], ALU.pow).then_inc(rstd_done[s], 1)

                @block.tensor
                def _(pe):
                    for stage, s in order:
                        if stage == "adj":
                            pe.wait_ge(adj_cast[s], 1)
                            if graph is not None:
                                pe.wait_ge(cand_in[s], CT)
                            for t in range(NT):
                                for q in range(NT):
                                    at = t % 2 * N + q * P
                                    mm = pe.transpose(bank[s][:, 2 + t // 2].bitcast(BF16)[:, at:at + P],
                                                      adj_b[s][:, q, t * P:(t + 1) * P], ident_b[:])
                                if t % 2:
                                    mm.then_inc(adj_turned[s], 1)
                        elif stage in ("map0", "map1"):
                            half = int(stage[3])
                            if half:
                                pe.wait_ge(added[s], 2 * NT)
                            for t in range(NT):
                                for c in range(CT):
                                    mm = product(pe, bank[s][:, t],
                                                 (feats[s][:, 0, c, t * P:(t + 1) * P],
                                                  feats[s][:, 1, c, t * P:(t + 1) * P]),
                                                 (split["wd"][0][:, c, half * N:(half + 1) * N],
                                                  split["wd"][1][:, c, half * N:(half + 1) * N]), c == 0, c == CT - 1)
                                mm.then_inc(map_done[s], 1)
                        elif stage.startswith("label"):
                            d = int(stage[5])
                            if d >= 2:
                                pe.wait_ge(masked[s], d - 1)
                            pe.wait_ge(map_hi[s], NT * (d // 2 + 1))
                            pe.wait_ge(map_lo[s], NT * (d // 2 + 1))
                            for m in range(NT):
                                if d % 2:
                                    pe.wait_ge(added[s], NT * d)
                                for k in range(NT):
                                    near = mask[s][:, d % 2, k, m * P:(m + 1) * P]
                                    if k:
                                        pe.matmul(bank[s][:, m, 0:D], near, mapped_lo[s][:, k, d % 2],
                                                  start=False, stop=False)
                                    mm = pe.matmul(bank[s][:, m, 0:D + 2], near, mapped_hi[s][:, k, d % 2],
                                                   start=k == 0, stop=k == NT - 1)
                                    if not k:
                                        pe.matmul(bank[s][:, m, 0:D], near, mapped_lo[s][:, k, d % 2],
                                                  start=False, stop=False)
                                mm.then_inc(averaged[s], 1)
                        elif stage == "turn":
                            pe.wait_ge(added[s], LABELS * NT)
                            for c in range(CT):
                                for t in range(NT):
                                    mm = pe.transpose(bank[s][:, c, t * P:(t + 1) * P],
                                                      acc[s][:, t, c * P:(c + 1) * P], ident[:])
                                mm.then_inc(agg_turned[s], 1)
                        elif stage in ("gates0", "gates1"):
                            b = int(stage[5])
                            pe.wait_ge(agg_hi[s], CT)
                            pe.wait_ge(agg_lo[s], CT)
                            if b:
                                pe.wait_ge(gate_ready[s], 2)
                                pe.wait_ge(cand_in[s], 1)
                            for n, terms in enumerate((("ri", "rh"), ("zi", "zh"), ("nh",), ("ni",))):
                                for a, k in enumerate(terms):
                                    x = agg[s] if k[1] == "i" else feats[s]
                                    for c in range(CT):
                                        wh, wl = split["w" + k]
                                        mm = product(pe, bank[s][:, n],
                                                     (wh[:, c, b * P:(b + 1) * P], wl[:, c, b * P:(b + 1) * P]),
                                                     (x[:, 0, c], x[:, 1, c]), a == 0 and c == 0,
                                                     a == len(terms) - 1 and c == CT - 1)
                                mm.then_inc(gate_done[s], 1)
                        elif stage == "turn_new":
                            pe.wait_ge(blended[s], 2 * CT)
                            pe.wait_ge(gate_ready[s], 2 * CT)
                            for t in range(NT):
                                for c in range(CT):
                                    mm = pe.transpose(bank[s][:, t // 2, (t % 2 * CT + c) * P:(t % 2 * CT + c + 1) * P],
                                                      new_t[s][:, c, t * P:(t + 1) * P], ident[:])
                                mm.then_inc(new_turned[s], 1)

                @block.scalar
                def _(act):
                    for stage, s in order:
                        if stage == "adj":
                            if graph is not None:
                                act.wait_ge(masked[s], 2)
                            for b in range(2):
                                act.wait_ge(adj_turned[s], b + 1)
                                act.activation(adj_t[s][:, 2 * b:2 * b + 2],
                                               bank[s][:, 2 + b].bitcast(BF16).rearrange("p (t n) -> p t n", t=2),
                                               ACT.Copy).then_inc(adj_ready[s], 1)
                        elif stage == "split":
                            act.wait_ge(hid_loaded[s], 16)
                            if graph is not None:
                                act.wait_ge(gate_done[s], 4 * CT)
                            for c in range(CT):
                                act.activation(feats[s][:, 0, c], hid_in[s][:, c], ACT.Copy).then_inc(feats_hi[s], 1)
                        elif stage in ("map0", "map1"):
                            half = int(stage[3])
                            for t in range(NT):
                                act.wait_ge(map_done[s], NT * half + t + 1)
                                act.activation(mapped_hi[s][:, t, :, 0:D], bank[s][:, t].rearrange("p (l d) -> p l d", d=D),
                                               ACT.Copy).then_inc(map_hi[s], 1)
                        elif stage == "turn":
                            for c in range(CT):
                                act.wait_ge(agg_turned[s], c + 1)
                                act.activation(agg[s][:, 0, c], bank[s][:, c], ACT.Relu).then_inc(agg_hi[s], 1)
                        elif stage in ("gates0", "gates1"):
                            b = int(stage[5])
                            for n, (to, k) in enumerate(((gate_r, "ri"), (gate_z, "zi"))):
                                act.wait_ge(gate_done[s], 4 * b + n + 1)
                                act.activation(to[s][:, b], bank[s][:, n], ACT.Sigmoid,
                                               bias=gate_bias[k][:, b:b + 1]).then_inc(gate_ready[s], 1)
                            act.wait_ge(cand_in[s], b + 1)
                            act.activation(cand[s][:, b], cand[s][:, b], ACT.Tanh).then_inc(cand_ready[s], 1)

                @block.vector
                def _(dve):
                    for stage, s in order:
                        if stage == "cast":
                            dve.wait_ge(adj_loaded[s], 16)
                            dve.tensor_copy(adj_b[s][:], adj_sb[s][:]).then_inc(adj_cast[s], 1)
                        elif stage == "split":
                            for c in range(CT):
                                dve.wait_ge(feats_hi[s], c + 1)
                                dve.tensor_tensor(feats[s][:, 1, c], hid_in[s][:, c], feats[s][:, 0, c].bitcast(F32),
                                                  ALU.subtract).then_inc(feats_lo[s], 1)
                        elif stage in ("mask0", "mask1"):
                            half = int(stage[4])
                            if not half:
                                dve.wait_ge(adj_ready[s], 2)
                            for d in (2 * half, 2 * half + 1):
                                if graph is not None:
                                    dve.wait_ge(averaged[s], NT * (d - 1 if half else d + 3))
                                dve.tensor_scalar(mask[s][:, d % 2], adj_t[s][:], float(d + 1), None, ALU.is_equal)\
                                    .then_inc(masked[s], 1)
                        elif stage in ("map0", "map1"):
                            half = int(stage[3])
                            for t in range(NT):
                                dve.wait_ge(map_hi[s], NT * half + t + 1)
                                dve.tensor_tensor(mapped_lo[s][:, t], bank[s][:, t].rearrange("p (l d) -> p l d", d=D),
                                                  mapped_hi[s][:, t, :, 0:D].bitcast(F32), ALU.subtract).then_inc(map_lo[s], 1)
                        elif stage.startswith("mean"):
                            d = int(stage[4])
                            dve.wait_ge(averaged[s], NT * (d + 1))
                            dve.tensor_scalar(count[s][:, d], bank[s][:, :, D], 1e-8, None, ALU.add)\
                                .then_inc(counted[s], 1)
                            dve.wait_ge(counted[s], 2 * d + 1)
                            dve.reciprocal(count[s][:, d], count[s][:, d]).then_inc(counted[s], 1)
                            dve.wait_ge(counted[s], 2 * d + 2)
                            for m in range(NT):
                                if d:
                                    dve.wait_ge(added[s], NT * (d - 1) + m + 1)
                                dve.scalar_tensor_tensor(
                                    out=acc[s][:, m], in0=bank[s][:, m, 0:D], scalar=count[s][:, d, m:m + 1],
                                    in1=acc[s][:, m] if d else bd[:], op0=ALU.mult, op1=ALU.add)\
                                    .then_inc(added[s], 1)
                        elif stage == "turn":
                            for c in range(CT):
                                dve.wait_ge(agg_hi[s], c + 1)
                                dve.scalar_tensor_tensor(
                                    out=agg[s][:, 1, c], in0=bank[s][:, c], scalar=0.0,
                                    in1=agg[s][:, 0, c].bitcast(F32), op0=ALU.max, op1=ALU.subtract)\
                                    .then_inc(agg_lo[s], 1)
                        elif stage in ("gates0", "gates1"):
                            b = int(stage[5])
                            dve.wait_ge(gate_ready[s], 2 * b + 1)
                            dve.wait_ge(gate_done[s], 4 * b + 3)
                            dve.scalar_tensor_tensor(out=gate_r[s][:, b], in0=bank[s][:, 2],
                                                     scalar=gate_bias["nh"][:, b:b + 1], in1=gate_r[s][:, b],
                                                     op0=ALU.add, op1=ALU.mult).then_inc(reset_done[s], 1)
                            dve.wait_ge(reset_done[s], b + 1)
                            dve.wait_ge(gate_done[s], 4 * b + 4)
                            dve.scalar_tensor_tensor(out=cand[s][:, b], in0=bank[s][:, 3],
                                                     scalar=gate_bias["ni"][:, b:b + 1], in1=gate_r[s][:, b],
                                                     op0=ALU.add, op1=ALU.add).then_inc(cand_in[s], 1)
                        elif stage in ("blend0", "blend1"):
                            b = int(stage[5])
                            dve.wait_ge(cand_ready[s], b + 1)
                            dve.wait_ge(kept[s], b + 1)
                            dve.scalar_tensor_tensor(out=gate_z[s][:, b], in0=gate_z[s][:, b], scalar=-1.0,
                                                     in1=cand[s][:, b], op0=ALU.add, op1=ALU.mult)\
                                .then_inc(blended[s], 1)
                            dve.wait_ge(blended[s], 2 * b + 1)
                            dve.tensor_tensor(new_t[s][:, b], new_t[s][:, b], gate_z[s][:, b], ALU.subtract)\
                                .then_inc(blended[s], 1)
                        elif stage in ("stats", "norm"):
                            rows_of = [bank[s][:, t // 2, t % 2 * D:(t % 2 + 1) * D] for t in range(NT)]
                            if stage == "stats":
                                for t in range(NT):
                                    dve.wait_ge(new_turned[s], t // 2 * 2 + 2)
                                    dve.bn_stats(stat[s][:, t], rows_of[t]).then_inc(stats_done[s], 1)
                                for t in range(NT):
                                    dve.wait_ge(stats_done[s], t + 1)
                                    dve.bn_aggr(mean_var[s][:, t], stat[s][:, t]).then_inc(stats_done[s], 1)
                            else:
                                dve.wait_ge(rstd_done[s], 2)
                                for t in range(NT):
                                    dve.scalar_tensor_tensor(out=acc[s][:, t], in0=rows_of[t],
                                                             scalar=mean_var[s][:, t, 0:1], in1=ln_g[:],
                                                             op0=ALU.subtract, op1=ALU.mult).then_inc(normed[s], 1)
                                for t in range(NT):
                                    dve.wait_ge(normed[s], t + 1)
                                    dve.scalar_tensor_tensor(out=acc[s][:, t], in0=acc[s][:, t],
                                                             scalar=rstd[s][:, t:t + 1], in1=ln_b[:],
                                                             op0=ALU.mult, op1=ALU.add).then_inc(finished[s], 1)

        emit(merged(prepare, 1), None, 0)
        ph.clear()
        with nc.Fori(0, graphs // STREAMS) as pair:
            emit(merged(stages, 1), pair * STREAMS, (pair * STREAMS + STREAMS) % graphs)
            ph.clear()


def build(nc, a, out, graphs, only=None, x_in=None):
    x1 = nc.dram_tensor("x1", [graphs, N, D], F32, kind="Internal").ap()
    x2 = nc.dram_tensor("x2", [graphs, N, D], F32, kind="Internal").ap()
    x3_t = nc.dram_tensor("x3_t", [graphs, D, N], F32, kind="Internal").ap()
    adj = a["adj"]
    l0 = {k: a["L0_gnn_" + k] for k in ("wq", "wk", "wv", "wo", "w1", "w2", "bq", "bk", "bv", "bo", "b1", "b2",
                                        "ln1_g", "ln1_b", "ln2_g", "ln2_b")}
    encoder_phase(nc, "l0", a["x"], adj, x1, l0, graphs, True)
    l1 = {k: a["L1_gnn_W" + k[1]] for k in ("wq", "wk", "wv", "wo")} | {k: a["L1_gnn_" + k] for k in ("bq", "bk", "bv", "bo")}
    encoder_phase(nc, "l1", x1, adj, x2, l1 | {"ln_g": a["L1_gnn_gamma"], "ln_b": a["L1_gnn_beta"]}, graphs, False)
    l2 = {"wq_t": a["L2_gnn_Wq"], "wk_t": a["L2_gnn_Wk"], "wv_t": a["L2_gnn_Wv"], "wo": a["L2_gnn_Wo"],
          "bo": a["L2_gnn_bo"], "ln_g": a["L2_gnn_gamma"], "ln_b": a["L2_gnn_beta"]}
    graph_attention_phase(nc, "l2", x2, adj, x3_t, l2, graphs)
    gates = ("ri", "zi", "ni", "rh", "zh", "nh")
    l3 = {"wd": a["L3_gnn_Wd"], "bd": a["L3_gnn_bd"], "ln_g": a["L3_gnn_gamma"], "ln_b": a["L3_gnn_beta"]}
    l3 |= {"w" + k: a["L3_gnn_W" + k] for k in gates} | {"b" + k: a["L3_gnn_b" + k] for k in gates}
    gated_phase(nc, "l3", x3_t, adj, out, l3, graphs)


TRANSPOSED = ("L2_gnn_Wq", "L2_gnn_Wk", "L2_gnn_Wv") + tuple("L3_gnn_W" + k for k in ("ri", "zi", "ni", "rh", "zh", "nh"))

COLUMNS = tuple("L0_gnn_" + k for k in ("bq", "bk", "bv", "b1", "ln1_g", "ln1_b", "ln2_g", "ln2_b")) + (
    "L1_gnn_bq", "L1_gnn_bk", "L1_gnn_bv", "L2_gnn_gamma", "L2_gnn_beta") + tuple(
    "L3_gnn_b" + k for k in ("ri", "zi", "ni", "rh", "zh", "nh"))


def laid_out(name, a):
    if name in COLUMNS:
        return np.ascontiguousarray(a.reshape(-1, P).T)
    if name in TRANSPOSED:
        return np.ascontiguousarray(a.T)
    if name == "L3_gnn_Wd":
        return np.ascontiguousarray(a.reshape(D, LABELS, D).transpose(2, 1, 0).reshape(D, LABELS * D))
    return np.ascontiguousarray(a)


def kernel(**inputs):
    import concourse.bacc as bacc
    from concourse.bass_utils import run_bass_kernel_spmd

    nc = bacc.Bacc("TRN2", target_bir_lowering=False, num_devices=1)
    arrays = {name: laid_out(name, np.asarray(a)) for name, a in inputs.items()}
    args = {name: nc.dram_tensor(name, a.shape, mybir.dt.from_np(a.dtype), kind="ExternalInput").ap()
            for name, a in arrays.items()}
    graphs = arrays["x"].shape[0]
    out = nc.dram_tensor("out", (graphs, N, D), F32, kind="ExternalOutput").ap()
    build(nc, args, out, graphs)
    result = run_bass_kernel_spmd(nc, [arrays], core_ids=[0])
    return result.results[0]["out"]
```

```python
from contextlib import ExitStack

import concourse.bass as bass
import numpy as np
from concourse import mybir

F32 = mybir.dt.float32
F32R = mybir.dt.float32r
BF16 = mybir.dt.bfloat16
I32 = mybir.dt.int32
ALU = mybir.AluOpType
ACT = mybir.ActivationFunctionType

P = 128
N = 512
D = 256
HEADS = 8
HD = D // HEADS
NT = N // P
CT = D // P
GROUPS = CT
GH = HEADS // GROUPS
FF = 4 * D
LABELS = 4
STREAMS = 2
EPS = 1e-5
MASKED = -(2.0 ** 100)
HEAD_SCALE = float(HD) ** -0.5
TILES = HEADS * NT

LAG_T = 3
LAG_V = LAG_T + 5
STEPS = TILES + LAG_V
STACKED = 16 * 4


def copied_by_dve(i):
    return i % 2 == 0


def merged(stages, lag):
    order = []
    for t in range(len(stages) + lag):
        if t < len(stages):
            order.append((stages[t], 0))
        if t >= lag:
            order.append((stages[t - lag], 1))
    return order


def placed(order):
    return [(stage, int(s)) for stage, s in (place.rsplit(".", 1) for place in order.split())]


ORDER_0 = """
    residual.0 stack0.0 qk0.0 v.0 stack1.0 heads0.0 residual.1 stack2.0 qk0.1 stack3.0 stack0.1 heads1.0 v.1
    stack1.1 heads2.0 heads0.1 stack2.1 heads3.0 heads1.1 stack3.1 q1.0 heads2.1 heads4.0 heads3.1 k1.0 q1.1
    heads5.0 k1.1 heads4.1 heads6.0 heads7.0 heads5.1 heads8.0 heads6.1 heads9.0 heads7.1 heads10.0 heads8.1
    heads11.0 heads9.1 heads12.0 heads10.1 heads13.0 heads11.1 heads14.0 heads12.1 heads15.0 heads13.1 heads16.0
    heads14.1 heads17.0 heads15.1 heads18.0 heads16.1 heads19.0 heads17.1 heads20.0 heads18.1 heads21.0
    heads19.1 heads22.0 heads20.1 heads23.0 heads21.1 heads22.1 heads24.0 heads25.0 heads23.1 heads26.0
    heads24.1 heads27.0 heads25.1 heads28.0 heads26.1 heads29.0 heads27.1 heads30.0 heads28.1 heads31.0
    heads29.1 heads32.0 heads30.1 heads33.0 heads31.1 heads34.0 heads32.1 heads35.0 heads33.1 heads36.0
    heads34.1 heads37.0 heads35.1 heads38.0 heads36.1 heads39.0 heads37.1 mix.0 heads38.1 load.0 scale.0
    heads39.1 mix.1 split_mix.0 scale.1 project.0 split_mix.1 load.1 x1.0 stats2.0 project.1 norm2.0 x1.1
    turn2.0 stats2.1 feats2.0 norm2.1 bias.0 turn2.1 feats2.1 split0.0 bias.1 up0.0 up1.0 up0.1 split1.0
    split0.1 up2.0 up1.1 split2.0 split1.1 up3.0 up2.1 split3.0 split2.1 stats1.0 up3.1 up4.0 split3.1 up5.0
    stats1.1 norm1.0 up4.1 down0.0 down0.1 up5.1 split4.0 norm1.1 split5.0 sum0.0 split4.1 up6.0 up6.1 split5.1
    split6.0 sum0.1 up7.0 split7.0 split6.1 sum1.0 up7.1 down1.0 split7.1 turn1.0 sum1.1 feats1.0 down1.1
    store.0 turn1.1 feats1.1 store.1
"""
ORDER_1 = """
    residual.0 heads0.0 residual.1 heads0.1 heads1.0 stack2.1 stack3.0 heads1.1 heads2.0 stack2.0 stack3.1
    heads3.0 heads2.1 q1.0 heads3.1 heads4.0 q1.1 k1.0 heads4.1 heads5.0 k1.1 heads6.0 heads5.1 heads7.0
    heads6.1 heads8.0 heads7.1 heads9.0 heads8.1 heads10.0 heads9.1 heads11.0 heads10.1 heads12.0 heads11.1
    heads13.0 heads12.1 heads14.0 heads13.1 heads15.0 heads14.1 heads16.0 heads15.1 heads17.0 heads16.1
    heads18.0 heads17.1 heads19.0 heads18.1 load.0 heads19.1 heads20.0 load.1 heads21.0 heads20.1 heads22.0
    heads21.1 heads23.0 heads22.1 heads24.0 heads23.1 heads25.0 heads24.1 heads26.0 heads25.1 heads27.0
    heads26.1 heads28.0 heads27.1 heads29.0 heads28.1 heads30.0 heads29.1 heads31.0 heads30.1 heads32.0
    heads31.1 heads33.0 heads32.1 heads34.0 heads33.1 heads35.0 heads34.1 heads36.0 heads35.1 heads37.0 turn1.0
    heads36.1 heads38.0 heads37.1 heads39.0 heads38.1 heads39.1 mix.0 turn1.1 feats1.0 mix.1 scale.0 scale.1
    feats1.1 qk0.0 split_mix.0 stack0.0 split_mix.1 qk0.1 project.0 stack0.1 x1.0 project.1 stats2.0 x1.1
    stack1.0 stats2.1 v.0 stack1.1 norm2.0 v.1 bias.0 norm2.1 store.0 bias.1 store.1
"""
ORDER_2 = """
    residual.1 load.1 residual.0 load.0 step0.0 step1.0 step0.1 step2.0 step1.1 step3.0 step2.1 step4.0 step3.1
    step5.0 step4.1 step6.0 step5.1 stats.0 feats.0 turn.0 step6.1 turn.1 norm.0 feats.1 stats.1 query.0
    turn_out.0 norm.1 query.1 turn_out.1 value.0 bias.0 value.1 store.0 bias.1 store.1
"""
ORDER_3 = """
    load.0 hold.0 load.1 map0.0 hold.1 map0.1 label0.0 mean0.0 label0.1 label1.0 mean0.1 mean1.0 label1.1
    mask1.0 mean1.1 map1.0 mask1.1 map1.1 label2.0 mean2.0 label2.1 cast.0 mean2.1 label3.0 cast.1 mean3.0
    label3.1 turn.0 mean3.1 gates0.0 turn.1 gates1.0 gates0.1 blend0.0 gates1.1 adj.0 blend0.1 blend1.0 adj.1
    turn_new.0 blend1.1 turn_new.1 stats.0 split.1 norm.0 stats.1 store.0 split.0 norm.1 mask0.0 store.1 mask0.1
"""


class Phase:

    def __init__(self, nc, ctx, name):
        self.nc, self.ctx, self.name = nc, ctx, name
        self.all = []

    def buf(self, name, shape, dt=F32):
        return self.ctx.enter_context(self.nc.sbuf_tensor(f"{self.name}_{name}", shape, dt))

    def bufs(self, name, shape, dt=F32):
        return [self.buf(f"{name}{s}", shape, dt) for s in range(STREAMS)]

    def sem(self, name):
        h = self.ctx.enter_context(self.nc.semaphore(f"{self.name}_{name}"))
        self.all.append(h)
        return h

    def sems(self, name):
        return [self.sem(f"{name}{s}") for s in range(STREAMS)]

    def clear(self):
        nums = [h.num for h in self.all]
        self.nc.all_engine_barrier(sems_to_clear=range(min(nums), max(nums) + 1))


def rows(ap):
    return ap.rearrange("(t p) n -> p t n", p=P)


def product(pe, out, left, right, first, last):
    (lh, ll), (rh, rl) = left, right
    pe.matmul(out, lh, rh, start=first, stop=False)
    pe.matmul(out, ll, rh, start=False, stop=False)
    return pe.matmul(out, lh, rl, start=False, stop=last)


def load_weights(nc, ph, weights, vectors, staging, power, ident, *others):
    loaded = [ph.sem(f"weight{n}_loaded") for n in range(len(weights))]
    vectors_loaded, made_hi, made_lo, made = (
        ph.sem(k) for k in ("vectors_loaded", "weights_hi", "weights_lo", "identity_made"))
    places, used = [], [0] * len(staging)
    for src, hi, lo in weights:
        k, m = src.shape
        size = k // P * m
        n = next(i for i, b in enumerate(staging) if used[i] + size <= b.shape[1])
        places.append(staging[n][:, used[n]:used[n] + size].rearrange("p (t m) -> p t m", m=m))
        used[n] += size
    with nc.Block(no_gpsimd_drain=True) as block:
        @block.sync
        def _(sp):
            for n, ((src, _, _), raw) in enumerate(zip(weights, places)):
                sp.dma_start(raw, src.rearrange("(t p) m -> p t m", p=P)).then_inc(loaded[n], 16)
            for src, to in vectors:
                sp.dma_start(to, src).then_inc(vectors_loaded, 16)
            sp.wait_ge(vectors_loaded, 16 * len(vectors))

        @block.scalar
        def _(act):
            for n, ((_, hi, _), raw) in enumerate(zip(weights, places)):
                act.wait_ge(loaded[n], 16)
                act.activation(hi[:], raw, ACT.Copy).then_inc(made_hi, 1)

        @block.vector
        def _(dve):
            for n, ((_, hi, lo), raw) in enumerate(zip(weights, places)):
                dve.wait_ge(made_hi, n + 1)
                dve.tensor_tensor(lo[:], raw, hi[:].bitcast(F32), ALU.subtract).then_inc(made_lo, 1)
            dve.wait_ge(made_lo, len(weights))

        @block.gpsimd
        def _(pool):
            pool.memset(power[:], -0.5)
            pool.memset(ident[:], 0.0).then_inc(made, 1)
            pool.wait_ge(made, 1)
            pool.affine_select(out=ident[:], in_=ident[:], compare_op=ALU.not_equal, fill=1.0, base=0,
                               pattern=[[-1, P]], channel_multiplier=1).then_inc(made, 1)
            pool.wait_ge(made, 2)
            for n, other in enumerate(others):
                pool.tensor_copy(other[:], ident[:]).then_inc(made, 1)
            pool.wait_ge(made, 2 + len(others))


def encoder_phase(nc, name, x_in, adj, no_edge, out, w, graphs, ffn):
    with ExitStack() as ctx:
        ph = Phase(nc, ctx, name)
        split = {}
        for k, m in (("wq", D), ("wk", D), ("wv", D), ("wo", D)) + ((("w1", FF),) if ffn else ()):
            split[k] = (ph.buf(k + "h", [P, CT, m], F32R), ph.buf(k + "l", [P, CT, m], F32R))
        if ffn:
            split["w2"] = (ph.buf("w2h", [P, FF // P, D], F32R), ph.buf("w2l", [P, FF // P, D], F32R))
        ident = ph.buf("ident", [P, P])
        power = ph.buf("power", [P, NT])
        bq, bk, bv = ph.buf("bq", [P, CT]), ph.buf("bk", [P, CT]), ph.buf("bv", [P, CT])
        bo = ph.buf("bo", [P, D])
        if ffn:
            ln1_g, ln1_b = ph.buf("ln1_g", [P, CT]), ph.buf("ln1_b", [P, CT])
            ln2_g, ln2_b = ph.buf("ln2_g", [P, CT]), ph.buf("ln2_b", [P, CT])
            b1, b2 = ph.buf("b1", [P, FF // P]), ph.buf("b2", [P, D])
        else:
            ln_g, ln_b = ph.buf("ln_g", [P, D]), ph.buf("ln_b", [P, D])
        xres = ph.bufs("xres", [P, NT, D])
        bias = ph.bufs("bias", [P, NT, N], F32 if ffn else BF16)
        norm = ph.bufs("norm", [P, NT, D])
        feats = ph.bufs("feats", [P, 2, CT, N], F32R)
        parts = ph.bufs("parts", [P, 4, N], F32R)
        stack = ph.bufs("stack", [P, 2, GH, N], F32R)
        value = ph.bufs("value", [P, NT, D])
        x_sb = value if ffn else ph.bufs("x_sb", [P, NT, D])
        prob = ph.bufs("prob", [P, 4, N])
        probT = ph.bufs("probT", [P, 2, NT, N])
        low = ph.bufs("low", [P, TILES])
        total = ph.bufs("total", [P, TILES])
        stat, mean_var = ph.bufs("stat", [P, NT, 6]), ph.bufs("mean_var", [P, NT, 2])
        veps, rstd = ph.bufs("veps", [P, NT]), ph.bufs("rstd", [P, NT])
        bank = [ctx.enter_context(nc.psum_tensor(f"{name}_bank{s}", [P, 4, N], F32)) for s in range(STREAMS)]
        adj_sb = [probT[s][:, 0].bitcast(I32) for s in range(STREAMS)]
        sq = [probT[s][:, 1] for s in range(STREAMS)]
        normT = [norm[s][:].rearrange("p t d -> p (t d)").rearrange("p (c n) -> p c n", c=CT) for s in range(STREAMS)]
        no_edge_sb = [norm[s][:].bitcast(BF16).rearrange("p t (a n) -> p (t a) n", n=N) for s in range(STREAMS)]
        mixT = ([parts[s][:].rearrange("p (a c) n -> p a c n", a=2) for s in range(STREAMS)] if ffn
                else ph.bufs("mixT", [P, 2, CT, N], F32R))
        spread_bank = 0 if ffn else 2
        wide = [prob[s][:, 0:2].rearrange("p a n -> p (a n)").rearrange("p (q d) -> p q d", d=D)
                for s in range(STREAMS)]
        hidden = stack

        load_weights(
            nc, ph, [(w[k], *split[k]) for k in split],
            [(w["bq"], bq[:]), (w["bk"], bk[:]), (w["bv"], bv[:]),
             (w["bo"].partition_broadcast(P), bo[:])]
            + ([(w["ln1_g"], ln1_g[:]), (w["ln1_b"], ln1_b[:]), (w["ln2_g"], ln2_g[:]),
                (w["ln2_b"], ln2_b[:]), (w["b1"], b1[:]), (w["b2"].partition_broadcast(P), b2[:])]
               if ffn else [(w["ln_g"].partition_broadcast(P), ln_g[:]), (w["ln_b"].partition_broadcast(P), ln_b[:])]),
            [probT[s][:].rearrange("p a t n -> p (a t n)") for s in range(STREAMS)], power, ident)
        x_loaded, adj_loaded = ph.sems("x_loaded"), ph.sems("adj_loaded")
        bias_made = ph.sems("bias_made")
        res_made = ph.sems("res_made")
        stats_done, rstd_done, normed = ph.sems("stats_done"), ph.sems("rstd_done"), ph.sems("normed")
        turned_x, feats_hi, feats_lo = ph.sems("turned_x"), ph.sems("feats_hi"), ph.sems("feats_lo")
        qk_done, qk_hi, qk_lo = ph.sems("qk_done"), ph.sems("qk_hi"), ph.sems("qk_lo")
        stacked = [ph.sems(f"stacked{h}_") for h in range(GH)]
        v_done, v_ready = ph.sems("v_done"), ph.sems("v_ready")
        scores, biased, probs, turned = ph.sems("scores"), ph.sems("biased"), ph.sems("probs"), ph.sems("turned")
        copied_dve, copied_act = ph.sems("copied_dve"), ph.sems("copied_act")
        mixed, mix_raw, inverse, spread = ph.sems("mixed"), ph.sems("mix_raw"), ph.sems("inverse"), ph.sems("spread")
        mix_scaled, mix_hi, mix_lo = ph.sems("mix_scaled"), ph.sems("mix_hi"), ph.sems("mix_lo")
        projected, x1_made = ph.sems("projected"), ph.sems("x1_made")
        hid_done, hid_gelu, hid_hi, hid_lo = ph.sems("hid_done"), ph.sems("hid_gelu"), ph.sems("hid_hi"), ph.sems("hid_lo")
        down_done, summed, stored = ph.sems("down_done"), ph.sems("summed"), ph.sems("stored")
        feats_full, adj_squared = ph.sems("feats_full"), ph.sems("adj_squared")
        no_edge_made, no_edge_stored = ph.sems("no_edge_made"), ph.sems("no_edge_stored")

        if ffn:
            order, prepare = placed(ORDER_0), ["load", "bias", "stats1", "norm1", "turn1", "feats1"]
        else:
            order = placed(ORDER_1)
            prepare = ["load", "bias", "turn1", "feats1", "qk0", "stack0", "stack1", "v"]
        ahead = () if ffn else (0, 1)
        split_stages = [f"split{i}" for i in range(FF // P)]
        stage_parts = {"qk0": (0, 1), "q1": (2,), "k1": (3,)}
        second_group = [f"heads{max((h + 1) * NT - 1, 5)}" for h in range(GH)]

        def wait_copied(eng, s, i):
            by_dve = sum(map(copied_by_dve, range(i + 1)))
            eng.wait_ge(copied_dve[s], by_dve)
            if i + 1 > by_dve:
                eng.wait_ge(copied_act[s], i + 1 - by_dve)

        def out_tile(ap, i):
            h, q = divmod(i, NT)
            return ap[:, h % 2, :, q * P:(q + 1) * P]

        def emit(order, graph, following):
            early = 0 if graph is None or not ffn else 1

            def nth(n):
                if ffn:
                    return n
                return n - 2 if n >= 2 else n if graph is None else n + 2

            with nc.Block(no_gpsimd_drain=True) as block:
                @block.sync
                def _(sp):
                    def stack_head(s, h):
                        src = parts[s][HD * h:HD * (h + 1)].bitcast(F32)
                        for n, part in enumerate((src[:, 0::2], src[:, 0::3], src[:, 1:3], src[:, 1::2])):
                            sp.dma_start(stack[s][HD * n:HD * (n + 1), :, h].bitcast(F32), part)\
                                .then_inc(stacked[h][s], 16)

                    for stage, s in order:
                        if stage == "load":
                            if graph is not None:
                                if ffn:
                                    sp.wait_ge(mixed[s], HEADS)
                                else:
                                    sp.wait_ge(res_made[s], 1)
                            sp.dma_start(x_sb[s][:], rows(x_in[following + s])).then_inc(x_loaded[s], 16)
                            if ffn:
                                sp.dma_start(adj_sb[s], rows(adj[following + s])).then_inc(adj_loaded[s], 16)
                        elif stage == "bias" and not ffn:
                            if graph is not None:
                                sp.wait_ge(biased[s], TILES)
                            sp.dma_start(bias[s][:], rows(no_edge[following + s])).then_inc(adj_loaded[s], 16)
                        elif stage == "heads8" and ffn:
                            sp.wait_ge(no_edge_made[s], 1)
                            sp.dma_start(rows(no_edge[graph + s]), no_edge_sb[s]).then_inc(no_edge_stored[s], 16)
                        elif stage.startswith("stack"):
                            h = int(stage[5:])
                            if ffn or h in ahead:
                                sp.wait_ge(qk_hi[s], nth(1) + 1)
                                sp.wait_ge(qk_lo[s], nth(1) + 1)
                            if h in ahead and graph is not None:
                                sp.wait_ge(scores[s], TILES)
                            stack_head(s, h)
                        elif stage in second_group:
                            h = second_group.index(stage)
                            sp.wait_ge(qk_hi[s], nth(3) + 1)
                            sp.wait_ge(qk_lo[s], nth(3) + 1)
                            sp.wait_ge(scores[s], NT * (h + 1))
                            stack_head(s, h)
                        elif stage == "store":
                            sp.wait_ge(summed[s], 4 if ffn else NT)
                            sp.dma_start(rows(out[graph + s]), xres[s][:]).then_inc(stored[s], 16)
                    for s in range(STREAMS):
                        sp.wait_ge(adj_loaded[s], 16)
                        for h in ahead:
                            sp.wait_ge(stacked[h][s], STACKED * (1 if graph is None else 2))
                        if graph is not None:
                            sp.wait_ge(stored[s], 16)

                @block.gpsimd
                def _(pool):
                    def reciprocal_root(s, n):
                        pool.wait_ge(stats_done[s], 2 * NT * (n + 1))
                        pool.tensor_scalar(veps[s][:], mean_var[s][:, :, 1], EPS, 1.0, ALU.add, ALU.mult)\
                            .then_inc(rstd_done[s], 1)
                        pool.wait_ge(rstd_done[s], 2 * n + 1)
                        pool.tensor_tensor(rstd[s][:], veps[s][:], power[:], ALU.pow).then_inc(rstd_done[s], 1)

                    for stage, s in order:
                        if stage == "stats1":
                            reciprocal_root(s, early)
                        elif stage == "stats2":
                            reciprocal_root(s, 0)
                        elif stage == "residual":
                            pool.tensor_tensor(xres[s][:], x_sb[s][:],
                                               bo[:].unsqueeze(1).to_broadcast([P, NT, D]), ALU.add)\
                                .then_inc(res_made[s], 1)
                            if ffn:
                                pool.tensor_scalar(no_edge_sb[s], adj_sb[s], 0.0, MASKED, ALU.is_equal, ALU.mult)\
                                    .then_inc(no_edge_made[s], 1)
                        elif stage == "norm2" and ffn:
                            pool.wait_ge(normed[s], NT)
                            pool.tensor_tensor(xres[s][:], xres[s][:],
                                               b2[:].unsqueeze(1).to_broadcast([P, NT, D]), ALU.add)\
                                .then_inc(res_made[s], 1)

                @block.tensor
                def _(pe):
                    def turn(s, src, ready):
                        for sem, count in ready:
                            pe.wait_ge(sem, count)
                        for c in range(CT):
                            for t in range(NT):
                                mm = pe.transpose(bank[s][:, c, t * P:(t + 1) * P],
                                                  src[:, t, c * P:(c + 1) * P], ident[:])
                            mm.then_inc(turned_x[s], 1)

                    def feature(s, c, lo, hi):
                        return feats[s][:, 0, c, lo:hi], feats[s][:, 1, c, lo:hi]

                    def weight(k, c, lo, hi):
                        return split[k][0][:, c, lo:hi], split[k][1][:, c, lo:hi]

                    def step(s, j):
                        if j < TILES:
                            h, q = divmod(j, NT)
                            if q == 0:
                                made = h // GH + (h % GH not in ahead)
                                if made:
                                    pe.wait_ge(stacked[h % GH][s], STACKED * made)
                            if j == 0 and ffn:
                                pe.wait_ge(v_ready[s], 2)
                                pe.wait_ge(qk_hi[s], 2)
                                pe.wait_ge(qk_lo[s], 2)
                            if j - 2 - LAG_T >= 0:
                                wait_copied(pe, s, j - 2 - LAG_T)
                            elif j >= 3:
                                pe.wait_ge(biased[s], j - 2)
                            pe.matmul(bank[s][:, 2 * j % 3], stack[s][:, 0, h % GH, q * P:(q + 1) * P],
                                      stack[s][:, 1, h % GH], start=True, stop=True).then_inc(scores[s], 1)
                        i = j - LAG_T
                        if 0 <= i < TILES:
                            pe.wait_ge(probs[s], i + 1)
                            if j - 1 < TILES:
                                pe.wait_ge(biased[s], j)
                            else:
                                wait_copied(pe, s, i - 3)
                            for k in range(NT):
                                mm = pe.transpose(bank[s][:, (2 * j + 1) % 3, k * P:(k + 1) * P],
                                                  prob[s][:, i % 4, k * P:(k + 1) * P], ident[:])
                            mm.then_inc(turned[s], 1)
                        i = j - LAG_V
                        if 0 <= i < TILES:
                            h, k = divmod(i, NT)
                            if k == 0:
                                wait_copied(pe, s, NT * h + NT - 1)
                                if h == 0:
                                    pe.wait_ge(qk_hi[s], nth(3) + 1)
                                    pe.wait_ge(qk_lo[s], nth(3) + 1)
                                if h == GH:
                                    pe.wait_ge(mix_raw[s], 1)
                            mm = pe.matmul(bank[s][HD * (h % GH):HD * (h % GH + 1), 3],
                                           value[s][:, k, HD * h:HD * (h + 1)], probT[s][:, h % 2, k],
                                           start=k == 0, stop=k == NT - 1)
                            if k == NT - 1:
                                mm.then_inc(mixed[s], 1)

                    for stage, s in order:
                        if stage == "turn1":
                            ready = [(normed[s], NT * (early + 1))] if ffn else [(x_loaded[s], 16)]
                            if graph is not None:
                                if ffn:
                                    pe.wait_ge(hid_gelu[s], FF // P)
                                else:
                                    wait_copied(pe, s, TILES - 1)
                            turn(s, norm[s] if ffn else x_sb[s], ready)
                        elif stage in stage_parts:
                            for n in stage_parts[stage]:
                                if n == 0 and not ffn:
                                    pe.wait_ge(feats_hi[s], CT)
                                    pe.wait_ge(feats_lo[s], CT)
                                if n == 2 and ffn:
                                    pe.wait_ge(v_ready[s], 2)
                                if n == 3:
                                    pe.wait_ge(qk_hi[s], nth(2) + 1)
                                    pe.wait_ge(qk_lo[s], nth(2) + 1)
                                for c in range(CT):
                                    mm = product(pe, bank[s][:, n if n < 2 else 3],
                                                 weight(("wq", "wk")[n % 2], c, n // 2 * P, (n // 2 + 1) * P),
                                                 feature(s, c, 0, N), c == 0, c == CT - 1)
                                mm.then_inc(qk_done[s], 1)
                        elif stage == "v":
                            if not ffn:
                                pe.wait_ge(feats_hi[s], CT)
                                pe.wait_ge(feats_lo[s], CT)
                                if graph is not None:
                                    pe.wait_ge(x1_made[s], 2)
                            for t in range(NT):
                                for c in range(CT):
                                    mm = product(pe, bank[s][:, 2 + t // 2, t % 2 * D:(t % 2 + 1) * D],
                                                 feature(s, c, t * P, (t + 1) * P), weight("wv", c, 0, D),
                                                 c == 0, c == CT - 1)
                                if t % 2:
                                    mm.then_inc(v_done[s], 1)
                        elif stage.startswith("heads"):
                            step(s, int(stage[5:]))
                        elif stage == "mix":
                            pe.wait_ge(inverse[s], 2)
                            wait_copied(pe, s, TILES - 1)
                            pe.wait_ge(mix_raw[s], GROUPS)
                            for g in range(GROUPS):
                                for q in range(NT):
                                    mm = pe.transpose(bank[s][:, spread_bank + g, q * P:(q + 1) * P],
                                                      wide[s][:, q, g * P:(g + 1) * P], ident[:])
                                mm.then_inc(spread[s], 1)
                        elif stage == "project":
                            pe.wait_ge(mix_raw[s], GROUPS)
                            pe.wait_ge(mix_hi[s], GROUPS)
                            pe.wait_ge(mix_lo[s], GROUPS)
                            for t in range(NT):
                                for c in range(CT):
                                    mm = product(pe, bank[s][:, 2 + t // 2, t % 2 * D:(t % 2 + 1) * D],
                                                 (mixT[s][:, 0, c, t * P:(t + 1) * P],
                                                  mixT[s][:, 1, c, t * P:(t + 1) * P]),
                                                 weight("wo", c, 0, D), c == 0, c == CT - 1)
                                if t % 2:
                                    mm.then_inc(projected[s], 1)
                        elif stage == "turn2":
                            turn(s, norm[s], [(normed[s], NT)])
                        elif stage.startswith("up"):
                            i = int(stage[2])
                            if i == 0:
                                pe.wait_ge(feats_hi[s], CT)
                                pe.wait_ge(feats_lo[s], CT)
                            if i >= 2:
                                pe.wait_ge(hid_gelu[s], i - 1)
                            for c in range(CT):
                                mm = product(pe, bank[s][:, i % 2], weight("w1", c, i * P, (i + 1) * P),
                                             feature(s, c, 0, N), c == 0, c == CT - 1)
                            mm.then_inc(hid_done[s], 1)
                        elif stage in ("down0", "down1"):
                            half = int(stage[4])
                            pe.wait_ge(hid_lo[s], 4 * half + 4)
                            if half:
                                pe.wait_ge(summed[s], 2)
                            for t in range(NT):
                                for k in range(4):
                                    mm = product(pe, bank[s][:, 2 + t // 2, t % 2 * D:(t % 2 + 1) * D],
                                                 (hidden[s][:, 0, k, t * P:(t + 1) * P],
                                                  hidden[s][:, 1, k, t * P:(t + 1) * P]),
                                                 weight("w2", 4 * half + k, 0, D), k == 0, k == 3)
                                if t % 2:
                                    mm.then_inc(down_done[s], 1)

                @block.scalar
                def _(act):
                    for stage, s in order:
                        if stage in ("feats1", "feats2"):
                            n = early if stage == "feats1" else 0
                            for c in range(CT):
                                act.wait_ge(turned_x[s], CT * n + (CT if ffn else c + 1))
                                if ffn:
                                    gain, off = (ln1_g, ln1_b) if stage == "feats1" else (ln2_g, ln2_b)
                                    act.activation(normT[s][:, c], bank[s][:, c], ACT.Identity,
                                                   scale=gain[:, c:c + 1], bias=off[:, c:c + 1])\
                                        .then_inc(feats_full[s], 1)
                                    act.wait_ge(feats_full[s], CT * n + c + 1)
                                    act.activation(feats[s][:, 0, c], normT[s][:, c], ACT.Copy)\
                                        .then_inc(feats_hi[s], 1)
                                else:
                                    act.activation(feats[s][:, 0, c], bank[s][:, c], ACT.Copy)\
                                        .then_inc(feats_hi[s], 1)
                        elif stage in stage_parts:
                            for n in stage_parts[stage]:
                                act.wait_ge(qk_done[s], nth(n) + 1)
                                if n == 2:
                                    for h in range(GH):
                                        if h not in ahead:
                                            act.wait_ge(stacked[h][s], STACKED)
                                if n == 0 and not ffn and graph is not None:
                                    for h in range(GH):
                                        act.wait_ge(stacked[h][s], STACKED * (GROUPS - (h in ahead)))
                                act.activation(parts[s][:, 2 * (n % 2)], bank[s][:, n if n < 2 else 3], ACT.Identity,
                                               bias=(bq, bk)[n % 2][:, n // 2:n // 2 + 1]).then_inc(qk_hi[s], 1)
                        elif stage.startswith("heads"):
                            j = int(stage[5:])
                            i = j - LAG_T
                            if 0 <= i < TILES and not copied_by_dve(i):
                                if ffn and i == 1:
                                    act.wait_ge(no_edge_made[s], 1)
                                act.wait_ge(turned[s], i + 1)
                                if i >= 2 * NT:
                                    act.wait_ge(mixed[s], i // NT - 1)
                                act.activation(
                                    out_tile(probT[s], i),
                                    bank[s][:, (2 * j + 1) % 3].rearrange("p (k q) -> p k q", q=P),
                                    ACT.Copy).then_inc(copied_act[s], 1)
                            if j < TILES:
                                act.wait_ge(biased[s], j + 1)
                                act.activation(prob[s][:, j % 4], prob[s][:, j % 4], ACT.Exp,
                                               bias=low[s][:, j:j + 1], scale=-1.0,
                                               accum_out=total[s][:, j:j + 1]).then_inc(probs[s], 1)
                            i = j - LAG_V
                            if 0 <= i < TILES and i % (GH * NT) == GH * NT - 1:
                                g = i // (GH * NT)
                                act.wait_ge(mixed[s], GH * (g + 1))
                                if ffn:
                                    act.wait_ge(no_edge_stored[s], 16)
                                act.activation(normT[s][:, g], bank[s][:, 3], ACT.Copy)\
                                    .then_inc(mix_raw[s], 1)
                        elif stage == "v" and not ffn:
                            if graph is not None:
                                act.wait_ge(mixed[s], HEADS)
                            for b in range(2):
                                act.wait_ge(v_done[s], b + 1)
                                act.activation(value[s][:, 2 * b:2 * b + 2],
                                               bank[s][:, 2 + b].rearrange("p (t d) -> p t d", d=D), ACT.Copy)\
                                    .then_inc(v_ready[s], 1)
                        elif stage == "mix":
                            act.wait_ge(inverse[s], 1)
                            act.wait_ge(turned[s], TILES)
                            act.activation(
                                wide[s].rearrange("p q (h d) -> p q h d", d=HD),
                                total[s][:].rearrange("p (h q) -> p q h", q=NT).unsqueeze(3)
                                .to_broadcast([P, NT, HEADS, HD]), ACT.Copy).then_inc(inverse[s], 1)
                        elif stage == "scale":
                            for h in range(GH):
                                act.wait_ge(stacked[h][s], STACKED * (GROUPS - (h in ahead)))
                            for g in range(GROUPS):
                                act.wait_ge(mix_scaled[s], g + 1)
                                act.activation(mixT[s][:, 0, g], normT[s][:, g], ACT.Identity, bias=bv[:, g:g + 1])\
                                    .then_inc(mix_hi[s], 1)
                        elif stage.startswith("up"):
                            i = int(stage[2])
                            act.wait_ge(hid_done[s], i + 1)
                            if i >= 4:
                                act.wait_ge(hid_lo[s], i - 3)
                            act.activation(prob[s][:, i % 4], bank[s][:, i % 2], ACT.Gelu,
                                           bias=b1[:, i:i + 1]).then_inc(hid_gelu[s], 1)
                        elif stage == "bias" and ffn:
                            act.wait_ge(adj_loaded[s], 16)
                            act.activation(sq[s], adj_sb[s], ACT.Square).then_inc(adj_squared[s], 1)

                @block.vector
                def _(dve):
                    def row_stats(s, src, n):
                        for t in range(NT):
                            dve.bn_stats(stat[s][:, t], src[:, t]).then_inc(stats_done[s], 1)
                        for t in range(NT):
                            dve.wait_ge(stats_done[s], 2 * NT * n + t + 1)
                            dve.bn_aggr(mean_var[s][:, t], stat[s][:, t]).then_inc(stats_done[s], 1)

                    def norm_rows(s, src, to, n):
                        dve.wait_ge(rstd_done[s], 2 * n + 2)
                        for t in range(NT):
                            dve.tensor_scalar(to[:, t], src[:, t], mean_var[s][:, t, 0:1], rstd[s][:, t:t + 1],
                                              ALU.subtract, ALU.mult).then_inc(normed[s], 1)

                    for stage, s in order:
                        if stage == "bias" and ffn:
                            dve.wait_ge(adj_loaded[s], 16)
                            dve.tensor_scalar(bias[s][:], adj_sb[s], 0.0, MASKED, ALU.is_le, ALU.mult)\
                                .then_inc(bias_made[s], 1)
                            dve.wait_ge(bias_made[s], 1)
                            dve.wait_ge(adj_squared[s], 1)
                            dve.scalar_tensor_tensor(
                                out=bias[s][:].rearrange("p t n -> p (t n)"), in0=sq[s].rearrange("p t n -> p (t n)"),
                                scalar=0.1 / HEAD_SCALE, in1=bias[s][:].rearrange("p t n -> p (t n)"),
                                op0=ALU.mult, op1=ALU.add).then_inc(bias_made[s], 1)
                        elif stage == "stats1":
                            dve.wait_ge(x_loaded[s], 16)
                            row_stats(s, x_sb[s], early)
                        elif stage == "norm1":
                            norm_rows(s, value[s], norm[s], early)
                        elif stage in ("feats1", "feats2"):
                            n = early if stage == "feats1" else 0
                            for c in range(CT):
                                dve.wait_ge(feats_hi[s], CT * n + c + 1)
                                dve.tensor_tensor(feats[s][:, 1, c], normT[s][:, c] if ffn else bank[s][:, c],
                                                  feats[s][:, 0, c].bitcast(F32), ALU.subtract)\
                                    .then_inc(feats_lo[s], 1)
                        elif stage in stage_parts:
                            for n in stage_parts[stage]:
                                dve.wait_ge(qk_hi[s], nth(n) + 1)
                                dve.scalar_tensor_tensor(
                                    out=parts[s][:, 2 * (n % 2) + 1], in0=bank[s][:, n if n < 2 else 3],
                                    scalar=(bq, bk)[n % 2][:, n // 2:n // 2 + 1],
                                    in1=parts[s][:, 2 * (n % 2)].bitcast(F32), op0=ALU.add, op1=ALU.subtract)\
                                    .then_inc(qk_lo[s], 1)
                        elif stage == "v" and ffn:
                            dve.wait_ge(res_made[s], 1)
                            for b in range(2):
                                dve.wait_ge(v_done[s], b + 1)
                                dve.tensor_copy(value[s][:, 2 * b:2 * b + 2],
                                                bank[s][:, 2 + b].rearrange("p (t d) -> p t d", d=D))\
                                    .then_inc(v_ready[s], 1)
                        elif stage.startswith("heads"):
                            j = int(stage[5:])
                            if j < TILES:
                                dve.wait_ge(scores[s], j + 1)
                                if j >= 4:
                                    dve.wait_ge(turned[s], j - 3)
                                dve.tensor_tensor_reduce(
                                    prob[s][:, j % 4], bank[s][:, 2 * j % 3], bias[s][:, j % NT],
                                    -HEAD_SCALE, 3e38, ALU.add, ALU.min, low[s][:, j:j + 1])\
                                    .then_inc(biased[s], 1)
                            i = j - LAG_T
                            if 0 <= i < TILES and copied_by_dve(i):
                                if ffn and i == 0:
                                    dve.wait_ge(no_edge_made[s], 1)
                                dve.wait_ge(turned[s], i + 1)
                                if i >= 2 * NT:
                                    dve.wait_ge(mixed[s], i // NT - 1)
                                dve.tensor_copy(
                                    out_tile(probT[s], i),
                                    bank[s][:, (2 * j + 1) % 3].rearrange("p (k q) -> p k q", q=P))\
                                    .then_inc(copied_dve[s], 1)
                        elif stage == "mix":
                            dve.wait_ge(probs[s], TILES)
                            dve.reciprocal(total[s][:], total[s][:]).then_inc(inverse[s], 1)
                        elif stage == "scale":
                            for g in range(GROUPS):
                                dve.wait_ge(spread[s], g + 1)
                                dve.wait_ge(mix_raw[s], g + 1)
                                dve.tensor_tensor(normT[s][:, g], normT[s][:, g], bank[s][:, spread_bank + g],
                                                  ALU.mult)\
                                    .then_inc(mix_scaled[s], 1)
                        elif stage == "split_mix":
                            for g in range(GROUPS):
                                dve.wait_ge(mix_hi[s], g + 1)
                                dve.scalar_tensor_tensor(out=mixT[s][:, 1, g], in0=normT[s][:, g],
                                                         scalar=bv[:, g:g + 1], in1=mixT[s][:, 0, g].bitcast(F32),
                                                         op0=ALU.add, op1=ALU.subtract)\
                                    .then_inc(mix_lo[s], 1)
                        elif stage == "x1":
                            dve.wait_ge(res_made[s], 1)
                            for b in range(2):
                                dve.wait_ge(projected[s], b + 1)
                                dve.tensor_tensor(xres[s][:, 2 * b:2 * b + 2],
                                                  bank[s][:, 2 + b].rearrange("p (t d) -> p t d", d=D),
                                                  xres[s][:, 2 * b:2 * b + 2], ALU.add).then_inc(x1_made[s], 1)
                        elif stage == "stats2":
                            dve.wait_ge(x1_made[s], 2)
                            row_stats(s, xres[s], 0)
                        elif stage == "norm2":
                            if ffn:
                                norm_rows(s, xres[s], norm[s], 0)
                            else:
                                dve.wait_ge(stats_done[s], 2 * NT)
                                for t in range(NT):
                                    dve.scalar_tensor_tensor(out=xres[s][:, t], in0=xres[s][:, t],
                                                             scalar=mean_var[s][:, t, 0:1], in1=ln_g[:],
                                                             op0=ALU.subtract, op1=ALU.mult).then_inc(normed[s], 1)
                                dve.wait_ge(rstd_done[s], 2)
                                for t in range(NT):
                                    dve.wait_ge(normed[s], t + 1)
                                    dve.scalar_tensor_tensor(out=xres[s][:, t], in0=xres[s][:, t],
                                                             scalar=rstd[s][:, t:t + 1], in1=ln_b[:],
                                                             op0=ALU.mult, op1=ALU.add).then_inc(summed[s], 1)
                        elif stage in split_stages:
                            i = int(stage[5])
                            dve.wait_ge(hid_gelu[s], i + 1)
                            if i == 4:
                                dve.wait_ge(down_done[s], 2)
                            dve.tensor_copy(hidden[s][:, 0, i % 4], prob[s][:, i % 4]).then_inc(hid_hi[s], 1)
                            dve.wait_ge(hid_hi[s], i + 1)
                            dve.tensor_tensor(hidden[s][:, 1, i % 4], prob[s][:, i % 4],
                                              hidden[s][:, 0, i % 4].bitcast(F32), ALU.subtract)\
                                .then_inc(hid_lo[s], 1)
                        elif stage in ("sum0", "sum1"):
                            half = int(stage[3])
                            dve.wait_ge(res_made[s], 2)
                            for b in range(2):
                                dve.wait_ge(down_done[s], 2 * half + b + 1)
                                if half:
                                    dve.wait_ge(summed[s], b + 1)
                                dve.tensor_tensor(xres[s][:, 2 * b:2 * b + 2],
                                                  bank[s][:, 2 + b].rearrange("p (t d) -> p t d", d=D),
                                                  xres[s][:, 2 * b:2 * b + 2], ALU.add).then_inc(summed[s], 1)

        emit(merged(prepare, 1), None, 0)
        ph.clear()
        with nc.Fori(0, graphs // STREAMS) as pair:
            emit(order, pair * STREAMS, (pair * STREAMS + STREAMS) % graphs)
            ph.clear()


def graph_attention_phase(nc, name, x_in, no_edge, out_t, w, graphs):
    scale = float(D) ** -0.5
    with ExitStack() as ctx:
        ph = Phase(nc, ctx, name)
        raw_names = ("wq_t", "wk_t", "wv_t", "wo")
        split = {k: (ph.buf(k + "h", [P, CT, D], F32R), ph.buf(k + "l", [P, CT, D], F32R)) for k in raw_names}
        folded = {k: (ph.buf(k + "h", [P, CT, D], F32R), ph.buf(k + "l", [P, CT, D], F32R)) for k in ("qk", "vo")}
        ident, power = ph.buf("ident", [P, P]), ph.buf("power", [P, NT])
        bo, ln_g, ln_b = ph.buf("bo", [P, D]), ph.buf("ln_g", [P, CT]), ph.buf("ln_b", [P, CT])
        x_sb, xres = ph.bufs("x_sb", [P, NT, D]), ph.bufs("xres", [P, NT, D])
        bias = ph.bufs("bias", [P, NT, N], BF16)
        norm = ph.bufs("norm", [P, NT, D])
        feats = ph.bufs("feats", [P, 2, CT, N], F32R)
        query = ph.bufs("query", [P, 2, CT, N], F32R)
        value = ph.bufs("value", [P, NT, D])
        prob = ph.bufs("prob", [P, NT, N])
        probT = ph.bufs("probT", [P, NT, N])
        hid_t = ph.bufs("hid_t", [P, CT, N])
        low, total = ph.bufs("low", [P, NT]), ph.bufs("total", [P, NT])
        stat, mean_var = ph.bufs("stat", [P, NT, 6]), ph.bufs("mean_var", [P, NT, 2])
        veps, rstd = ph.bufs("veps", [P, NT]), ph.bufs("rstd", [P, NT])
        bank = [ctx.enter_context(nc.psum_tensor(f"{name}_bank{s}", [P, 4, N], F32)) for s in range(STREAMS)]
        load_weights(nc, ph, [(w[k], *split[k]) for k in raw_names],
                     [(w["bo"].partition_broadcast(P), bo[:]), (w["ln_g"], ln_g[:]), (w["ln_b"], ln_b[:])],
                     [prob[s][:].rearrange("p t n -> p (t n)") for s in range(STREAMS)], power, ident)
        multiplied, folded_hi, folded_lo = ph.sem("multiplied"), ph.sem("folded_hi"), ph.sem("folded_lo")
        with nc.Block(no_gpsimd_drain=True) as block:
            pairs = (("qk", "wq_t", "wk_t"), ("vo", "wv_t", "wo"))

            @block.tensor
            def _(pe):
                for s, (_, left, right) in enumerate(pairs):
                    for i in range(CT):
                        for c in range(CT):
                            mm = product(pe, bank[s][:, i, 0:D],
                                         (split[left][0][:, c, i * P:(i + 1) * P], split[left][1][:, c, i * P:(i + 1) * P]),
                                         (split[right][0][:, c], split[right][1][:, c]), c == 0, c == CT - 1)
                        mm.then_inc(multiplied, 1)

            @block.vector
            def _(dve):
                for s, (k, _, _) in enumerate(pairs):
                    for i in range(CT):
                        dve.wait_ge(multiplied, CT * s + i + 1)
                        dve.tensor_copy(folded[k][0][:, i], bank[s][:, i, 0:D]).then_inc(folded_hi, 1)
                        dve.wait_ge(folded_hi, CT * s + i + 1)
                        dve.tensor_tensor(folded[k][1][:, i], bank[s][:, i, 0:D],
                                          folded[k][0][:, i].bitcast(F32), ALU.subtract).then_inc(folded_lo, 1)
        x_loaded, bias_loaded, res_made = (ph.sems(k) for k in ("x_loaded", "bias_loaded", "res_made"))
        turned_x, feats_hi, feats_lo = (ph.sems(k) for k in ("turned_x", "feats_hi", "feats_lo"))
        q_done, q_hi, q_lo, v_done, v_ready = (ph.sems(k) for k in ("q_done", "q_hi", "q_lo", "v_done", "v_ready"))
        scores, biased, probs, turned, copied = (ph.sems(k) for k in ("scores", "biased", "probs", "turned", "copied"))
        inverse, mixed, x1_made = (ph.sems(k) for k in ("inverse", "mixed", "x1_made"))
        stats_done, rstd_done, normed = (ph.sems(k) for k in ("stats_done", "rstd_done", "normed"))
        turned_out, out_made, stored = (ph.sems(k) for k in ("turned_out", "out_made", "stored"))

        lag_t, lag_v = 2, 3
        steps = [f"step{j}" for j in range(NT + lag_v)]
        prepare = ["load", "bias", "turn", "feats", "query", "value"]

        def emit(order, graph, following):
            with nc.Block(no_gpsimd_drain=True) as block:
                @block.sync
                def _(sp):
                    for stage, s in order:
                        if stage == "load":
                            if graph is not None:
                                sp.wait_ge(res_made[s], 1)
                            sp.dma_start(x_sb[s][:], rows(x_in[following + s])).then_inc(x_loaded[s], 16)
                        elif stage == "bias":
                            if graph is not None:
                                sp.wait_ge(biased[s], NT)
                            sp.dma_start(bias[s][:], rows(no_edge[following + s])).then_inc(bias_loaded[s], 16)
                        elif stage == "store":
                            sp.wait_ge(out_made[s], CT)
                            sp.dma_start(out_t[graph + s].rearrange("(c p) n -> p c n", p=P), hid_t[s][:])\
                                .then_inc(stored[s], 16)
                    for s in range(STREAMS):
                        sp.wait_ge(bias_loaded[s], 16)
                        if graph is not None:
                            sp.wait_ge(stored[s], 16)

                @block.gpsimd
                def _(pool):
                    for stage, s in order:
                        if stage == "residual":
                            pool.tensor_tensor(xres[s][:], x_sb[s][:],
                                               bo[:].unsqueeze(1).to_broadcast([P, NT, D]), ALU.add)\
                                .then_inc(res_made[s], 1)
                        elif stage == "stats":
                            pool.wait_ge(stats_done[s], 2 * NT)
                            pool.tensor_scalar(veps[s][:], mean_var[s][:, :, 1], EPS, 1.0, ALU.add, ALU.mult)\
                                .then_inc(rstd_done[s], 1)
                            pool.wait_ge(rstd_done[s], 1)
                            pool.tensor_tensor(rstd[s][:], veps[s][:], power[:], ALU.pow).then_inc(rstd_done[s], 1)

                @block.tensor
                def _(pe):
                    def turn(s, src, first, done):
                        for c in range(CT):
                            for t in range(NT):
                                mm = pe.transpose(bank[s][:, first + c, t * P:(t + 1) * P],
                                                  src[:, t, c * P:(c + 1) * P], ident[:])
                            mm.then_inc(done, 1)

                    for stage, s in order:
                        if stage == "turn":
                            pe.wait_ge(x_loaded[s], 16)
                            if graph is not None:
                                pe.wait_ge(biased[s], NT)
                            turn(s, x_sb[s], 0, turned_x[s])
                        elif stage == "query":
                            pe.wait_ge(feats_hi[s], CT)
                            pe.wait_ge(feats_lo[s], CT)
                            for b in range(CT):
                                for c in range(CT):
                                    mm = product(pe, bank[s][:, b],
                                                 (folded["qk"][0][:, c, b * P:(b + 1) * P],
                                                  folded["qk"][1][:, c, b * P:(b + 1) * P]),
                                                 (feats[s][:, 0, c], feats[s][:, 1, c]), c == 0, c == CT - 1)
                                mm.then_inc(q_done[s], 1)
                        elif stage == "value":
                            pe.wait_ge(q_hi[s], CT)
                            pe.wait_ge(q_lo[s], CT)
                            for t in range(NT):
                                for c in range(CT):
                                    mm = product(pe, bank[s][:, t // 2, t % 2 * D:(t % 2 + 1) * D],
                                                 (feats[s][:, 0, c, t * P:(t + 1) * P],
                                                  feats[s][:, 1, c, t * P:(t + 1) * P]),
                                                 (folded["vo"][0][:, c], folded["vo"][1][:, c]), c == 0, c == CT - 1)
                                if t % 2:
                                    mm.then_inc(v_done[s], 1)
                        elif stage in steps:
                            j = int(stage[4:])
                            if j < NT:
                                if j >= 2:
                                    pe.wait_ge(biased[s], j - 1)
                                for c in range(CT):
                                    mm = product(pe, bank[s][:, j % 2],
                                                 (query[s][:, 0, c, j * P:(j + 1) * P],
                                                  query[s][:, 1, c, j * P:(j + 1) * P]),
                                                 (feats[s][:, 0, c], feats[s][:, 1, c]), c == 0, c == CT - 1)
                                mm.then_inc(scores[s], 1)
                            i = j - lag_t
                            if 0 <= i < NT:
                                pe.wait_ge(probs[s], i + 1)
                                if i:
                                    pe.wait_ge(copied[s], i)
                                for k in range(NT):
                                    mm = pe.transpose(bank[s][:, 2, k * P:(k + 1) * P],
                                                      prob[s][:, i, k * P:(k + 1) * P], ident[:])
                                mm.then_inc(turned[s], 1)
                            i = j - lag_v
                            if 0 <= i < NT:
                                pe.wait_ge(copied[s], i + 1)
                                if i >= 1:
                                    pe.wait_ge(x1_made[s], i)
                                for k in range(NT):
                                    mm = pe.matmul(bank[s][:, 3, 0:D],
                                                   probT[s][:, k, i * P:(i + 1) * P], value[s][:, k],
                                                   start=k == 0, stop=k == NT - 1)
                                mm.then_inc(mixed[s], 1)
                        elif stage == "turn_out":
                            pe.wait_ge(normed[s], NT)
                            pe.wait_ge(copied[s], NT)
                            turn(s, norm[s], 2, turned_out[s])

                @block.scalar
                def _(act):
                    for stage, s in order:
                        if stage == "feats":
                            for c in range(CT):
                                act.wait_ge(turned_x[s], c + 1)
                                act.activation(feats[s][:, 0, c], bank[s][:, c], ACT.Copy).then_inc(feats_hi[s], 1)
                        elif stage == "query":
                            for b in range(CT):
                                act.wait_ge(q_done[s], b + 1)
                                act.activation(query[s][:, 0, b], bank[s][:, b], ACT.Copy).then_inc(q_hi[s], 1)
                        elif stage in steps:
                            j = int(stage[4:])
                            if j < NT:
                                act.wait_ge(biased[s], j + 1)
                                act.activation(prob[s][:, j], prob[s][:, j], ACT.Exp, bias=low[s][:, j:j + 1],
                                               scale=-1.0, accum_out=total[s][:, j:j + 1]).then_inc(probs[s], 1)
                            i = j - lag_t
                            if 0 <= i < NT:
                                act.wait_ge(turned[s], i + 1)
                                act.activation(probT[s][:, :, i * P:(i + 1) * P],
                                               bank[s][:, 2].rearrange("p (k q) -> p k q", q=P), ACT.Copy)\
                                    .then_inc(copied[s], 1)
                        elif stage == "turn_out":
                            for c in range(CT):
                                act.wait_ge(turned_out[s], c + 1)
                                act.activation(hid_t[s][:, c], bank[s][:, 2 + c], ACT.Identity,
                                               scale=ln_g[:, c:c + 1], bias=ln_b[:, c:c + 1]).then_inc(out_made[s], 1)

                @block.vector
                def _(dve):
                    for stage, s in order:
                        if stage == "feats":
                            for c in range(CT):
                                dve.wait_ge(feats_hi[s], c + 1)
                                dve.tensor_tensor(feats[s][:, 1, c], bank[s][:, c], feats[s][:, 0, c].bitcast(F32),
                                                  ALU.subtract).then_inc(feats_lo[s], 1)
                        elif stage == "query":
                            for b in range(CT):
                                dve.wait_ge(q_hi[s], b + 1)
                                dve.tensor_tensor(query[s][:, 1, b], bank[s][:, b], query[s][:, 0, b].bitcast(F32),
                                                  ALU.subtract).then_inc(q_lo[s], 1)
                        elif stage == "value":
                            for b in range(2):
                                dve.wait_ge(v_done[s], b + 1)
                                if graph is not None:
                                    dve.wait_ge(mixed[s], NT)
                                dve.tensor_copy(value[s][:, 2 * b:2 * b + 2],
                                                bank[s][:, b].rearrange("p (t d) -> p t d", d=D))\
                                    .then_inc(v_ready[s], 1)
                        elif stage in steps:
                            j = int(stage[4:])
                            if j < NT:
                                dve.wait_ge(scores[s], j + 1)
                                dve.tensor_tensor_reduce(prob[s][:, j], bank[s][:, j % 2], bias[s][:, j],
                                                         -scale, 3e38, ALU.add, ALU.min, low[s][:, j:j + 1])\
                                    .then_inc(biased[s], 1)
                            i = j - lag_v
                            if 0 <= i < NT:
                                if i == 0:
                                    dve.wait_ge(probs[s], NT)
                                    dve.reciprocal(total[s][:], total[s][:]).then_inc(inverse[s], 1)
                                    dve.wait_ge(inverse[s], 1)
                                    dve.wait_ge(res_made[s], 1)
                                dve.wait_ge(mixed[s], i + 1)
                                dve.scalar_tensor_tensor(
                                    out=xres[s][:, i], in0=bank[s][:, 3, 0:D],
                                    scalar=total[s][:, i:i + 1], in1=xres[s][:, i], op0=ALU.mult, op1=ALU.add)\
                                    .then_inc(x1_made[s], 1)
                                dve.wait_ge(x1_made[s], i + 1)
                                dve.bn_stats(stat[s][:, i], xres[s][:, i]).then_inc(stats_done[s], 1)
                        elif stage == "stats":
                            for t in range(NT):
                                dve.wait_ge(stats_done[s], t + 1)
                                dve.bn_aggr(mean_var[s][:, t], stat[s][:, t]).then_inc(stats_done[s], 1)
                        elif stage == "norm":
                            dve.wait_ge(rstd_done[s], 2)
                            for t in range(NT):
                                dve.tensor_scalar(norm[s][:, t], xres[s][:, t], mean_var[s][:, t, 0:1],
                                                  rstd[s][:, t:t + 1], ALU.subtract, ALU.mult)\
                                    .then_inc(normed[s], 1)

        emit(merged(prepare, 1), None, 0)
        ph.clear()
        with nc.Fori(0, graphs // STREAMS) as pair:
            emit(placed(ORDER_2), pair * STREAMS, (pair * STREAMS + STREAMS) % graphs)
            ph.clear()


def gated_phase(nc, name, hid_t, adj, out, w, graphs):
    with ExitStack() as ctx:
        ph = Phase(nc, ctx, name)
        gates = ("ri", "zi", "ni", "rh", "zh", "nh")
        split = {"wd": (ph.buf("wdh", [P, CT, LABELS * D], F32R), ph.buf("wdl", [P, CT, LABELS * D], F32R))}
        for k in gates:
            split["w" + k] = (ph.buf(f"w{k}h", [P, CT, D], F32R), ph.buf(f"w{k}l", [P, CT, D], F32R))
        ident, ident_b, power = ph.buf("ident", [P, P]), ph.buf("ident_b", [P, P], BF16), ph.buf("power", [P, NT])
        bd, ln_g, ln_b = ph.buf("bd", [P, D]), ph.buf("ln_g", [P, D]), ph.buf("ln_b", [P, D])
        gate_bias = {k: ph.buf("b" + k, [P, CT]) for k in gates}
        adj_sb = ph.bufs("adj", [P, NT, N], I32)
        adj_b, adj_t = ph.bufs("adj_b", [P, NT, N], BF16), ph.bufs("adj_t", [P, NT, N], BF16)
        hid_in, hid = ph.bufs("hid_in", [P, CT, N]), ph.bufs("hid", [P, CT, N])
        feats = ph.bufs("feats", [P, 2, CT, N], F32R)
        mask = ph.bufs("mask", [P, 2, NT, N], F32R)
        mapped_hi, mapped_lo = ph.bufs("mapped_hi", [P, NT, 2, D + 2], F32R), ph.bufs("mapped_lo", [P, NT, 2, D], F32R)
        acc = ph.bufs("acc", [P, NT, D])
        gate_r, gate_z = ph.bufs("gate_r", [P, CT, N]), ph.bufs("gate_z", [P, CT, N])
        count = ph.bufs("count", [P, LABELS, NT])
        stat, mean_var = ph.bufs("stat", [P, NT, 6]), ph.bufs("mean_var", [P, NT, 2])
        veps, rstd = ph.bufs("veps", [P, NT]), ph.bufs("rstd", [P, NT])
        bank = [ctx.enter_context(nc.psum_tensor(f"{name}_bank{s}", [P, 4, N], F32)) for s in range(STREAMS)]
        agg = [mapped_lo[s][:].rearrange("p (a c) l d -> p a c (l d)", a=2) for s in range(STREAMS)]
        cand = [acc[s][:].rearrange("p t d -> p (t d)").rearrange("p (c n) -> p c n", c=CT) for s in range(STREAMS)]
        new_t = gate_r
        load_weights(
            nc, ph, [(w[k], *split[k]) for k in split],
            [(w["bd"].partition_broadcast(P), bd[:]), (w["ln_g"].partition_broadcast(P), ln_g[:]),
             (w["ln_b"].partition_broadcast(P), ln_b[:])] + [(w["b" + k], gate_bias[k][:]) for k in gates],
            [adj_sb[s][:].bitcast(F32).rearrange("p t n -> p (t n)") for s in range(STREAMS)]
            + [hid[s][:].rearrange("p t n -> p (t n)") for s in range(STREAMS)], power, ident, ident_b)
        summed_bias = ph.sem("summed_bias")
        with nc.Block(no_gpsimd_drain=True) as block:
            @block.vector
            def _(dve):
                for k in ("r", "z"):
                    dve.tensor_tensor(gate_bias[k + "i"][:], gate_bias[k + "i"][:], gate_bias[k + "h"][:], ALU.add)\
                        .then_inc(summed_bias, 1)
                for s in range(STREAMS):
                    for t in range(NT):
                        for d in range(2):
                            dve.tensor_scalar(mapped_hi[s][:, t, d, D:D + 2], ident[:, 0:2], 0.0, 1.0,
                                              ALU.mult, ALU.add).then_inc(summed_bias, 1)
        adj_loaded, hid_loaded, adj_cast, adj_turned, adj_ready = (
            ph.sems(k) for k in ("adj_loaded", "hid_loaded", "adj_cast", "adj_turned", "adj_ready"))
        feats_hi, feats_lo, map_done, map_hi, map_lo = (
            ph.sems(k) for k in ("feats_hi", "feats_lo", "map_done", "map_hi", "map_lo"))
        masked, averaged, counted, added = (ph.sems(k) for k in ("masked", "averaged", "counted", "added"))
        agg_turned, agg_hi, agg_lo = (ph.sems(k) for k in ("agg_turned", "agg_hi", "agg_lo"))
        gate_done, gate_ready, reset_done, cand_in, cand_ready, kept, blended, held = (
            ph.sems(k) for k in ("gate_done", "gate_ready", "reset_done", "cand_in", "cand_ready", "kept", "blended", "held"))
        new_turned, stats_done, rstd_done, normed, finished, stored = (
            ph.sems(k) for k in ("new_turned", "stats_done", "rstd_done", "normed", "finished", "stored"))

        prepare = ["load", "cast", "adj", "split", "mask0"]

        def emit(order, graph, following):
            with nc.Block(no_gpsimd_drain=True) as block:
                @block.sync
                def _(sp):
                    for stage, s in order:
                        if stage == "load":
                            sp.dma_start(adj_sb[s][:], rows(adj[following + s])).then_inc(adj_loaded[s], 16)
                            if graph is not None:
                                sp.wait_ge(held[s], 1)
                            sp.dma_start(hid_in[s][:], hid_t[following + s].rearrange("(c p) n -> p c n", p=P))\
                                .then_inc(hid_loaded[s], 16)
                        elif stage == "store":
                            sp.wait_ge(finished[s], NT)
                            sp.dma_start(rows(out[graph + s]), acc[s][:]).then_inc(stored[s], 16)
                    if graph is not None:
                        for s in range(STREAMS):
                            sp.wait_ge(stored[s], 16)

                @block.gpsimd
                def _(pool):
                    for stage, s in order:
                        if stage == "hold":
                            pool.tensor_copy(hid[s][:], hid_in[s][:]).then_inc(held[s], 1)
                        elif stage in ("blend0", "blend1"):
                            b = int(stage[5])
                            pool.wait_ge(held[s], 1)
                            pool.wait_ge(cand_in[s], b + 1)
                            pool.wait_ge(gate_ready[s], 2 * b + 2)
                            pool.tensor_tensor(new_t[s][:, b], hid[s][:, b], gate_z[s][:, b], ALU.mult)\
                                .then_inc(kept[s], 1)
                        elif stage == "stats":
                            pool.wait_ge(stats_done[s], 2 * NT)
                            pool.tensor_scalar(veps[s][:], mean_var[s][:, :, 1], EPS, 1.0, ALU.add, ALU.mult)\
                                .then_inc(rstd_done[s], 1)
                            pool.wait_ge(rstd_done[s], 1)
                            pool.tensor_tensor(rstd[s][:], veps[s][:], power[:], ALU.pow).then_inc(rstd_done[s], 1)

                @block.tensor
                def _(pe):
                    for stage, s in order:
                        if stage == "adj":
                            pe.wait_ge(adj_cast[s], 1)
                            if graph is not None:
                                pe.wait_ge(cand_in[s], CT)
                            for t in range(NT):
                                for q in range(NT):
                                    at = t % 2 * N + q * P
                                    mm = pe.transpose(bank[s][:, 2 + t // 2].bitcast(BF16)[:, at:at + P],
                                                      adj_b[s][:, q, t * P:(t + 1) * P], ident_b[:])
                                if t % 2:
                                    mm.then_inc(adj_turned[s], 1)
                        elif stage in ("map0", "map1"):
                            half = int(stage[3])
                            if half:
                                pe.wait_ge(added[s], 2 * NT)
                            for t in range(NT):
                                for c in range(CT):
                                    mm = product(pe, bank[s][:, t],
                                                 (feats[s][:, 0, c, t * P:(t + 1) * P],
                                                  feats[s][:, 1, c, t * P:(t + 1) * P]),
                                                 (split["wd"][0][:, c, half * N:(half + 1) * N],
                                                  split["wd"][1][:, c, half * N:(half + 1) * N]), c == 0, c == CT - 1)
                                mm.then_inc(map_done[s], 1)
                        elif stage.startswith("label"):
                            d = int(stage[5])
                            if d >= 2:
                                pe.wait_ge(masked[s], d - 1)
                            pe.wait_ge(map_hi[s], NT * (d // 2 + 1))
                            pe.wait_ge(map_lo[s], NT * (d // 2 + 1))
                            for m in range(NT):
                                if d % 2:
                                    pe.wait_ge(added[s], NT * d)
                                for k in range(NT):
                                    near = mask[s][:, d % 2, k, m * P:(m + 1) * P]
                                    if k:
                                        pe.matmul(bank[s][:, m, 0:D], near, mapped_lo[s][:, k, d % 2],
                                                  start=False, stop=False)
                                    mm = pe.matmul(bank[s][:, m, 0:D + 2], near, mapped_hi[s][:, k, d % 2],
                                                   start=k == 0, stop=k == NT - 1)
                                    if not k:
                                        pe.matmul(bank[s][:, m, 0:D], near, mapped_lo[s][:, k, d % 2],
                                                  start=False, stop=False)
                                mm.then_inc(averaged[s], 1)
                        elif stage == "turn":
                            pe.wait_ge(added[s], LABELS * NT)
                            for c in range(CT):
                                for t in range(NT):
                                    mm = pe.transpose(bank[s][:, c, t * P:(t + 1) * P],
                                                      acc[s][:, t, c * P:(c + 1) * P], ident[:])
                                mm.then_inc(agg_turned[s], 1)
                        elif stage in ("gates0", "gates1"):
                            b = int(stage[5])
                            pe.wait_ge(agg_hi[s], CT)
                            pe.wait_ge(agg_lo[s], CT)
                            if b:
                                pe.wait_ge(gate_ready[s], 2)
                                pe.wait_ge(cand_in[s], 1)
                            for n, terms in enumerate((("ri", "rh"), ("zi", "zh"), ("nh",), ("ni",))):
                                for a, k in enumerate(terms):
                                    x = agg[s] if k[1] == "i" else feats[s]
                                    for c in range(CT):
                                        wh, wl = split["w" + k]
                                        mm = product(pe, bank[s][:, n],
                                                     (wh[:, c, b * P:(b + 1) * P], wl[:, c, b * P:(b + 1) * P]),
                                                     (x[:, 0, c], x[:, 1, c]), a == 0 and c == 0,
                                                     a == len(terms) - 1 and c == CT - 1)
                                mm.then_inc(gate_done[s], 1)
                        elif stage == "turn_new":
                            pe.wait_ge(blended[s], 2 * CT)
                            pe.wait_ge(gate_ready[s], 2 * CT)
                            for t in range(NT):
                                for c in range(CT):
                                    mm = pe.transpose(bank[s][:, t // 2, (t % 2 * CT + c) * P:(t % 2 * CT + c + 1) * P],
                                                      new_t[s][:, c, t * P:(t + 1) * P], ident[:])
                                mm.then_inc(new_turned[s], 1)

                @block.scalar
                def _(act):
                    for stage, s in order:
                        if stage == "adj":
                            if graph is not None:
                                act.wait_ge(masked[s], 2)
                            for b in range(2):
                                act.wait_ge(adj_turned[s], b + 1)
                                act.activation(adj_t[s][:, 2 * b:2 * b + 2],
                                               bank[s][:, 2 + b].bitcast(BF16).rearrange("p (t n) -> p t n", t=2),
                                               ACT.Copy).then_inc(adj_ready[s], 1)
                        elif stage == "split":
                            act.wait_ge(hid_loaded[s], 16)
                            if graph is not None:
                                act.wait_ge(gate_done[s], 4 * CT)
                            for c in range(CT):
                                act.activation(feats[s][:, 0, c], hid_in[s][:, c], ACT.Copy).then_inc(feats_hi[s], 1)
                        elif stage in ("map0", "map1"):
                            half = int(stage[3])
                            for t in range(NT):
                                act.wait_ge(map_done[s], NT * half + t + 1)
                                act.activation(mapped_hi[s][:, t, :, 0:D], bank[s][:, t].rearrange("p (l d) -> p l d", d=D),
                                               ACT.Copy).then_inc(map_hi[s], 1)
                        elif stage == "turn":
                            for c in range(CT):
                                act.wait_ge(agg_turned[s], c + 1)
                                act.activation(agg[s][:, 0, c], bank[s][:, c], ACT.Relu).then_inc(agg_hi[s], 1)
                        elif stage in ("gates0", "gates1"):
                            b = int(stage[5])
                            for n, (to, k) in enumerate(((gate_r, "ri"), (gate_z, "zi"))):
                                act.wait_ge(gate_done[s], 4 * b + n + 1)
                                act.activation(to[s][:, b], bank[s][:, n], ACT.Sigmoid,
                                               bias=gate_bias[k][:, b:b + 1]).then_inc(gate_ready[s], 1)
                            act.wait_ge(cand_in[s], b + 1)
                            act.activation(cand[s][:, b], cand[s][:, b], ACT.Tanh).then_inc(cand_ready[s], 1)

                @block.vector
                def _(dve):
                    for stage, s in order:
                        if stage == "cast":
                            dve.wait_ge(adj_loaded[s], 16)
                            dve.tensor_copy(adj_b[s][:], adj_sb[s][:]).then_inc(adj_cast[s], 1)
                        elif stage == "split":
                            for c in range(CT):
                                dve.wait_ge(feats_hi[s], c + 1)
                                dve.tensor_tensor(feats[s][:, 1, c], hid_in[s][:, c], feats[s][:, 0, c].bitcast(F32),
                                                  ALU.subtract).then_inc(feats_lo[s], 1)
                        elif stage in ("mask0", "mask1"):
                            half = int(stage[4])
                            if not half:
                                dve.wait_ge(adj_ready[s], 2)
                            for d in (2 * half, 2 * half + 1):
                                if graph is not None:
                                    dve.wait_ge(averaged[s], NT * (d - 1 if half else d + 3))
                                dve.tensor_scalar(mask[s][:, d % 2], adj_t[s][:], float(d + 1), None, ALU.is_equal)\
                                    .then_inc(masked[s], 1)
                        elif stage in ("map0", "map1"):
                            half = int(stage[3])
                            for t in range(NT):
                                dve.wait_ge(map_hi[s], NT * half + t + 1)
                                dve.tensor_tensor(mapped_lo[s][:, t], bank[s][:, t].rearrange("p (l d) -> p l d", d=D),
                                                  mapped_hi[s][:, t, :, 0:D].bitcast(F32), ALU.subtract).then_inc(map_lo[s], 1)
                        elif stage.startswith("mean"):
                            d = int(stage[4])
                            dve.wait_ge(averaged[s], NT * (d + 1))
                            dve.tensor_scalar(count[s][:, d], bank[s][:, :, D], 1e-8, None, ALU.add)\
                                .then_inc(counted[s], 1)
                            dve.wait_ge(counted[s], 2 * d + 1)
                            dve.reciprocal(count[s][:, d], count[s][:, d]).then_inc(counted[s], 1)
                            dve.wait_ge(counted[s], 2 * d + 2)
                            for m in range(NT):
                                if d:
                                    dve.wait_ge(added[s], NT * (d - 1) + m + 1)
                                dve.scalar_tensor_tensor(
                                    out=acc[s][:, m], in0=bank[s][:, m, 0:D], scalar=count[s][:, d, m:m + 1],
                                    in1=acc[s][:, m] if d else bd[:], op0=ALU.mult, op1=ALU.add)\
                                    .then_inc(added[s], 1)
                        elif stage == "turn":
                            for c in range(CT):
                                dve.wait_ge(agg_hi[s], c + 1)
                                dve.scalar_tensor_tensor(
                                    out=agg[s][:, 1, c], in0=bank[s][:, c], scalar=0.0,
                                    in1=agg[s][:, 0, c].bitcast(F32), op0=ALU.max, op1=ALU.subtract)\
                                    .then_inc(agg_lo[s], 1)
                        elif stage in ("gates0", "gates1"):
                            b = int(stage[5])
                            dve.wait_ge(gate_ready[s], 2 * b + 1)
                            dve.wait_ge(gate_done[s], 4 * b + 3)
                            dve.scalar_tensor_tensor(out=gate_r[s][:, b], in0=bank[s][:, 2],
                                                     scalar=gate_bias["nh"][:, b:b + 1], in1=gate_r[s][:, b],
                                                     op0=ALU.add, op1=ALU.mult).then_inc(reset_done[s], 1)
                            dve.wait_ge(reset_done[s], b + 1)
                            dve.wait_ge(gate_done[s], 4 * b + 4)
                            dve.scalar_tensor_tensor(out=cand[s][:, b], in0=bank[s][:, 3],
                                                     scalar=gate_bias["ni"][:, b:b + 1], in1=gate_r[s][:, b],
                                                     op0=ALU.add, op1=ALU.add).then_inc(cand_in[s], 1)
                        elif stage in ("blend0", "blend1"):
                            b = int(stage[5])
                            dve.wait_ge(cand_ready[s], b + 1)
                            dve.wait_ge(kept[s], b + 1)
                            dve.scalar_tensor_tensor(out=gate_z[s][:, b], in0=gate_z[s][:, b], scalar=-1.0,
                                                     in1=cand[s][:, b], op0=ALU.add, op1=ALU.mult)\
                                .then_inc(blended[s], 1)
                            dve.wait_ge(blended[s], 2 * b + 1)
                            dve.tensor_tensor(new_t[s][:, b], new_t[s][:, b], gate_z[s][:, b], ALU.subtract)\
                                .then_inc(blended[s], 1)
                        elif stage in ("stats", "norm"):
                            rows_of = [bank[s][:, t // 2, t % 2 * D:(t % 2 + 1) * D] for t in range(NT)]
                            if stage == "stats":
                                for t in range(NT):
                                    dve.wait_ge(new_turned[s], t // 2 * 2 + 2)
                                    dve.bn_stats(stat[s][:, t], rows_of[t]).then_inc(stats_done[s], 1)
                                for t in range(NT):
                                    dve.wait_ge(stats_done[s], t + 1)
                                    dve.bn_aggr(mean_var[s][:, t], stat[s][:, t]).then_inc(stats_done[s], 1)
                            else:
                                dve.wait_ge(rstd_done[s], 2)
                                for t in range(NT):
                                    dve.scalar_tensor_tensor(out=acc[s][:, t], in0=rows_of[t],
                                                             scalar=mean_var[s][:, t, 0:1], in1=ln_g[:],
                                                             op0=ALU.subtract, op1=ALU.mult).then_inc(normed[s], 1)
                                for t in range(NT):
                                    dve.wait_ge(normed[s], t + 1)
                                    dve.scalar_tensor_tensor(out=acc[s][:, t], in0=acc[s][:, t],
                                                             scalar=rstd[s][:, t:t + 1], in1=ln_b[:],
                                                             op0=ALU.mult, op1=ALU.add).then_inc(finished[s], 1)

        emit(merged(prepare, 1), None, 0)
        ph.clear()
        with nc.Fori(0, graphs // STREAMS) as pair:
            emit(placed(ORDER_3), pair * STREAMS, (pair * STREAMS + STREAMS) % graphs)
            ph.clear()


def build(nc, a, out, graphs, only=None, x_in=None):
    x1 = nc.dram_tensor("x1", [graphs, N, D], F32, kind="Internal").ap()
    x2 = nc.dram_tensor("x2", [graphs, N, D], F32, kind="Internal").ap()
    x3_t = nc.dram_tensor("x3_t", [graphs, D, N], F32, kind="Internal").ap()
    no_edge = nc.dram_tensor("no_edge", [graphs, N, N], BF16, kind="Internal").ap()
    adj = a["adj"]
    l0 = {k: a["L0_gnn_" + k] for k in ("wq", "wk", "wv", "wo", "w1", "w2", "bq", "bk", "bv", "bo", "b1", "b2",
                                        "ln1_g", "ln1_b", "ln2_g", "ln2_b")}
    encoder_phase(nc, "l0", a["x"], adj, no_edge, x1, l0, graphs, True)
    l1 = {k: a["L1_gnn_W" + k[1]] for k in ("wq", "wk", "wv", "wo")} | {k: a["L1_gnn_" + k] for k in ("bq", "bk", "bv", "bo")}
    encoder_phase(nc, "l1", x1, None, no_edge, x2, l1 | {"ln_g": a["L1_gnn_gamma"], "ln_b": a["L1_gnn_beta"]}, graphs, False)
    l2 = {"wq_t": a["L2_gnn_Wq"], "wk_t": a["L2_gnn_Wk"], "wv_t": a["L2_gnn_Wv"], "wo": a["L2_gnn_Wo"],
          "bo": a["L2_gnn_bo"], "ln_g": a["L2_gnn_gamma"], "ln_b": a["L2_gnn_beta"]}
    graph_attention_phase(nc, "l2", x2, no_edge, x3_t, l2, graphs)
    gates = ("ri", "zi", "ni", "rh", "zh", "nh")
    l3 = {"wd": a["L3_gnn_Wd"], "bd": a["L3_gnn_bd"], "ln_g": a["L3_gnn_gamma"], "ln_b": a["L3_gnn_beta"]}
    l3 |= {"w" + k: a["L3_gnn_W" + k] for k in gates} | {"b" + k: a["L3_gnn_b" + k] for k in gates}
    gated_phase(nc, "l3", x3_t, adj, out, l3, graphs)


TRANSPOSED = ("L2_gnn_Wq", "L2_gnn_Wk", "L2_gnn_Wv") + tuple("L3_gnn_W" + k for k in ("ri", "zi", "ni", "rh", "zh", "nh"))

COLUMNS = tuple("L0_gnn_" + k for k in ("bq", "bk", "bv", "b1", "ln1_g", "ln1_b", "ln2_g", "ln2_b")) + (
    "L1_gnn_bq", "L1_gnn_bk", "L1_gnn_bv", "L2_gnn_gamma", "L2_gnn_beta") + tuple(
    "L3_gnn_b" + k for k in ("ri", "zi", "ni", "rh", "zh", "nh"))


def laid_out(name, a):
    if name in COLUMNS:
        return np.ascontiguousarray(a.reshape(-1, P).T)
    if name in TRANSPOSED:
        return np.ascontiguousarray(a.T)
    if name == "L3_gnn_Wd":
        return np.ascontiguousarray(a.reshape(D, LABELS, D).transpose(2, 1, 0).reshape(D, LABELS * D))
    return np.ascontiguousarray(a)


def kernel(**inputs):
    import concourse.bacc as bacc
    from concourse.bass_utils import run_bass_kernel_spmd

    nc = bacc.Bacc("TRN2", target_bir_lowering=False, num_devices=1)
    arrays = {name: laid_out(name, np.asarray(a)) for name, a in inputs.items()}
    args = {name: nc.dram_tensor(name, a.shape, mybir.dt.from_np(a.dtype), kind="ExternalInput").ap()
            for name, a in arrays.items()}
    graphs = arrays["x"].shape[0]
    out = nc.dram_tensor("out", (graphs, N, D), F32, kind="ExternalOutput").ap()
    build(nc, args, out, graphs)
    result = run_bass_kernel_spmd(nc, [arrays], core_ids=[0])
    return result.results[0]["out"]
```
